# Optimizing a Trainium2 kernel written in Bass

```python
import numpy as np
import jax
import jax.numpy as jnp

def _softmax(x, axis=-1):
    return jax.nn.softmax(x, axis=axis)

def _gelu(x):
    return jax.nn.gelu(x, approximate=True)

def _silu(x):
    return jax.nn.silu(x)

def _sigmoid(x):
    return jax.nn.sigmoid(x)

def _layernorm(x, axis=-1, eps=1e-05):
    m = jnp.mean(x, axis=axis, keepdims=True)
    v = jnp.var(x, axis=axis, keepdims=True)
    return (x - m) / jnp.sqrt(v + eps)

def _scatter_add(tgt, idx, src, axis=0):
    return tgt.at[idx].add(src)

def _segment_sum(src, seg, n):
    return jax.ops.segment_sum(src, seg, n)
kernel_name = 'mk_gnn_resnorm_d4_gnn_r64_75c7e6'

def setup_inputs(seed: int=0):
    np.random.seed(seed)
    _w = jnp.asarray

    def _rec_inputs():
        import jax
        import jax.numpy as jnp
        _gk = jax.random.key(seed)
        x = -0.000202 + 1 * jax.random.normal(jax.random.fold_in(_gk, 1), (50000, 128), jnp.float32)
        src = jax.random.randint(jax.random.fold_in(_gk, 2), (12500,), 0, 50000, jnp.int32)
        dst = jnp.minimum((50000 * jax.random.uniform(jax.random.fold_in(_gk, 3), (12500,)) ** 2.0).astype(jnp.int32), 49999)
        _o = jnp.argsort(dst, stable=True)
        src = src[_o]
        dst = dst[_o]
        edge_weight = jax.random.uniform(jax.random.fold_in(_gk, 13), (12500,), jnp.float32, 0.0, 0.999998)
        return (x, src, dst, edge_weight)
    x, src, dst, edge_weight = _rec_inputs()

    def _L0_gnn_setup():
        import jax, jax.numpy as jnp
        import numpy as np
        N_NODES = 50000
        N_EDGES = 12500
        D_IN = 128
        U = 128
        H = 128
        key = jax.random.key(seed)
        ks = jax.random.split(key, 8)
        s = lambda d: 1.0 / np.sqrt(d)
        x = jax.random.normal(ks[0], (N_NODES, D_IN), dtype=jnp.float32)
        edge_index = jax.random.randint(ks[1], (2, N_EDGES), 0, N_NODES, dtype=jnp.int64)
        W1 = jax.random.normal(ks[2], (D_IN, U), dtype=jnp.float32) * s(D_IN)
        b1 = jax.random.normal(ks[3], (U,), dtype=jnp.float32) * 0.01
        W2 = jax.random.normal(ks[4], (2 * U, H), dtype=jnp.float32) * s(2 * U)
        b2 = jax.random.normal(ks[5], (H,), dtype=jnp.float32) * 0.01
        W3 = jax.random.normal(ks[6], (H, H), dtype=jnp.float32) * s(H)
        b3 = jax.random.normal(ks[7], (H,), dtype=jnp.float32) * 0.01
        return {'x': x, 'edge_index': edge_index, 'W1': W1, 'b1': b1, 'W2': W2, 'b2': b2, 'W3': W3, 'b3': b3}
    _L0_gnn_all = _L0_gnn_setup()
    _L0_gnn_in = {k: v for k, v in _L0_gnn_all.items() if k in ('W1', 'b1', 'W2', 'b2', 'W3', 'b3')}
    del _L0_gnn_all

    def _L1_gnn_setup():
        import jax, jax.numpy as jnp
        import numpy as np
        N = 100000
        E = 25000
        L = 128
        H = 128
        O = 128

        def _gcn_conv(x, W, b, src, dst, norm, n_nodes):
            h = x @ W
            msg = h[src] * norm[:, None]
            out = jax.ops.segment_sum(msg, dst, num_segments=n_nodes)
            return out + b

        def _lstm_step(z, W_ih, W_hh, b_ih, b_hh):
            gates = z @ W_ih.T + jnp.zeros((1, H), z.dtype) @ W_hh.T + b_ih + b_hh
            i, f, g, o = jnp.split(gates, 4, axis=-1)
            c = jax.nn.sigmoid(i) * jnp.tanh(g)
            return jax.nn.sigmoid(o) * jnp.tanh(c)
        key = jax.random.key(seed)
        ks = jax.random.split(key, 16)
        s = 1.0 / np.sqrt(H)
        inp = {'z': jax.random.normal(ks[0], (N, L), dtype=jnp.float32), 'edge_index': jax.random.randint(ks[1], (2, E), 0, N, dtype=jnp.int64), 'W_ih': jax.random.uniform(ks[2], (4 * H, L), jnp.float32, -s, s), 'W_hh': jax.random.uniform(ks[3], (4 * H, H), jnp.float32, -s, s), 'b_ih': jax.random.uniform(ks[4], (4 * H,), jnp.float32, -s, s), 'b_hh': jax.random.uniform(ks[5], (4 * H,), jnp.float32, -s, s), 'W1': jax.random.uniform(ks[6], (H, H), jnp.float32, -s, s), 'b1': jnp.zeros((H,), jnp.float32), 'W2': jax.random.uniform(ks[7], (H, H), jnp.float32, -s, s), 'b2': jnp.zeros((H,), jnp.float32), 'W3': jax.random.uniform(ks[8], (O, H), jnp.float32, -s, s), 'b3': jax.random.uniform(ks[9], (O,), jnp.float32, -s, s)}
        return inp
    _L1_gnn_all = _L1_gnn_setup()
    _L1_gnn_in = {k: v for k, v in _L1_gnn_all.items() if k in ('W_ih', 'W_hh', 'b_ih', 'b_hh', 'W1', 'b1', 'W2', 'b2', 'W3', 'b3')}
    del _L1_gnn_all

    def _L2_gnn_setup():
        import jax, jax.numpy as jnp
        import numpy as np
        N = 50000
        E = 12500
        D = 128

        def _left_norm_agg(x, s, d, inv_deg_s, num_nodes):
            msg = (x * inv_deg_s[:, None])[s]
            return jax.ops.segment_sum(msg, d, num_segments=num_nodes)
        key = jax.random.key(seed)
        ks = jax.random.split(key, 10)
        x = jax.random.normal(ks[0], (N, D), dtype=jnp.float32)
        src = jax.random.randint(ks[1], (E,), 0, N, dtype=jnp.int32)
        dst = jax.random.randint(ks[2], (E,), 0, N, dtype=jnp.int32)
        sc = 1.0 / np.sqrt(3 * D)
        W0 = jax.random.uniform(ks[3], (3 * D, D), jnp.float32, -sc, sc)
        b0 = jax.random.uniform(ks[4], (D,), jnp.float32, -sc, sc)
        W1 = jax.random.uniform(ks[5], (3 * D, D), jnp.float32, -sc, sc)
        b1 = jax.random.uniform(ks[6], (D,), jnp.float32, -sc, sc)
        W2 = jax.random.uniform(ks[7], (3 * D, D), jnp.float32, -sc, sc)
        b2 = jax.random.uniform(ks[8], (D,), jnp.float32, -sc, sc)
        return {'x': x, 'W0': W0, 'b0': b0, 'W1': W1, 'b1': b1, 'W2': W2, 'b2': b2, 'src': src, 'dst': dst}
    _L2_gnn_all = _L2_gnn_setup()
    _L2_gnn_in = {k: v for k, v in _L2_gnn_all.items() if k in ('W0', 'b0', 'W1', 'b1', 'W2', 'b2')}
    del _L2_gnn_all

    def _L3_gnn_setup():
        import jax, jax.numpy as jnp
        import numpy as np
        N_NODES = 50000

        def gcn_layer(x, src, dst, ew, W, b, n_nodes):
            loop = jnp.arange(n_nodes, dtype=src.dtype)
            s = jnp.concatenate([src, loop])
            d = jnp.concatenate([dst, loop])
            w = jnp.concatenate([ew, jnp.ones((n_nodes,), dtype=ew.dtype)])
            deg = jax.ops.segment_sum(w, d, num_segments=n_nodes)
            dinv = jnp.where(deg > 0, jax.lax.rsqrt(jnp.where(deg > 0, deg, 1.0)), 0.0)
            norm = dinv[s] * w * dinv[d]
            h = x @ W
            msg = h[s] * norm[:, None]
            out = jax.ops.segment_sum(msg, d, num_segments=n_nodes)
            return out + b
        key = jax.random.key(seed)
        k1, k2, k3, k4, k5, k6, k7 = jax.random.split(key, 7)
        N, E, C_IN, C_OUT = (N_NODES, 9375, 128, 128)
        x = jax.random.normal(k1, (N, C_IN), dtype=jnp.float32)
        edge_index = jax.random.randint(k2, (2, E), 0, N, dtype=jnp.int64)
        edge_weight = jax.random.uniform(k3, (E,), dtype=jnp.float32)
        s1 = 1.0 / np.sqrt(C_IN)
        s2 = 1.0 / np.sqrt(C_OUT)
        W1 = jax.random.uniform(k4, (C_IN, C_OUT), jnp.float32, -s1, s1)
        b1 = jnp.zeros((C_OUT,), dtype=jnp.float32)
        W2 = jax.random.uniform(k5, (C_OUT, C_OUT), jnp.float32, -s2, s2)
        b2 = jnp.zeros((C_OUT,), dtype=jnp.float32)
        return {'x': x, 'edge_index': edge_index, 'edge_weight': edge_weight, 'W1': W1, 'b1': b1, 'W2': W2, 'b2': b2}
    _L3_gnn_all = _L3_gnn_setup()
    _L3_gnn_in = {k: v for k, v in _L3_gnn_all.items() if k in ('W1', 'b1', 'W2', 'b2')}
    del _L3_gnn_all
    return {'x': x, 'src': src, 'dst': dst, 'edge_weight': edge_weight, 'L0_gnn_W1': _L0_gnn_in['W1'], 'L0_gnn_b1': _L0_gnn_in['b1'], 'L0_gnn_W2': _L0_gnn_in['W2'], 'L0_gnn_b2': _L0_gnn_in['b2'], 'L0_gnn_W3': _L0_gnn_in['W3'], 'L0_gnn_b3': _L0_gnn_in['b3'], 'L1_gnn_W_ih': _L1_gnn_in['W_ih'], 'L1_gnn_W_hh': _L1_gnn_in['W_hh'], 'L1_gnn_b_ih': _L1_gnn_in['b_ih'], 'L1_gnn_b_hh': _L1_gnn_in['b_hh'], 'L1_gnn_W1': _L1_gnn_in['W1'], 'L1_gnn_b1': _L1_gnn_in['b1'], 'L1_gnn_W2': _L1_gnn_in['W2'], 'L1_gnn_b2': _L1_gnn_in['b2'], 'L1_gnn_W3': _L1_gnn_in['W3'], 'L1_gnn_b3': _L1_gnn_in['b3'], 'L2_gnn_W0': _L2_gnn_in['W0'], 'L2_gnn_b0': _L2_gnn_in['b0'], 'L2_gnn_W1': _L2_gnn_in['W1'], 'L2_gnn_b1': _L2_gnn_in['b1'], 'L2_gnn_W2': _L2_gnn_in['W2'], 'L2_gnn_b2': _L2_gnn_in['b2'], 'L3_gnn_W1': _L3_gnn_in['W1'], 'L3_gnn_b1': _L3_gnn_in['b1'], 'L3_gnn_W2': _L3_gnn_in['W2'], 'L3_gnn_b2': _L3_gnn_in['b2']}

def reference(x, src, dst, edge_weight, L0_gnn_W1, L0_gnn_b1, L0_gnn_W2, L0_gnn_b2, L0_gnn_W3, L0_gnn_b3, L1_gnn_W_ih, L1_gnn_W_hh, L1_gnn_b_ih, L1_gnn_b_hh, L1_gnn_W1, L1_gnn_b1, L1_gnn_W2, L1_gnn_b2, L1_gnn_W3, L1_gnn_b3, L2_gnn_W0, L2_gnn_b0, L2_gnn_W1, L2_gnn_b1, L2_gnn_W2, L2_gnn_b2, L3_gnn_W1, L3_gnn_b1, L3_gnn_W2, L3_gnn_b2):
    import jax
    import jax.numpy as jnp

    def _L0_gnn_ref(x, edge_index, W1, b1, W2, b2, W3, b3):
        import jax, jax.numpy as jnp
        import numpy as np
        N_NODES = 50000
        N_EDGES = 12500
        D_IN = 128
        U = 128
        H = 128
        h = x @ W1 + b1
        src = edge_index[0]
        dst = edge_index[1]
        h_i = h[dst]
        h_j = h[src]
        e = jnp.concatenate([h_i, h_j - h_i], axis=-1)
        m = jax.nn.relu(e @ W2 + b2)
        m = jax.nn.relu(m @ W3 + b3)
        out = jax.ops.segment_max(m, dst, num_segments=N_NODES)
        return jax.nn.relu(out)

    def _L1_gnn_ref(z, edge_index, W_ih, W_hh, b_ih, b_hh, W1, b1, W2, b2, W3, b3):
        import jax, jax.numpy as jnp
        import numpy as np
        N = 100000
        E = 25000
        L = 128
        H = 128
        O = 128

        def _gcn_conv(x, W, b, src, dst, norm, n_nodes):
            h = x @ W
            msg = h[src] * norm[:, None]
            out = jax.ops.segment_sum(msg, dst, num_segments=n_nodes)
            return out + b

        def _lstm_step(z, W_ih, W_hh, b_ih, b_hh):
            gates = z @ W_ih.T + jnp.zeros((1, H), z.dtype) @ W_hh.T + b_ih + b_hh
            i, f, g, o = jnp.split(gates, 4, axis=-1)
            c = jax.nn.sigmoid(i) * jnp.tanh(g)
            return jax.nn.sigmoid(o) * jnp.tanh(c)
        n = z.shape[0]
        loop = jnp.arange(n, dtype=edge_index.dtype)
        src = jnp.concatenate([edge_index[0], loop])
        dst = jnp.concatenate([edge_index[1], loop])
        deg = jax.ops.segment_sum(jnp.ones_like(dst, dtype=z.dtype), dst, num_segments=n)
        dinv = jnp.where(deg > 0, jax.lax.rsqrt(deg), 0.0)
        norm = dinv[src] * dinv[dst]
        h = _lstm_step(z, W_ih, W_hh, b_ih, b_hh)
        x = jax.nn.relu(_gcn_conv(h, W1, b1, src, dst, norm, n))
        x = _gcn_conv(x, W2, b2, src, dst, norm, n)
        return jax.nn.relu(x @ W3.T + b3)

    def _L2_gnn_ref(x, W0, b0, W1, b1, W2, b2, src, dst):
        import jax, jax.numpy as jnp
        import numpy as np
        N = 50000
        E = 12500
        D = 128

        def _left_norm_agg(x, s, d, inv_deg_s, num_nodes):
            msg = (x * inv_deg_s[:, None])[s]
            return jax.ops.segment_sum(msg, d, num_segments=num_nodes)
        ones = jnp.ones((src.shape[0],), dtype=x.dtype)
        out_deg = jax.ops.segment_sum(ones, src, num_segments=N)
        in_deg = jax.ops.segment_sum(ones, dst, num_segments=N)
        inv_out = 1.0 / jnp.clip(out_deg, 1.0)
        inv_in = 1.0 / jnp.clip(in_deg, 1.0)
        params = [(W0, b0), (W1, b1), (W2, b2)]
        for i, (W, b) in enumerate(params):
            fwd = _left_norm_agg(x, src, dst, inv_out, N)
            bwd = _left_norm_agg(x, dst, src, inv_in, N)
            h = jnp.concatenate((x, fwd, bwd), axis=1)
            x = h @ W + b
            if i < len(params) - 1:
                x = jax.nn.relu(x)
        return x

    def _L3_gnn_ref(x, edge_index, edge_weight, W1, b1, W2, b2):
        import jax, jax.numpy as jnp
        import numpy as np
        N_NODES = 50000

        def gcn_layer(x, src, dst, ew, W, b, n_nodes):
            loop = jnp.arange(n_nodes, dtype=src.dtype)
            s = jnp.concatenate([src, loop])
            d = jnp.concatenate([dst, loop])
            w = jnp.concatenate([ew, jnp.ones((n_nodes,), dtype=ew.dtype)])
            deg = jax.ops.segment_sum(w, d, num_segments=n_nodes)
            dinv = jnp.where(deg > 0, jax.lax.rsqrt(jnp.where(deg > 0, deg, 1.0)), 0.0)
            norm = dinv[s] * w * dinv[d]
            h = x @ W
            msg = h[s] * norm[:, None]
            out = jax.ops.segment_sum(msg, d, num_segments=n_nodes)
            return out + b
        src, dst = (edge_index[0], edge_index[1])
        h = jax.nn.relu(gcn_layer(x, src, dst, edge_weight, W1, b1, N_NODES))
        return jax.nn.relu(gcn_layer(h, src, dst, edge_weight, W2, b2, N_NODES))
    edge_index = jnp.stack([src, dst])
    x = _layernorm(x + _L0_gnn_ref(x, edge_index, L0_gnn_W1, L0_gnn_b1, L0_gnn_W2, L0_gnn_b2, L0_gnn_W3, L0_gnn_b3), axis=-1)
    x = _layernorm(x + _L1_gnn_ref(x, edge_index, L1_gnn_W_ih, L1_gnn_W_hh, L1_gnn_b_ih, L1_gnn_b_hh, L1_gnn_W1, L1_gnn_b1, L1_gnn_W2, L1_gnn_b2, L1_gnn_W3, L1_gnn_b3), axis=-1)
    x = _layernorm(x + _L2_gnn_ref(x, L2_gnn_W0, L2_gnn_b0, L2_gnn_W1, L2_gnn_b1, L2_gnn_W2, L2_gnn_b2, src, dst), axis=-1)
    x = _layernorm(x + _L3_gnn_ref(x, edge_index, edge_weight, L3_gnn_W1, L3_gnn_b1, L3_gnn_W2, L3_gnn_b2), axis=-1)
    return x

_drawn_inputs = setup_inputs


def setup_inputs(seed=0):
    import zlib

    import numpy as np

    out = dict(_drawn_inputs(seed))
    spreads = {'L1_gnn_b1': (0.0, 0.512),
     'L1_gnn_b2': (0.0, 0.1),
     'L3_gnn_b1': (0.0, 0.296),
     'L3_gnn_b2': (0.0, 0.1)}
    factors = {'edge_weight': 2.711,
     'L0_gnn_b1': 43.801,
     'L0_gnn_b2': 28.263,
     'L0_gnn_b3': 22.119,
     'L1_gnn_W_ih': 6.129,
     'L1_gnn_b_ih': 8.0,
     'L1_gnn_b_hh': 8.0,
     'L1_gnn_W1': 6.045,
     'L1_gnn_W2': 2.834,
     'L2_gnn_b0': 23.397,
     'L2_gnn_b1': 6.681}
    for name, (base, spread) in spreads.items():
        noise = np.random.default_rng([zlib.crc32(name.encode()), seed]).standard_normal(out[name].shape)
        drawn = base * np.exp(spread * noise) if base else spread * noise
        out[name] = jnp.asarray(drawn.astype(out[name].dtype))
    for name, factor in factors.items():
        out[name] = (out[name] * factor).astype(out[name].dtype)
    return out
```

```python
from contextlib import ExitStack

import numpy as np

import concourse.bass as bass
import concourse.mybir as mybir

F32 = mybir.dt.float32
BF16 = mybir.dt.bfloat16
I32 = mybir.dt.int32
U32 = mybir.dt.uint32
ALU = mybir.AluOpType
ACT = mybir.ActivationFunctionType
AX = mybir.AxisListType.X

P = 128
N = 50000
E = 12500
D = 128
BLK = 512
Q = BLK // P
NB = 26
EP = NB * BLK
T = EP // P
HI, LO = 98, 512
PAD = HI * LO - 1
DP = 125
DB = N // (DP * Q)
LANES = 4
SCANS = (0, 2, 4, 6, 7, 9, 10, 12, 13, 15, 17)
EPS = 1e-5
PRIME = 64
SKIP = 60000
F_FULL, F_REST = E // P, E % P

N_ENDD, N_ENDS, N_DINV1, N_DINV3, N_INVOUT, N_INVIN, N_CNTD, NF = 0, 1, 2, 3, 4, 5, 6, 8
(R_DST, R_SRC, R_W, R_DINV1A, R_DINV3A, R_INVIN, R_ENDD_DST, R_ENDS_DST,
 R_DINV1B, R_DINV3B, R_INVOUT, R_ENDD_SRC, R_ENDS_SRC, R_CNTD_SRC, R_POSS) = range(15)
RF = 16
(C_SAMED, C_W, C_D1A, C_D1B, C_D3A, C_D3B, C_INVOUT, C_SAMES, C_INVIN) = range(9)
CF = 9


class Steps:

    def __init__(self, sems, base, steps, lanes):
        self.sems, self.base, self.lanes = sems, base, lanes
        self.order = {}
        for name, eng in steps:
            self.order.setdefault(eng, []).append(name)
        self.where = {n: (eng, k) for eng, names in self.order.items() for k, n in enumerate(names)}
        assert len(self.where) == len(steps)
        self.next = {(eng, c): 0 for eng in self.order for c in range(lanes)}

    def after(self, name, c, i):
        eng, k = self.where[name]
        return self.sems[eng][c], i * len(self.order[eng]) + (self.base[eng][c] + k + 1)

    def did(self, name, c):
        eng, k = self.where[name]
        assert self.next[eng, c] % len(self.order[eng]) == k, (name, c)
        self.next[eng, c] += 1
        return self.sems[eng][c]

    def close(self, n):
        for eng, names in self.order.items():
            for c in range(self.lanes):
                self.base[eng][c] += n * len(names)


class Arrivals:

    def __init__(self, sem, base=0):
        self.sem, self.base = sem, base

    def after(self, i, dmas=1):
        return self.sem, i * (16 * dmas) + (self.base + 16 * dmas)

    def close(self, n, dmas=1):
        self.base += 16 * dmas * n


def build(nc, a, out, upto=99, dbg=None):
    ctx = ExitStack()
    with ctx:
        def sb(name, shape, dt=F32):
            return ctx.enter_context(nc.sbuf_tensor(name, shape, dt))

        def sem(name):
            return ctx.enter_context(nc.semaphore(name))

        def dram(name, shape, dt=F32):
            return nc.dram_tensor(name, shape, dt).ap()

        node_tab = dram("node_tab", [HI * LO, NF])
        rec_d = dram("rec_d", [EP, RF])
        rec_s = dram("rec_s", [EP, RF])
        key_d = dram("key_d", [EP + P])
        key_s = dram("key_s", [EP + P])
        scal = dram("scal", [CF, NB, BLK])
        st_x = dram("st_x", [2, NB, P, BLK])
        st_v = dram("st_v", [2, NB, P, BLK])
        tab_f = dram("tab_f", [EP + P, D])
        tab_b = dram("tab_b", [EP + P, D])
        tab_u = dram("tab_u", [EP + P, D])

        def rows_of(tab):
            return tab[0:EP, :].rearrange("(j q p) f -> j p q f", q=Q, p=P)

        pidx = sb("pidx", [P, 1])
        iota_i = sb("iota_i", [P, LO], I32)
        iot = sb("iot", [P, LO])
        ident = sb("ident", [P, P])
        identb = sb("identb", [P, P], BF16)
        before = sb("before", [P, P])
        above = sb("above", [P, P])
        ones = sb("ones", [P, LO])
        mhalf = sb("mhalf", [P, LO])
        zero = sb("zero", [P, LO])
        zerob = sb("zerob", [P, LO], BF16)
        minus1 = sb("minus1", [1, P])
        wnames = ["L0_W1", "L0_W2a", "L0_W2b", "L0_W3", "Wi", "Wg", "Wo", "L1_W1", "L1_W23",
                  "W0x", "W0f", "W0b", "W1x", "W1f", "W1b", "W2x", "W2f", "W2b", "L3_W1", "L3_W2"]
        W = {n: sb("w_" + n, [P, P]) for n in wnames}
        bnames = ["L0_b1", "L0_b2", "L0_b3", "bi", "bg", "bo", "L1_b1", "L1_b23",
                  "L2_b0", "L2_b1", "L2_b2", "L3_b1", "L3_b2"]
        B = {n: sb("b_" + n, [P, 1]) for n in bnames}
        IX = {n: sb("ix_" + n, [P, T], I32) for n in ["xa", "xb", "end_f", "end_bb", "end_ba", "dst_in_s", "out_a", "out_b"]}

        K = [ctx.enter_context(nc.psum_tensor(f"bank{k}", [P, BLK], F32)) for k in range(8)]

        engs = ["pe", "act", "dve", "pool", "gather"]
        lane_sems = {e: [sem(f"{e}_lane{c}") for c in range(LANES)] for e in engs}
        lane_base = {e: [PRIME] * LANES for e in engs}
        arr = {n: [Arrivals(sem(f"{n}_arrived{c}")) for c in range(LANES)] for n in ["v", "x", "s", "g1", "g2", "s2"]}
        stored = {n: [Arrivals(sem(f"{n}_stored{c}")) for c in range(LANES)] for n in ["v", "x", "r"]}
        setup_dma = Arrivals(sem("setup_dma"))
        table_dma = Arrivals(sem("table_dma"))
        pool_dma = Arrivals(sem("pool_dma"))
        s_pool, s_dve, s_pe, s_act = sem("pool_setup"), sem("dve_setup"), sem("pe_setup"), sem("act_setup")
        cnt = {"pool": 0, "dve": 0, "pe": 0, "act": 0}
        handle = {"pool": s_pool, "dve": s_dve, "pe": s_pe, "act": s_act}

        class Mark:

            def __init__(self, eng):
                cnt[eng] += 1
                self.sem, self.value = handle[eng], cnt[eng]

        def setup():
            with ExitStack() as loc:
                def lb(name, shape, dt=F32):
                    return loc.enter_context(nc.sbuf_tensor(name, shape, dt))

                rows_i = lb("rows_i", [T, 2, P], I32)
                rows_h = lb("rows_h", [T, 2, P], I32)
                rows_l = lb("rows_l", [T, 2, P], I32)
                rows_f = lb("rows_f", [T, 7, P])
                cols = lb("cols", [P, 7, T])
                wraw = lb("wraw", [P, 6, P])
                wt = lb("wt", [P, 2, P])
                braw = lb("braw", [P, 6])
                b2s = lb("b2s", [P, 1])
                loads = sem_loads
                m_iota, m_one, m_mh, m_z = [Mark("pool") for _ in range(4)]
                with nc.Block() as block:
                    @block.gpsimd
                    def _(pool):
                        nc.gpsimd.iota(iota_i[:], pattern=[[1, LO]], base=0, channel_multiplier=0)
                        nc.gpsimd.iota(pidx_i[:], pattern=[[0, 1]], base=0, channel_multiplier=1).then_inc(s_pool, 1)
                        nc.gpsimd.memset(ones[:], 1.0).then_inc(s_pool, 1)
                        nc.gpsimd.memset(mhalf[:], -0.5).then_inc(s_pool, 1)
                        nc.gpsimd.memset(zero[:], 0.0).then_inc(s_pool, 1)
                        for c in range(LANES):
                            pool.sem_inc(lane_sems["pool"][c], PRIME)
                            pool.sem_inc(lane_sems["gather"][c], PRIME)

                    dve_pad = Mark("dve")

                    @block.vector
                    def _(dve):
                        nc.vector.memset(rows_i[:], PAD)
                        nc.vector.memset(rows_f[:, 6, :], 0.0)
                        nc.vector.memset(minus1[:], -1.0)
                        nc.vector.memset(zerob[:], 0.0).then_inc(s_dve, 1)
                        dve.wait_ge(s_pool, m_iota.value)
                        nc.vector.tensor_copy(pidx[:], pidx_i[:])
                        nc.vector.tensor_copy(iot[:], iota_i[:]).then_inc(s_dve, 1)
                        dve.wait_ge(s_dve, 2)
                        nc.vector.tensor_scalar(ident[:], iot[:, 0:P], pidx[:, 0:1], None, ALU.is_equal)
                        nc.vector.tensor_scalar(identb[:], iot[:, 0:P], pidx[:, 0:1], None, ALU.is_equal)
                        nc.vector.tensor_scalar(before[:], iot[:, 0:P], pidx[:, 0:1], None, ALU.is_lt)
                        nc.vector.tensor_scalar(above[:], iot[:, 0:P], pidx[:, 0:1], None, ALU.is_gt).then_inc(s_dve, 1)
                        dve.wait_ge(loads, 16 * 6)
                        nc.vector.tensor_scalar(rows_h[:], rows_i[:], 9, None, ALU.arith_shift_right)
                        nc.vector.tensor_scalar(rows_l[:], rows_i[:], LO - 1, None, ALU.bitwise_and)
                        nc.vector.tensor_copy(rows_f[:, 0:2, :], rows_i[:]).then_inc(s_dve, 1)
                        dve.wait_ge(s_dve, 4)
                        nc.vector.tensor_copy(rows_f[:, 2:4, :], rows_h[:])
                        nc.vector.tensor_copy(rows_f[:, 4:6, :], rows_l[:]).then_inc(s_dve, 1)
                        dve.wait_ge(s_pe, 1)
                        nc.vector.tensor_copy(cols[:, 0:4, :], K[0][:, 0:4 * T].rearrange("p (a b) -> p a b", b=T))
                        nc.vector.tensor_copy(cols[:, 4:7, :], K[1][:, 0:3 * T].rearrange("p (a b) -> p a b", b=T)).then_inc(s_dve, 1)
                        dve.wait_ge(s_pe, 2)
                        for k, n in enumerate(["Wi", "Wg", "Wo"]):
                            nc.vector.tensor_copy(W[n][:], K[2][:, k * P:(k + 1) * P])
                        nc.vector.tensor_copy(wt[:, 0, :], K[3][:, 0:P])
                        nc.vector.tensor_copy(wt[:, 1, :], K[3][:, P:2 * P]).then_inc(s_dve, 1)
                        nc.vector.tensor_tensor(braw[:, 0:3], braw[:, 0:3], braw[:, 3:6], ALU.add).then_inc(s_dve, 1)
                        dve.wait_ge(s_dve, 8)
                        dve.wait_ge(s_pe, 3)
                        nc.vector.tensor_copy(W["L1_W23"][:], K[4][:, 0:P])
                        nc.vector.tensor_tensor(B["L1_b23"][:], K[5][:, 0:1], b3raw[:], ALU.add)
                        for k, n in enumerate(["bi", "bg", "bo"]):
                            nc.vector.tensor_tensor(B[n][:], K[6][:, k:k + 1], braw[:, k:k + 1], ALU.add)
                        nc.vector.drain().then_inc(s_dve, 1)
                        for c in range(LANES):
                            dve.sem_inc(lane_sems["dve"][c], PRIME)

                    @block.sync
                    def _(sp):
                        sp.wait_ge(s_dve, 1)
                        for k, n in enumerate(["dst", "src"]):
                            sp.dma_start(rows_i[0:F_FULL, k, :], a[n][0:F_FULL * P].rearrange("(t p) -> t p", p=P)).then_inc(loads, 16)
                            sp.dma_start(rows_i[F_FULL:F_FULL + 1, k, 0:F_REST], a[n][F_FULL * P:E].rearrange("(t p) -> t p", t=1)).then_inc(loads, 16)
                        ew = a["edge_weight"]
                        sp.dma_start(rows_f[0:F_FULL, 6, :], ew[0:F_FULL * P].rearrange("(t p) -> t p", p=P)).then_inc(loads, 16)
                        sp.dma_start(rows_f[F_FULL:F_FULL + 1, 6, 0:F_REST], ew[F_FULL * P:E].rearrange("(t p) -> t p", t=1)).then_inc(loads, 16)
                        wih, whh = a["L1_gnn_W_ih"], a["L1_gnn_W_hh"]
                        for k, g in enumerate([0, 2, 3]):
                            sp.dma_start(wraw[:, k, :], wih[g * P:(g + 1) * P, :]).then_inc(loads2, 16)
                            sp.dma_start(whraw[:, k, :], whh[g * P:(g + 1) * P, :]).then_inc(loads2, 16)
                            sp.dma_start(braw[:, k:k + 1], a["L1_gnn_b_ih"][g * P:(g + 1) * P].unsqueeze(1)).then_inc(loads2, 16)
                            sp.dma_start(braw[:, 3 + k:4 + k], a["L1_gnn_b_hh"][g * P:(g + 1) * P].unsqueeze(1)).then_inc(loads2, 16)
                        sp.dma_start(wraw[:, 3, :], a["L1_gnn_W2"]).then_inc(loads2, 16)
                        sp.dma_start(wraw[:, 4, :], a["L1_gnn_W3"]).then_inc(loads2, 16)
                        sp.dma_start(b2s[:], a["L1_gnn_b2"].unsqueeze(1)).then_inc(loads2, 16)
                        sp.dma_start(b3raw[:], a["L1_gnn_b3"].unsqueeze(1)).then_inc(loads2, 16)
                        direct = [("L0_W1", a["L0_gnn_W1"]), ("L0_W2a", a["L0_gnn_W2"][0:P, :]), ("L0_W2b", a["L0_gnn_W2"][P:2 * P, :]),
                                  ("L0_W3", a["L0_gnn_W3"]), ("L1_W1", a["L1_gnn_W1"]), ("L3_W1", a["L3_gnn_W1"]), ("L3_W2", a["L3_gnn_W2"])]
                        for k in range(3):
                            for m, t in enumerate("xfb"):
                                direct.append((f"W{k}{t}", a[f"L2_gnn_W{k}"][m * P:(m + 1) * P, :]))
                        for n, src in direct:
                            sp.dma_start(W[n][:], src).then_inc(loads2, 16)
                        dbias = [("L0_b1", "L0_gnn_b1"), ("L0_b2", "L0_gnn_b2"), ("L0_b3", "L0_gnn_b3"), ("L1_b1", "L1_gnn_b1"),
                                 ("L2_b0", "L2_gnn_b0"), ("L2_b1", "L2_gnn_b1"), ("L2_b2", "L2_gnn_b2"), ("L3_b1", "L3_gnn_b1"), ("L3_b2", "L3_gnn_b2")]
                        for n, src in dbias:
                            sp.dma_start(B[n][:], a[src].unsqueeze(1)).then_inc(loads2, 16)
                        sp.wait_ge(loads2, 16 * N_LOADS2)
                        sp.wait_ge(s_pool, m_z.value)
                        for c in range(LANES):
                            for n, tab in (("v", tab_f), ("x", tab_b), ("r", tab_u)):
                                sp.dma_start(tab[EP + 32 * c:EP + 32 * c + 32, :], zero[0:32, 0:D]).then_inc(stored[n][c].sem, 16)
                        sp.dma_start(key_d[0:1].unsqueeze(0), minus1[0:1, 0:1]).then_inc(setup_dma.sem, 16)
                        sp.dma_start(key_s[0:1].unsqueeze(0), minus1[0:1, 0:1]).then_inc(setup_dma.sem, 16)
                        for c in range(LANES):
                            for n in ("v", "x", "r"):
                                sp.wait_ge(stored[n][c].sem, 16)
                                stored[n][c].base = 16
                        sp.wait_ge(setup_dma.sem, 32)
                        setup_dma.base = 32

                    @block.tensor
                    def _(pe):
                        pe.wait_ge(s_dve, 5)
                        for k in range(7):
                            last = nc.tensor.transpose(K[k // 4][:, (k % 4) * T:(k % 4 + 1) * T], rows_f[:, k, :], ident[0:T, 0:T])
                        last.then_inc(s_pe, 1)
                        pe.wait_ge(loads2, 16 * N_LOADS2)
                        for k in range(3):
                            nc.tensor.transpose(K[2][:, k * P:(k + 1) * P], wraw[:, k, :], ident[:])
                        nc.tensor.transpose(K[3][:, 0:P], wraw[:, 3, :], ident[:])
                        nc.tensor.transpose(K[3][:, P:2 * P], wraw[:, 4, :], ident[:]).then_inc(s_pe, 1)
                        pe.wait_ge(s_dve, 7)
                        nc.tensor.matmul(K[4][:, 0:P], wt[:, 0, :], wt[:, 1, :], start=True, stop=True)
                        nc.tensor.matmul(K[5][:, 0:1], wt[:, 1, :], b2s[:], start=True, stop=True)
                        for k in range(3):
                            last = nc.tensor.transpose(K[7][:, k * P:(k + 1) * P], whraw[:, k, :], ident[:])
                        last.then_inc(s_pe2, 1)
                        pe.wait_ge(s_act, 1)
                        pe.wait_ge(s_pool, m_z.value)
                        for k in range(3):
                            last = nc.tensor.matmul(K[6][:, k:k + 1], whT[:, k, :], zero[:, 0:1], start=True, stop=True)
                        last.then_inc(s_pe, 1)
                        for c in range(LANES):
                            pe.sem_inc(lane_sems["pe"][c], PRIME)

                    @block.scalar
                    def _(act):
                        act.wait_ge(s_pe2, 1)
                        nc.scalar.activation(whT[:].rearrange("p a b -> p (a b)"), K[7][:, 0:3 * P], ACT.Copy).then_inc(s_act, 1)
                        for c in range(LANES):
                            act.sem_inc(lane_sems["act"][c], PRIME)
                sort(cols, loc)

        def sort(cols, loc):
            def lb(name, shape, dt=F32):
                return loc.enter_context(nc.sbuf_tensor(name, shape, dt))

            oneh = [[lb(f"oneh{b}_{k}", [P, HI], BF16) for k in range(2)] for b in range(2)]
            onel = [[lb(f"onel{b}_{k}", [P, LO], BF16) for k in range(2)] for b in range(2)]
            onehf = [lb(f"onehf{b}", [P, HI]) for b in range(2)]
            onelw = [lb(f"onelw{b}", [P, LO]) for b in range(2)]
            hist = lb("hist", [HI, 3, LO])
            base = lb("base", [HI, 2, LO])
            rowtot = lb("rowtot", [HI, 2])
            rowbase = lb("rowbase", [HI, 2])
            nt = lb("nt", [HI, LO, NF])
            t1 = lb("t1", [HI, LO])
            t2 = lb("t2", [HI, LO])
            t3 = lb("t3", [HI, LO])
            t4 = lb("t4", [HI, LO])

            with nc.Block() as block:
                @block.vector
                def _(dve):
                    with dve.Fori(0, T // 2) as i:
                        for b in range(2):
                            t = i * 2 + b
                            dve.wait_ge(hist_done, t + 1)
                            for k in range(2):
                                nc.vector.tensor_scalar(oneh[b][k][:], iot[:, 0:HI], cols[:, 2 + k, bass.ds(t, 1)], None, ALU.is_equal)
                                nc.vector.tensor_scalar(onel[b][k][:], iot[:], cols[:, 4 + k, bass.ds(t, 1)], None, ALU.is_equal)
                            nc.vector.tensor_scalar(onehf[b][:], iot[:, 0:HI], cols[:, 2, bass.ds(t, 1)], None, ALU.is_equal)
                            nc.vector.tensor_scalar(onelw[b][:], iot[:], cols[:, 4, bass.ds(t, 1)], cols[:, 6, bass.ds(t, 1)],
                                                    ALU.is_equal, ALU.mult).then_inc(onehots_ready, 1)
                    dve.wait_ge(hist_done, T + 3)
                    for k in range(3):
                        last = nc.vector.tensor_copy(hist[:, k, :], K[k][0:HI, :])
                    last.then_inc(s_dve, 1)

                @block.tensor
                def _(pe):
                    for k in range(3):
                        last = nc.tensor.matmul(K[k][0:HI, :], zerob[:, 0:HI], zerob[:], start=True, stop=False)
                        if k:
                            last.then_inc(hist_done, 1)
                    with pe.Fori(0, T // 2) as i:
                        for b in range(2):
                            pe.wait_ge(onehots_ready, i * 2 + (b + 1))
                            for k in range(2):
                                nc.tensor.matmul(K[k][0:HI, :], oneh[b][k][:], onel[b][k][:], start=False, stop=False)
                            nc.tensor.matmul(K[2][0:HI, :], onehf[b][:], onelw[b][:], start=False, stop=False).then_inc(hist_done, 1)
                    for k in range(3):
                        last = nc.tensor.matmul(K[k][0:HI, :], zerob[:, 0:HI], zerob[:], start=False, stop=True)
                    last.then_inc(hist_done, 1)

            d0 = 10
            with nc.Block() as block:
                @block.vector
                def _(dve):
                    n = [d0]

                    def link(ins):
                        n[0] += 1
                        ins.then_inc(s_dve, 1)
                        dve.wait_ge(s_dve, n[0])

                    link(nc.vector.tensor_reduce(rowtot[:], hist[:, 0:2, :], AX, ALU.add))
                    dve.wait_ge(s_pe, 4)
                    link(nc.vector.tensor_copy(rowbase[:], K[3][0:HI, 0:2]))
                    for k in range(2):
                        link(nc.vector.tensor_tensor_scan(t1[:], ones[0:HI, :], hist[:, k, :], rowbase[:, k:k + 1], ALU.mult, ALU.add))
                        nc.vector.tensor_tensor(base[:, k, :], t1[:], hist[:, k, :], ALU.subtract)
                        link(nc.vector.tensor_scalar(t2[:], hist[:, k, :], 1.0, None, ALU.min))
                        link(nc.vector.scalar_tensor_tensor(t3[:], t1[:], float(-1 - EP), t2[:], ALU.add, ALU.mult))
                        link(nc.vector.tensor_scalar(nt[:, :, N_ENDD + k], t3[:], float(EP), None, ALU.add))
                        link(nc.vector.tensor_scalar(t4[:], hist[:, k, :], 1.0, None, ALU.max))
                        link(nc.vector.reciprocal(nt[:, :, N_INVIN if k == 0 else N_INVOUT], t4[:]))
                    nc.vector.tensor_copy(nt[:, :, N_CNTD], hist[:, 0, :])
                    nc.vector.tensor_scalar(nt[:, :, 7], hist[:, 0, :], 0.0, None, ALU.mult)
                    link(nc.vector.tensor_scalar(t1[:], hist[:, 0, :], 1.0, None, ALU.add))
                    link(nc.vector.tensor_scalar(t2[:], hist[:, 2, :], 1.0, None, ALU.add))
                    link(nc.vector.tensor_scalar(t3[:], t2[:], 0.0, None, ALU.is_gt))
                    link(nc.vector.tensor_scalar(t4[:], t3[:], -1.0, 1.0, ALU.mult, ALU.add))
                    link(nc.vector.tensor_tensor(t2[:], t2[:], t3[:], ALU.mult))
                    link(nc.vector.tensor_tensor(t2[:], t2[:], t4[:], ALU.add))
                    dve.sem_inc(degrees_ready, 1)
                    dve.wait_ge(s_pool, 6)
                    nc.vector.tensor_copy(nt[:, :, N_DINV1], hist[:, 0, :])
                    link(nc.vector.tensor_tensor(nt[:, :, N_DINV3], hist[:, 1, :], t3[:], ALU.mult))

                @block.gpsimd
                def _(pool):
                    pool.wait_ge(degrees_ready, 1)
                    nc.gpsimd.tensor_tensor(hist[:, 0, :], t1[:], mhalf[0:HI, :], ALU.pow).then_inc(s_pool, 1)
                    nc.gpsimd.tensor_tensor(hist[:, 1, :], t2[:], mhalf[0:HI, :], ALU.pow).then_inc(s_pool, 1)

                @block.tensor
                def _(pe):
                    pe.wait_ge(s_dve, d0 + 1)
                    nc.tensor.matmul(K[3][0:HI, 0:2], above[0:HI, 0:HI], rowtot[:], start=True, stop=True).then_inc(s_pe, 1)

                @block.sync
                def _(sp):
                    sp.wait_ge(s_dve, d0 + 2 + 2 * 6 + 7)
                    sp.dma_start(node_tab.rearrange("(h l) f -> h (l f)", h=HI), nt[:].rearrange("h l f -> h (l f)")).then_inc(setup_dma.sem, 16)
                    sp.wait_ge(setup_dma.sem, 48)
                    setup_dma.base = 48

            pos = lb("pos", [P, 2, T])
            ohT = [lb(f"ohT{k}", [HI, P]) for k in range(2)]
            kc = [lb(f"kc{k}", [P, 1]) for k in range(2)]
            kbc = [lb(f"kbc{k}", [P, P]) for k in range(2)]
            pick = [lb(f"pick{k}", [P, LO]) for k in range(2)]
            tie = [lb(f"tie{k}", [P, P]) for k in range(2)]
            acc = [lb(f"acc{k}", [P, 2]) for k in range(2)]
            rank_steps = [("hots", "dve"), ("trans", "pe"), ("ohT", "act"), ("look", "pe"), ("tie", "dve"),
                          ("pick", "dve"), ("pos", "dve"), ("base", "dve")]
            S = Steps(lane_sems, lane_base, rank_steps, 2)
            bank = [[K[4 * k + m] for m in range(4)] for k in range(2)]
            with nc.Block() as block:
                @block.vector
                def _(dve):
                    with dve.Fori(0, T) as t:
                        for k in range(2):
                            dve.wait_ge(*S.after("look", k, t - 1))
                            nc.vector.tensor_scalar(onehf[k][:], iot[:, 0:HI], cols[:, 2 + k, bass.ds(t, 1)], None, ALU.is_equal)
                            nc.vector.tensor_scalar(oneh[0][k][:], iot[:, 0:HI], cols[:, 2 + k, bass.ds(t, 1)], None, ALU.is_equal)
                            nc.vector.tensor_scalar(onel[0][k][:], iot[:], cols[:, 4 + k, bass.ds(t, 1)], None, ALU.is_equal)
                            nc.vector.tensor_copy(kc[k][:], cols[:, k, bass.ds(t, 1)])
                            nc.vector.tensor_scalar(kbc[k][:], ones[:, 0:P], cols[:, k, bass.ds(t, 1)], None, ALU.mult).then_inc(S.did("hots", k), 1)
                        for k in range(2):
                            dve.wait_ge(*S.after("hots", k, t))
                            dve.wait_ge(*S.after("trans", k, t))
                            nc.vector.scalar_tensor_tensor(tie[k][:], bank[k][1][:, 0:P], kc[k][:, 0:1], before[:], ALU.is_equal, ALU.mult,
                                                           accum_out=acc[k][:, 0:1]).then_inc(S.did("tie", k), 1)
                            dve.wait_ge(*S.after("look", k, t))
                            nc.vector.scalar_tensor_tensor(pick[k][:], bank[k][2][:], 1.0, onel[0][k][:], ALU.mult, ALU.mult,
                                                           accum_out=acc[k][:, 1:2]).then_inc(S.did("pick", k), 1)
                            dve.wait_ge(*S.after("pick", k, t))
                            nc.vector.tensor_tensor(pos[:, k, bass.ds(t, 1)], acc[k][:, 0:1], acc[k][:, 1:2], ALU.add).then_inc(S.did("pos", k), 1)
                            nc.vector.tensor_tensor(base[:, k, :], base[:, k, :], bank[k][3][0:HI, :], ALU.add).then_inc(S.did("base", k), 1)

                @block.tensor
                def _(pe):
                    with pe.Fori(0, T) as t:
                        for k in range(2):
                            pe.wait_ge(*S.after("hots", k, t))
                            pe.wait_ge(*S.after("base", k, t - 1))
                            nc.tensor.transpose(bank[k][0][0:HI, 0:P], onehf[k][:], ident[:])
                            nc.tensor.transpose(bank[k][1][:, 0:P], kbc[k][:], ident[:]).then_inc(S.did("trans", k), 1)
                        for k in range(2):
                            nc.tensor.matmul(bank[k][3][0:HI, :], oneh[0][k][:], onel[0][k][:], start=True, stop=True)
                            pe.wait_ge(*S.after("ohT", k, t))
                            nc.tensor.matmul(bank[k][2][:], ohT[k][:], base[:, k, :], start=True, stop=True).then_inc(S.did("look", k), 1)

                @block.scalar
                def _(act):
                    with act.Fori(0, T) as t:
                        for k in range(2):
                            act.wait_ge(*S.after("trans", k, t))
                            nc.scalar.activation(ohT[k][:], bank[k][0][0:HI, 0:P], ACT.Copy).then_inc(S.did("ohT", k), 1)
            S.close(T)
            records(cols, pos, loc)

        def records(cols, pos, loc):
            def lb(name, shape, dt=F32):
                return loc.enter_context(nc.sbuf_tensor(name, shape, dt))

            G = 8
            idx_i = lb("idx_i", [P, 4, T], I32)
            rec = lb("rec", [P, T, RF])
            idx_g = lb("idx_g", [P, 2, G], I32)
            got = [lb(f"got{k}", [P, G, NF]) for k in range(2)]
            part = lb("part", [P, G, RF])
            m0 = {"dve": d0 + 2 + 2 * 6 + 7 + 1, "pool": 6}
            rd_c = lb("rd_c", [P, T, RF])
            rs_c = lb("rs_c", [P, T, RF])
            with nc.Block() as block:
                @block.vector
                def _(dve):
                    nc.vector.tensor_copy(idx_i[:, 0:2, :], cols[:, 0:2, :])
                    nc.vector.tensor_copy(idx_i[:, 2:4, :], pos[:])
                    nc.vector.tensor_copy(rec[:, :, R_DST], cols[:, 0, :])
                    nc.vector.tensor_copy(rec[:, :, R_SRC], cols[:, 1, :])
                    nc.vector.tensor_copy(rec[:, :, R_W], cols[:, 6, :])
                    nc.vector.tensor_copy(rec[:, :, R_POSS], pos[:, 1, :])
                    nc.vector.tensor_scalar(rec[:, :, 15], pos[:, 1, :], 0.0, None, ALU.mult).then_inc(rec_ready, 1)

                @block.gpsimd
                def _(pool):
                    pool.wait_ge(rec_ready, 1)
                    pool.sem_inc(copied, 1)
                    with pool.Fori(0, T // G) as r:
                        pool.wait_ge(copied, r * 3 + 1)
                        pool.sem_inc(pool_passed, 1)
                        nc.gpsimd.tensor_copy(idx_g[:], idx_i[:, 0:2, bass.ds(r * G, G)]).then_inc(copied, 1)
                        pool.wait_ge(copied, r * 3 + 2)
                        pool.sem_inc(pool_passed, 1)
                        for k in range(2):
                            for g in range(G):
                                nc.gpsimd.indirect_dma_start(
                                    out=got[k][:, g, :], out_offset=None, in_=node_tab,
                                    in_offset=bass.IndirectOffsetOnAxis(ap=idx_g[:, k, g:g + 1].bitcast(U32), axis=0),
                                    bounds_check=HI * LO - 1, oob_is_err=False).then_inc(pool_dma.sem, 16)
                        pool.wait_ge(pool_dma.sem, r * (32 * G) + 32 * G)
                        pool.sem_inc(pool_passed, 1)
                        view = rec[:, bass.ds(r * G, G), :]
                        for dst, side, src in ((R_DINV1A, 0, N_DINV1), (R_DINV3A, 0, N_DINV3), (R_INVIN, 0, N_INVIN),
                                               (R_ENDD_DST, 0, N_ENDD), (R_ENDS_DST, 0, N_ENDS),
                                               (R_DINV1B, 1, N_DINV1), (R_DINV3B, 1, N_DINV3), (R_INVOUT, 1, N_INVOUT),
                                               (R_ENDD_SRC, 1, N_ENDD), (R_ENDS_SRC, 1, N_ENDS)):
                            nc.gpsimd.tensor_copy(view[:, :, dst:dst + 1], got[side][:, :, src:src + 1])
                        nc.gpsimd.tensor_copy(view[:, :, R_CNTD_SRC:R_CNTD_SRC + 1], got[1][:, :, N_CNTD:N_CNTD + 1]).then_inc(copied, 1)
                        pool.wait_ge(copied, r * 3 + 3)
                        pool.sem_inc(copied, 1)
                    pool.wait_ge(copied, (T // G) * 3 + 1)
                    with pool.Fori(0, T // G) as r:
                        nc.gpsimd.tensor_copy(part[:], rec[:, bass.ds(r * G, G), :])
                        nc.gpsimd.tensor_copy(idx_g[:], idx_i[:, 2:4, bass.ds(r * G, G)]).then_inc(copied, 1)
                        pool.wait_ge(copied, r + ((T // G) * 3 + 2))
                        pool.sem_inc(pool_passed, 1)
                        for k, tab in enumerate((rec_d, rec_s)):
                            for g in range(G):
                                nc.gpsimd.indirect_dma_start(
                                    out=tab, out_offset=bass.IndirectOffsetOnAxis(ap=idx_g[:, k, g:g + 1].bitcast(U32), axis=0),
                                    in_=part[:, g, :], in_offset=None, bounds_check=EP - 1, oob_is_err=False).then_inc(pool_dma.sem, 16)
                        pool.wait_ge(pool_dma.sem, r * (32 * G) + (T // G + 1) * 32 * G)
                        pool.sem_inc(pool_passed, 1)
                    pool_dma.base = 2 * (T // G) * 32 * G

            sd_r = lb("sd_r", [T, 12, P])
            prev = lb("prev", [T, 2, P])
            e_pos = lb("e_pos", [P, T])
            e_pos_i = lb("e_pos_i", [P, T], I32)
            u1 = lb("u1", [P, T])
            u2 = lb("u2", [P, T])
            u3 = lb("u3", [P, T])
            with nc.Block() as block:
                @block.sync
                def _(sp):
                    sp.dma_start(rd_c[:], rec_d.rearrange("(t p) f -> p t f", p=P)).then_inc(setup_dma.sem, 16)
                    sp.dma_start(rs_c[:], rec_s.rearrange("(t p) f -> p t f", p=P)).then_inc(setup_dma.sem, 16)
                    sp.wait_ge(rows_done, 3)
                    sp.dma_start(key_d[1:1 + EP].rearrange("(t p) -> t p", p=P), sd_r[:, 0, :]).then_inc(setup_dma.sem, 16)
                    sp.dma_start(key_s[1:1 + EP].rearrange("(t p) -> t p", p=P), sd_r[:, 7, :]).then_inc(setup_dma.sem, 16)
                    sp.wait_ge(setup_dma.sem, 48 + 64)
                    sp.dma_start(prev[:, 0, :], key_d[0:EP].rearrange("(t p) -> t p", p=P)).then_inc(setup_dma.sem, 16)
                    sp.dma_start(prev[:, 1, :], key_s[0:EP].rearrange("(t p) -> t p", p=P)).then_inc(setup_dma.sem, 16)
                    sp.wait_ge(same_done, 1)
                    sc = scal.rearrange("c j b -> c (j b)").rearrange("c (t p) -> c t p", p=P)
                    for c, row in ((C_SAMED, 9), (C_W, 1), (C_D1A, 2), (C_D1B, 3), (C_D3A, 4), (C_D3B, 5), (C_INVOUT, 6),
                                   (C_SAMES, 10), (C_INVIN, 8)):
                        sp.dma_start(sc[c], sd_r[:, row, :]).then_inc(setup_dma.sem, 16)
                    sp.wait_ge(setup_dma.sem, 48 + 64 + 32 + 16 * CF)
                    setup_dma.base = 48 + 64 + 32 + 16 * CF

                @block.tensor
                def _(pe):
                    pe.wait_ge(setup_dma.sem, 48 + 32)
                    fields = [(rd_c, R_DST), (rd_c, R_W), (rd_c, R_DINV1A), (rd_c, R_DINV1B), (rd_c, R_DINV3A), (rd_c, R_DINV3B),
                              (rd_c, R_INVOUT), (rs_c, R_SRC), (rs_c, R_INVIN)]
                    for n, (src, f) in enumerate(fields):
                        last = nc.tensor.transpose(K[n // 4][0:T, (n % 4) * P:(n % 4 + 1) * P], src[:, :, f], ident[:])
                        if n % 4 == 3 or n == 8:
                            last.then_inc(rows_T, 1)

                @block.scalar
                def _(act):
                    for n in range(3):
                        w = 4 if n < 2 else 1
                        act.wait_ge(rows_T, n + 1)
                        nc.scalar.activation(sd_r[:, 4 * n:4 * n + w, :].rearrange("t a b -> t (a b)"), K[n][0:T, 0:w * P], ACT.Copy).then_inc(rows_done, 1)

                @block.gpsimd
                def _(pool):
                    nc.gpsimd.iota(e_pos_i[:], pattern=[[P, T]], base=0, channel_multiplier=1).then_inc(copied, 1)

                @block.vector
                def _(dve):
                    n = [0]

                    def link(ins):
                        n[0] += 1
                        ins.then_inc(lists_dve, 1)
                        dve.wait_ge(lists_dve, n[0])

                    dve.wait_ge(setup_dma.sem, 48 + 32)
                    dve.wait_ge(copied, (T // G) * 4 + 2)
                    nc.vector.tensor_copy(e_pos[:], e_pos_i[:])
                    nc.vector.tensor_scalar(IX["xa"][:], rd_c[:, :, R_DST], float(N - 1), None, ALU.min)
                    nc.vector.tensor_scalar(IX["xb"][:], rd_c[:, :, R_SRC], float(N - 1), None, ALU.min)
                    nc.vector.tensor_copy(IX["end_f"][:], rd_c[:, :, R_ENDD_SRC])
                    nc.vector.tensor_copy(IX["end_bb"][:], rd_c[:, :, R_ENDS_SRC])
                    nc.vector.tensor_copy(IX["end_ba"][:], rd_c[:, :, R_ENDS_DST])
                    nc.vector.tensor_copy(IX["dst_in_s"][:], rs_c[:, :, R_ENDD_DST])
                    link(nc.vector.tensor_scalar(u1[:], rd_c[:, :, R_DST], float(N - 1), None, ALU.is_le))
                    link(nc.vector.tensor_tensor(u2[:], e_pos[:], rd_c[:, :, R_ENDD_DST], ALU.is_equal))
                    link(nc.vector.tensor_tensor(u1[:], u1[:], u2[:], ALU.mult))
                    link(nc.vector.scalar_tensor_tensor(u3[:], rd_c[:, :, R_DST], float(-SKIP), u1[:], ALU.add, ALU.mult))
                    link(nc.vector.tensor_scalar(IX["out_a"][:], u3[:], float(SKIP), None, ALU.add))
                    link(nc.vector.tensor_scalar(u1[:], rd_c[:, :, R_SRC], float(N - 1), None, ALU.is_le))
                    link(nc.vector.tensor_tensor(u2[:], rd_c[:, :, R_POSS], rd_c[:, :, R_ENDS_SRC], ALU.is_equal))
                    link(nc.vector.tensor_tensor(u1[:], u1[:], u2[:], ALU.mult))
                    link(nc.vector.tensor_scalar(u2[:], rd_c[:, :, R_CNTD_SRC], 0.0, None, ALU.is_equal))
                    link(nc.vector.tensor_tensor(u1[:], u1[:], u2[:], ALU.mult))
                    link(nc.vector.scalar_tensor_tensor(u3[:], rd_c[:, :, R_SRC], float(-SKIP), u1[:], ALU.add, ALU.mult))
                    link(nc.vector.tensor_scalar(IX["out_b"][:], u3[:], float(SKIP), None, ALU.add))
                    dve.wait_ge(setup_dma.sem, 48 + 64 + 32)
                    dve.wait_ge(rows_done, 3)
                    nc.vector.tensor_tensor(sd_r[:, 9, :], sd_r[:, 0, :], prev[:, 0, :], ALU.is_equal)
                    nc.vector.tensor_tensor(sd_r[:, 10, :], sd_r[:, 7, :], prev[:, 1, :], ALU.is_equal).then_inc(same_done, 1)

        pidx_i = sb("pidx_i", [P, 1], I32)
        whraw = sb("whraw", [P, 3, P])
        whT = sb("whT", [P, 3, P])
        b3raw = sb("b3raw", [P, 1])
        sem_loads, loads2 = sem("edges_loaded"), sem("weights_loaded")
        N_LOADS2 = 12 + 4 + 16 + 9
        s_pe2 = sem("whh_transposed")
        hist_done, onehots_ready = sem("hist_done"), sem("onehots_ready")
        degrees_ready, rec_ready, copied = sem("degrees_ready"), sem("rec_ready"), sem("copied")
        rows_T, rows_done, same_done, lists_dve = sem("rows_T"), sem("rows_done"), sem("same_done"), sem("lists_dve")
        pool_passed = sem("pool_passed")
        dve_passed = sem("dve_passed")
        d0 = 10
        setup()
        if upto <= 0:
            return
        def lanes(name, shape=(P, BLK), dt=F32):
            return [sb(f"{name}{c}", list(shape), dt) for c in range(LANES)]

        LV, LX, LS, LT = lanes("in_v"), lanes("in_x"), lanes("in_scale"), lanes("in_same")
        G1, G2 = lanes("rows_f"), lanes("rows_b")
        GI = [[sb(f"gidx{m}_{c}", [P, Q], I32) for c in range(LANES)] for m in range(2)]
        B1, B2, Z = lanes("b1_"), lanes("b2_"), lanes("z_")
        OX, OV, R = lanes("out_x"), lanes("out_v"), lanes("out_rows")
        ST = lanes("stats", (P, Q, 6))
        MV = lanes("mean_var", (P, Q, 2))
        VE = lanes("var_eps", (P, Q))
        RS = lanes("rstd", (P, Q))
        sig = [sb(f"sig_o{c}", [P, BLK]) for c in range(LANES)]

        def tile_cols(buf, q, w=P):
            return buf[:, q * w:(q + 1) * w]

        def transposes(dst, src, rows=P, cols_=P):
            for q in range(Q):
                last = nc.tensor.transpose(dst[0:cols_, q * rows:(q + 1) * rows], src[0:rows, q * cols_:(q + 1) * cols_], ident[0:rows, 0:rows])
            return last

        def rows_out_view(tab, j):
            return rows_of(tab)[j]

        def bcast(c, j):
            return scal[c, j].partition_broadcast(P)

        LN = lambda t: [("lnT" + t, "pe"), ("stats" + t, "dve"), ("aggr" + t, "dve"), ("eps" + t, "dve"), ("rstd" + t, "pool"), ("norm" + t, "dve")]

        def ln_stats(dve, S, c, i, t, src, before_, pp):
            if before_:
                dve.wait_ge(*S.after(before_, c, i))
            for q in range(Q):
                last = nc.vector.bn_stats(ST[c][0:pp, q, :], src[0:pp, q * D:(q + 1) * D])
            last.then_inc(S.did("stats" + t, c), 1)
            dve.wait_ge(*S.after("stats" + t, c, i))
            dve.sem_inc(dve_passed, 1)
            for q in range(Q):
                last = nc.vector.bn_aggr(MV[c][0:pp, q, :], ST[c][0:pp, q, :])
            last.then_inc(S.did("aggr" + t, c), 1)
            dve.wait_ge(*S.after("aggr" + t, c, i))
            nc.vector.tensor_scalar(VE[c][0:pp, :], MV[c][0:pp, :, 1], EPS, None, ALU.add).then_inc(S.did("eps" + t, c), 1)

        def ln_rstd(pool, S, c, i, t, pp):
            pool.wait_ge(*S.after("eps" + t, c, i))
            nc.gpsimd.tensor_tensor(RS[c][0:pp, :], VE[c][0:pp, :], mhalf[0:pp, 0:Q], ALU.pow).then_inc(S.did("rstd" + t, c), 1)

        def ln_norm(dve, S, c, i, t, src, dst, pp):
            dve.wait_ge(*S.after("rstd" + t, c, i))
            for q in range(Q):
                last = nc.vector.tensor_scalar(dst[0:pp, q * D:(q + 1) * D], src[0:pp, q * D:(q + 1) * D],
                                               MV[c][0:pp, q, 0:1], RS[c][0:pp, q:q + 1], ALU.subtract, ALU.mult)
            last.then_inc(S.did("norm" + t, c), 1)

        LSTM = [("gates", "pe"), ("sig_i", "act"), ("tanh_g", "act"), ("cell", "dve"), ("gate_o", "pe"), ("sig_o", "act"), ("tanh_c", "act"), ("h", "dve")]

        def lstm_gates(pe, S, c, i, x, before_, w):
            pe.wait_ge(*S.after(before_, c, i))
            nc.tensor.matmul(K[2 * c + 1][:, 0:w], W["Wi"][:], x[:, 0:w], start=True, stop=True)
            nc.tensor.matmul(K[2 * c][:, 0:w], W["Wg"][:], x[:, 0:w], start=True, stop=True).then_inc(S.did("gates", c), 1)

        def lstm_gate_o(pe, S, c, i, x, w):
            pe.wait_ge(*S.after("sig_i", c, i))
            nc.tensor.matmul(K[2 * c + 1][:, 0:w], W["Wo"][:], x[:, 0:w], start=True, stop=True).then_inc(S.did("gate_o", c), 1)

        def lstm_act_ig(act, S, c, i, w):
            act.wait_ge(*S.after("gates", c, i))
            nc.scalar.activation(B1[c][:, 0:w], K[2 * c + 1][:, 0:w], ACT.Sigmoid, bias=B["bi"][:]).then_inc(S.did("sig_i", c), 1)
            nc.scalar.activation(B2[c][:, 0:w], K[2 * c][:, 0:w], ACT.Tanh, bias=B["bg"][:]).then_inc(S.did("tanh_g", c), 1)

        def lstm_act_oc(act, S, c, i, w):
            act.wait_ge(*S.after("gate_o", c, i))
            nc.scalar.activation(sig[c][:, 0:w], K[2 * c + 1][:, 0:w], ACT.Sigmoid, bias=B["bo"][:]).then_inc(S.did("sig_o", c), 1)
            act.wait_ge(*S.after("cell", c, i))
            nc.scalar.activation(B2[c][:, 0:w], B1[c][:, 0:w], ACT.Tanh).then_inc(S.did("tanh_c", c), 1)

        def lstm_cell(dve, S, c, i, w):
            dve.wait_ge(*S.after("tanh_g", c, i))
            nc.vector.tensor_tensor(B1[c][:, 0:w], B1[c][:, 0:w], B2[c][:, 0:w], ALU.mult).then_inc(S.did("cell", c), 1)

        def lstm_h(dve, S, c, i, w):
            dve.wait_ge(*S.after("tanh_c", c, i))
            nc.vector.tensor_tensor(B1[c][:, 0:w], B2[c][:, 0:w], sig[c][:, 0:w], ALU.mult).then_inc(S.did("h", c), 1)

        def gather(pool, S, c, i, free, streams):
            j = i * 2 + (c & 1)
            pool.wait_ge(*S.after(free, c, i - 1))
            pool.sem_inc(pool_passed, 1)
            for m, (lst, tab, dst, stream) in enumerate(streams):
                last = nc.gpsimd.tensor_copy(GI[m][c][:], IX[lst][:, bass.ds(j * Q, Q)])
            last.then_inc(S.did("idx", c), 1)
            pool.wait_ge(*S.after("idx", c, i))
            pool.sem_inc(pool_passed, 1)
            for m, (lst, tab, dst, stream) in enumerate(streams):
                rows = tab.shape[0]
                for q in range(Q):
                    nc.gpsimd.indirect_dma_start(out=dst[c][:, q * D:(q + 1) * D], out_offset=None, in_=tab,
                                                 in_offset=bass.IndirectOffsetOnAxis(ap=GI[m][c][:, q:q + 1].bitcast(U32), axis=0),
                                                 bounds_check=rows - 1, oob_is_err=False).then_inc(arr[stream][c].sem, 16)

        NI = NB // 2

        def edge_stage():
            steps = [("idx", "gather"), ("inT", "pe"), ("xa", "act"), ("xb", "dve"), ("proj", "pe"), ("hi", "act"), ("d", "dve"), ("mlp1", "pe"),
                     ("m1", "act"), ("mlp2", "pe"), ("m2", "act"), ("scan", "dve"), ("rowsT", "pe"), ("rows", "act")]
            S = Steps(lane_sems, lane_base, steps, 2)
            KK = [[K[4 * c + m] for m in range(4)] for c in range(2)]
            with nc.Block() as block:
                @block.gpsimd
                def _(pool):
                    with pool.Fori(0, NI) as i:
                        for c in range(2):
                            gather(pool, S, c, i, "inT", [("xa", a["x"], G1, "g1"), ("xb", a["x"], G2, "g2")])

                @block.sync
                def _(sp):
                    def load(c, i):
                        sp.wait_ge(*S.after("scan", c, i - 1))
                        sp.dma_start(LT[c][:], bcast(C_SAMED, i * 2 + c)).then_inc(arr["s2"][c].sem, 16)

                    def store(c, i):
                        j = i * 2 + c
                        sp.wait_ge(*S.after("xa", c, i))
                        sp.dma_start(st_x[0, j], OX[c][:]).then_inc(stored["x"][c].sem, 16)
                        sp.wait_ge(*S.after("xb", c, i))
                        sp.dma_start(st_x[1, j], OV[c][:]).then_inc(stored["v"][c].sem, 16)
                        sp.wait_ge(*S.after("rows", c, i))
                        sp.dma_start(rows_out_view(tab_f, j), R[c][:].rearrange("p (q f) -> p q f", q=Q)).then_inc(stored["r"][c].sem, 16)

                    for c in range(2):
                        load(c, 0)
                    with sp.Fori(0, NI - 1) as i:
                        for c in range(2):
                            store(c, i)
                            load(c, i + 1)
                    for c in range(2):
                        store(c, NI - 1)
                        for n in ("x", "v", "r"):
                            sp.wait_ge(*stored[n][c].after(NI - 1))

                @block.tensor
                def _(pe):
                    with pe.Fori(0, NI) as i:
                        for c in range(2):
                            pe.wait_ge(*arr["g1"][c].after(i, Q))
                            pe.wait_ge(*S.after("rows", c, i - 1))
                            transposes(KK[c][0], G1[c])
                            pe.wait_ge(*arr["g2"][c].after(i, Q))
                            transposes(KK[c][1], G2[c]).then_inc(S.did("inT", c), 1)
                        for c in range(2):
                            pe.wait_ge(*S.after("xa", c, i))
                            nc.tensor.matmul(KK[c][2][:], W["L0_W1"][:], OX[c][:], start=True, stop=True)
                            pe.wait_ge(*S.after("xb", c, i))
                            nc.tensor.matmul(KK[c][3][:], W["L0_W1"][:], OV[c][:], start=True, stop=True).then_inc(S.did("proj", c), 1)
                        for c in range(2):
                            pe.wait_ge(*S.after("hi", c, i))
                            nc.tensor.matmul(KK[c][0][:], W["L0_W2a"][:], B1[c][:], start=True, stop=False)
                            pe.wait_ge(*S.after("d", c, i))
                            nc.tensor.matmul(KK[c][0][:], W["L0_W2b"][:], B2[c][:], start=False, stop=True).then_inc(S.did("mlp1", c), 1)
                        for c in range(2):
                            pe.wait_ge(*S.after("m1", c, i))
                            nc.tensor.matmul(KK[c][1][:], W["L0_W3"][:], LV[c][:], start=True, stop=True).then_inc(S.did("mlp2", c), 1)
                        for c in range(2):
                            pe.wait_ge(*S.after("scan", c, i))
                            transposes(KK[c][2], Z[c]).then_inc(S.did("rowsT", c), 1)

                @block.scalar
                def _(act):
                    with act.Fori(0, NI) as i:
                        for c in range(2):
                            act.wait_ge(*S.after("inT", c, i))
                            act.wait_ge(*stored["x"][c].after(i - 1))
                            nc.scalar.activation(OX[c][:], KK[c][0][:], ACT.Copy).then_inc(S.did("xa", c), 1)
                        for c in range(2):
                            act.wait_ge(*S.after("proj", c, i))
                            nc.scalar.activation(B1[c][:], KK[c][2][:], ACT.Identity, bias=B["L0_b1"][:]).then_inc(S.did("hi", c), 1)
                        for c in range(2):
                            act.wait_ge(*S.after("mlp1", c, i))
                            nc.scalar.activation(LV[c][:], KK[c][0][:], ACT.Relu, bias=B["L0_b2"][:]).then_inc(S.did("m1", c), 1)
                        for c in range(2):
                            act.wait_ge(*S.after("mlp2", c, i))
                            nc.scalar.activation(LX[c][:], KK[c][1][:], ACT.Relu, bias=B["L0_b3"][:]).then_inc(S.did("m2", c), 1)
                        for c in range(2):
                            act.wait_ge(*S.after("rowsT", c, i))
                            act.wait_ge(*stored["r"][c].after(i - 1))
                            nc.scalar.activation(R[c][:], KK[c][2][:], ACT.Copy).then_inc(S.did("rows", c), 1)

                @block.vector
                def _(dve):
                    nc.vector.memset(Z[1][:, BLK - 1:BLK], 0.0).then_inc(scan_ready, 1)
                    dve.wait_ge(scan_ready, scans + 1)
                    with dve.Fori(0, NI) as i:
                        for c in range(2):
                            dve.wait_ge(*S.after("inT", c, i))
                            dve.wait_ge(*stored["v"][c].after(i - 1))
                            nc.vector.tensor_copy(OV[c][:], KK[c][1][:]).then_inc(S.did("xb", c), 1)
                        for c in range(2):
                            dve.wait_ge(*S.after("hi", c, i))
                            nc.vector.scalar_tensor_tensor(B2[c][:], KK[c][3][:], B["L0_b1"][:, 0:1], B1[c][:], ALU.add, ALU.subtract).then_inc(S.did("d", c), 1)
                        for c in range(2):
                            dve.wait_ge(*S.after("m2", c, i))
                            dve.wait_ge(*arr["s2"][c].after(i))
                            if c == 1:
                                dve.wait_ge(*S.after("scan", 0, i))
                            else:
                                dve.wait_ge(*S.after("scan", 1, i - 1))
                                dve.wait_ge(*S.after("rowsT", 0, i - 1))
                            nc.vector.tensor_tensor_scan(Z[c][:], LT[c][:], LX[c][:], Z[1 - c][:, BLK - 1:BLK], ALU.mult, ALU.max).then_inc(S.did("scan", c), 1)
            S.close(NI)
            for c in range(2):
                arr["g1"][c].close(NI, Q)
                arr["g2"][c].close(NI, Q)
                arr["s2"][c].close(NI)
                for n in ("x", "v", "r"):
                    stored[n][c].close(NI)

        def sum_stage(wname, src, same, scale, tab):
            gathered = isinstance(src, str)
            steps = ([("idx", "gather"), ("inT", "pe"), ("in", "act")] if gathered else []) + [("msg", "pe")] \
                + ([("scaled", "dve")] if scale is not None else []) + [("scan", "dve"), ("rowsT", "pe"), ("rows", "act")]
            S = Steps(lane_sems, lane_base, steps, 2)
            KK = [[K[4 * c + m] for m in range(4)] for c in range(2)]
            with nc.Block() as block:
                if gathered:
                    @block.gpsimd
                    def _(pool):
                        with pool.Fori(0, NI) as i:
                            for c in range(2):
                                gather(pool, S, c, i, "inT", [(src, tab_u, G1, "g1")])

                @block.sync
                def _(sp):
                    def load(c, i):
                        j = i * 2 + c
                        if not gathered:
                            sp.wait_ge(*S.after("msg", c, i - 1))
                            sp.dma_start(LV[c][:], src[0][src[1], j]).then_inc(arr["v"][c].sem, 16)
                        sp.wait_ge(*S.after("scan", c, i - 1))
                        sp.dma_start(LT[c][:], bcast(same, j)).then_inc(arr["s2"][c].sem, 16)
                        if scale is not None:
                            sp.dma_start(LS[c][:], bcast(scale, j)).then_inc(arr["s"][c].sem, 16)

                    def store(c, i):
                        sp.wait_ge(*S.after("rows", c, i))
                        sp.dma_start(rows_out_view(tab, i * 2 + c), R[c][:].rearrange("p (q f) -> p q f", q=Q)).then_inc(stored["r"][c].sem, 16)

                    for c in range(2):
                        load(c, 0)
                    with sp.Fori(0, NI - 1) as i:
                        for c in range(2):
                            load(c, i + 1)
                            store(c, i)
                    for c in range(2):
                        store(c, NI - 1)
                        sp.wait_ge(*stored["r"][c].after(NI - 1))

                @block.tensor
                def _(pe):
                    with pe.Fori(0, NI) as i:
                        if gathered:
                            for c in range(2):
                                pe.wait_ge(*arr["g1"][c].after(i, Q))
                                pe.wait_ge(*S.after("in", c, i - 1))
                                transposes(KK[c][0], G1[c]).then_inc(S.did("inT", c), 1)
                        for c in range(2):
                            if gathered:
                                pe.wait_ge(*S.after("in", c, i))
                            else:
                                pe.wait_ge(*arr["v"][c].after(i))
                            pe.wait_ge(*S.after("scan", c, i - 1))
                            nc.tensor.matmul(KK[c][1][:], W[wname][:], LV[c][:], start=True, stop=True).then_inc(S.did("msg", c), 1)
                        for c in range(2):
                            pe.wait_ge(*S.after("scan", c, i))
                            pe.wait_ge(*S.after("rows", c, i - 1))
                            transposes(KK[c][2], Z[c]).then_inc(S.did("rowsT", c), 1)

                @block.scalar
                def _(act):
                    with act.Fori(0, NI) as i:
                        if gathered:
                            for c in range(2):
                                act.wait_ge(*S.after("inT", c, i))
                                act.wait_ge(*S.after("msg", c, i - 1))
                                nc.scalar.activation(LV[c][:], KK[c][0][:], ACT.Copy).then_inc(S.did("in", c), 1)
                        for c in range(2):
                            act.wait_ge(*S.after("rowsT", c, i))
                            act.wait_ge(*stored["r"][c].after(i - 1))
                            nc.scalar.activation(R[c][:], KK[c][2][:], ACT.Copy).then_inc(S.did("rows", c), 1)

                @block.vector
                def _(dve):
                    nc.vector.memset(Z[1][:, BLK - 1:BLK], 0.0).then_inc(scan_ready, 1)
                    dve.wait_ge(scan_ready, scans + 1)
                    with dve.Fori(0, NI) as i:
                        for c in range(2):
                            dve.wait_ge(*S.after("msg", c, i))
                            m = KK[c][1]
                            if scale is not None:
                                dve.wait_ge(*arr["s"][c].after(i))
                                nc.vector.tensor_tensor(B1[c][:], KK[c][1][:], LS[c][:], ALU.mult).then_inc(S.did("scaled", c), 1)
                                dve.wait_ge(*S.after("scaled", c, i))
                                m = B1[c]
                            dve.wait_ge(*arr["s2"][c].after(i))
                            if c == 1:
                                dve.wait_ge(*S.after("scan", 0, i))
                            else:
                                dve.wait_ge(*S.after("scan", 1, i - 1))
                            dve.wait_ge(*S.after("rowsT", c, i - 1))
                            nc.vector.tensor_tensor_scan(Z[c][:], LT[c][:], m[:], Z[1 - c][:, BLK - 1:BLK], ALU.mult, ALU.add).then_inc(S.did("scan", c), 1)
            S.close(NI)
            for c in range(2):
                if gathered:
                    arr["g1"][c].close(NI, Q)
                else:
                    arr["v"][c].close(NI)
                arr["s2"][c].close(NI)
                if scale is not None:
                    arr["s"][c].close(NI)
                stored["r"][c].close(NI)

        def slot_stage(weight=None, bias=None, relu=True, two_way=False, v_from="v", pre=None, post=None,
                       resid=False, lstm=False, rows_to=False, final=False):
            steps = [("idx", "gather")]
            steps += [("pre", "pe")] + ([("scaled", "dve")] if weight and pre else []) + ([("act", "act")] if weight else [])
            norm = resid or lstm
            if norm:
                steps += [("z", "dve")] + LN("")
                if not final:
                    steps += [("lnB", "pe"), ("xf", "act")]
            if lstm:
                steps += LSTM
            keep_v = not final and not (resid and post is None and not lstm)
            if post:
                steps += [("v", "dve")]
            if rows_to and not norm:
                steps += [("uT", "pe"), ("uR", "act")]
            if final:
                steps += [("scattered", "pool")]
            S = Steps(lane_sems, lane_base, steps, LANES)
            L = range(LANES)
            KA, KB = [K[2 * c] for c in L], [K[2 * c + 1] for c in L]
            plain = {c: c < 2 for c in L}
            fetch = {c: ([("end_f", tab_f, G1, "g1")] if c >= 2 and not final else []) +
                        ([("end_ba" if c < 2 else "end_bb", tab_b, G2, "g2")] if two_way else []) for c in L}
            rows_in = {c: ([G1[c]] if plain[c] or not final else []) + ([G2[c]] if two_way else []) for c in L}
            need_s = bool(pre or post)
            last_v = "v" if post else ("act" if weight and not norm else None)
            pidx_of = {0: (C_D1A if 1 in (pre, post) else C_D3A), 1: (C_D1B if 1 in (pre, post) else C_D3B)}
            use_s = "v" if post else ("scaled" if pre else None)
            store_rows = {c: (rows_to and c < 2) for c in L}
            act_dst = [(OV[c] if (weight and not norm and not post) else B2[c]) for c in L]
            with nc.Block() as block:
                @block.gpsimd
                def _(pool):
                    def get(i):
                        for c in L:
                            if fetch[c]:
                                gather(pool, S, c, i, "pre", fetch[c])

                    def work(i):
                        if norm:
                            for c in L:
                                ln_rstd(pool, S, c, i, "", P)
                        if final:
                            for c in L:
                                lst = "out_a" if c < 2 else "out_b"
                                nc.gpsimd.tensor_copy(GI[0][c][:], IX[lst][:, bass.ds((i * 2 + (c & 1)) * Q, Q)]).then_inc(out_idx, 1)
                            pool.wait_ge(out_idx, i * LANES + LANES)
                            pool.sem_inc(pool_passed, 1)
                            for c in L:
                                pool.wait_ge(*S.after("norm", c, i))
                                pool.sem_inc(pool_passed, 1)
                                for q in range(Q):
                                    nc.gpsimd.indirect_dma_start(
                                        out=out, out_offset=bass.IndirectOffsetOnAxis(ap=GI[0][c][:, q:q + 1].bitcast(U32), axis=0),
                                        in_=R[c][:, q * D:(q + 1) * D], in_offset=None, bounds_check=N - 1, oob_is_err=False).then_inc(out_dma[c], 16)
                            for c in L:
                                pool.wait_ge(out_dma[c], i * (16 * Q) + 16 * Q)
                                pool.sem_inc(S.did("scattered", c), 1)
                    if any(fetch.values()):
                        get(0)
                        with pool.Fori(0, NI - 1) as i:
                            get(i + 1)
                            work(i)
                        work(NI - 1)
                    elif norm:
                        with pool.Fori(0, NI) as i:
                            work(i)

                @block.sync
                def _(sp):
                    def load(i):
                        for c in L:
                            j, side = i * 2 + (c & 1), c >> 1
                            sp.wait_ge(*S.after("pre", c, i - 1))
                            if weight:
                                sp.dma_start(LV[c][:], (st_v if v_from == "v" else st_x)[side, j]).then_inc(arr["v"][c].sem, 16)
                            if plain[c]:
                                sp.dma_start(G1[c][:].rearrange("p (q f) -> p q f", q=Q), rows_out_view(tab_f, j)).then_inc(arr["x2"][c].sem, 16)
                        for c in L:
                            j, side = i * 2 + (c & 1), c >> 1
                            if norm:
                                sp.wait_ge(*S.after("z", c, i - 1))
                                sp.dma_start(LX[c][:], st_x[side, j]).then_inc(arr["x"][c].sem, 16)
                            if need_s:
                                sp.wait_ge(*S.after(use_s, c, i - 1))
                                sp.dma_start(LS[c][:], bcast(pidx_of[side], j)).then_inc(arr["s"][c].sem, 16)

                    def store(i):
                        for c in L:
                            j, side = i * 2 + (c & 1), c >> 1
                            if store_rows[c]:
                                sp.wait_ge(*S.after("norm" if norm else "uR", c, i))
                                sp.dma_start(rows_out_view(tab_u, j), R[c][:].rearrange("p (q f) -> p q f", q=Q)).then_inc(stored["r"][c].sem, 16)
                            if norm and not final:
                                sp.wait_ge(*S.after("xf", c, i))
                                sp.dma_start(st_x[side, j], OX[c][:]).then_inc(stored["x"][c].sem, 16)
                            if last_v:
                                sp.wait_ge(*S.after(last_v, c, i))
                                sp.dma_start(st_v[side, j], OV[c][:]).then_inc(stored["v"][c].sem, 16)

                    load(0)
                    with sp.Fori(0, NI - 1) as i:
                        load(i + 1)
                        store(i)
                    store(NI - 1)
                    for c in L:
                        if store_rows[c]:
                            sp.wait_ge(*stored["r"][c].after(NI - 1))
                        if norm and not final:
                            sp.wait_ge(*stored["x"][c].after(NI - 1))
                        if last_v:
                            sp.wait_ge(*stored["v"][c].after(NI - 1))

                end = steps[-1][0] if not final else "norm"

                @block.tensor
                def _(pe):
                    with pe.Fori(0, NI) as i:
                        for c in L:
                            pe.wait_ge(*S.after(end if end != "uR" or store_rows[c] or True else "act", c, i - 1))
                            if plain[c]:
                                pe.wait_ge(*arr["x2"][c].after(i))
                            for _, _, _, stream in fetch[c]:
                                pe.wait_ge(*arr[stream][c].after(i, Q))
                            if weight:
                                pe.wait_ge(*arr["v"][c].after(i))
                                last = nc.tensor.matmul(KA[c][:], W[weight][:], LV[c][:], start=True, stop=not rows_in[c])
                                for m, g in enumerate(rows_in[c]):
                                    for q in range(Q):
                                        last = nc.tensor.matmul(tile_cols(KA[c], q), tile_cols(g, q), ident[:], start=False,
                                                                stop=(m == len(rows_in[c]) - 1 and q == Q - 1))
                            else:
                                last = transposes(KA[c], rows_in[c][0])
                            last.then_inc(S.did("pre", c), 1)
                        if norm:
                            for c in L:
                                pe.wait_ge(*S.after("z", c, i))
                                transposes(KB[c], Z[c]).then_inc(S.did("lnT", c), 1)
                            if not final:
                                for c in L:
                                    pe.wait_ge(*S.after("norm", c, i))
                                    transposes(KA[c], R[c]).then_inc(S.did("lnB", c), 1)
                        if lstm:
                            for c in L:
                                lstm_gates(pe, S, c, i, OX[c], "xf", BLK)
                            for c in L:
                                lstm_gate_o(pe, S, c, i, OX[c], BLK)
                        if rows_to and not norm:
                            for c in L:
                                pe.wait_ge(*S.after("act", c, i))
                                transposes(KB[c], OV[c]).then_inc(S.did("uT", c), 1)

                @block.scalar
                def _(act):
                    with act.Fori(0, NI) as i:
                        if weight:
                            for c in L:
                                act.wait_ge(*S.after("scaled" if pre else "pre", c, i))
                                if last_v == "act":
                                    act.wait_ge(*stored["v"][c].after(i - 1))
                                elif post and not norm:
                                    act.wait_ge(*S.after("v", c, i - 1))
                                elif norm:
                                    act.wait_ge(*S.after("z", c, i - 1))
                                nc.scalar.activation(act_dst[c][:], (B1 if pre else KA)[c][:], ACT.Relu if relu else ACT.Identity,
                                                     bias=B[bias][:]).then_inc(S.did("act", c), 1)
                        if norm and not final:
                            for c in L:
                                act.wait_ge(*S.after("lnB", c, i))
                                act.wait_ge(*stored["x"][c].after(i - 1))
                                nc.scalar.activation(OX[c][:], KA[c][:], ACT.Copy).then_inc(S.did("xf", c), 1)
                        if lstm:
                            for c in L:
                                lstm_act_ig(act, S, c, i, BLK)
                            for c in L:
                                lstm_act_oc(act, S, c, i, BLK)
                        if rows_to and not norm:
                            for c in L:
                                act.wait_ge(*S.after("uT", c, i))
                                if store_rows[c]:
                                    act.wait_ge(*stored["r"][c].after(i - 1))
                                nc.scalar.activation(R[c][:], KB[c][:], ACT.Copy).then_inc(S.did("uR", c), 1)

                @block.vector
                def _(dve):
                    with dve.Fori(0, NI) as i:
                        if weight and pre:
                            for c in L:
                                dve.wait_ge(*S.after("pre", c, i))
                                dve.wait_ge(*arr["s"][c].after(i))
                                nc.vector.tensor_tensor(B1[c][:], KA[c][:], LS[c][:], ALU.mult).then_inc(S.did("scaled", c), 1)
                        if norm:
                            for c in L:
                                dve.wait_ge(*S.after("act" if weight else "pre", c, i))
                                dve.wait_ge(*arr["x"][c].after(i))
                                nc.vector.tensor_tensor(Z[c][:], B2[c][:] if weight else KA[c][:], LX[c][:], ALU.add).then_inc(S.did("z", c), 1)
                            for c in L:
                                ln_stats(dve, S, c, i, "", KB[c], "lnT", P)
                            for c in L:
                                if store_rows[c]:
                                    dve.wait_ge(*stored["r"][c].after(i - 1))
                                if final:
                                    dve.wait_ge(*S.after("scattered", c, i - 1))
                                ln_norm(dve, S, c, i, "", KB[c], R[c], P)
                        if lstm:
                            for c in L:
                                lstm_cell(dve, S, c, i, BLK)
                            for c in L:
                                lstm_h(dve, S, c, i, BLK)
                        if post:
                            for c in L:
                                dve.wait_ge(*S.after("h" if lstm else "xf" if norm else "act", c, i))
                                dve.wait_ge(*stored["v"][c].after(i - 1))
                                dve.wait_ge(*arr["s"][c].after(i))
                                src = B1[c] if lstm else OX[c] if norm else B2[c]
                                nc.vector.tensor_tensor(OV[c][:], src[:], LS[c][:], ALU.mult).then_inc(S.did("v", c), 1)
            S.close(NI)
            for c in L:
                if not fetch[c]:
                    lane_base["gather"][c] -= NI
                if weight:
                    arr["v"][c].close(NI)
                if plain[c]:
                    arr["x2"][c].close(NI)
                for _, _, _, stream in fetch[c]:
                    arr[stream][c].close(NI, Q)
                if norm:
                    arr["x"][c].close(NI)
                if need_s:
                    arr["s"][c].close(NI)
                if store_rows[c]:
                    stored["r"][c].close(NI)
                if norm and not final:
                    stored["x"][c].close(NI)
                if last_v:
                    stored["v"][c].close(NI)

        def dense_stage():
            WD = DP * Q
            NI_ = DB // LANES
            x_in = a["x"].rearrange("(j p q) f -> j p (q f)", p=DP, q=Q)
            y_out = out.rearrange("(j p q) f -> j p (q f)", p=DP, q=Q)
            steps = LN("0")[1:] + [("lnB0", "pe"), ("xf0", "act")] + LSTM + [("r1", "pe"), ("ra1", "act"), ("y", "pe"), ("ya", "act"), ("z1", "dve")] + \
                LN("1") + [("lnB1", "pe"), ("xf1", "act")] + [("u0", "pe"), ("ua0", "act"), ("u1", "pe"), ("ua1", "act"), ("u2", "pe"), ("z2", "dve")] + \
                LN("2") + [("lnB2", "pe"), ("xf2", "act")] + [("v1", "pe"), ("va1", "act"), ("v2", "pe"), ("va2", "act"), ("z3", "dve")] + LN("3")
            S = Steps(lane_sems, lane_base, steps, LANES)
            L = range(LANES)
            KA, KB = [K[2 * c] for c in L], [K[2 * c + 1] for c in L]
            XR, X = LX, OX
            with nc.Block() as block:
                @block.sync
                def _(sp):
                    def load(i):
                        for c in L:
                            sp.wait_ge(*S.after("norm0", c, i - 1))
                            sp.dma_start(XR[c][0:DP, :], x_in[i * LANES + c]).then_inc(arr["x"][c].sem, 16)

                    def store(i):
                        for c in L:
                            sp.wait_ge(*S.after("norm3", c, i))
                            sp.dma_start(y_out[i * LANES + c], OV[c][0:DP, :]).then_inc(stored["v"][c].sem, 16)

                    load(0)
                    with sp.Fori(0, NI_ - 1) as i:
                        load(i + 1)
                        store(i)
                    store(NI_ - 1)
                    for c in L:
                        sp.wait_ge(*stored["v"][c].after(NI_ - 1))

                @block.gpsimd
                def _(pool):
                    with pool.Fori(0, NI_) as i:
                        for t in "0123":
                            for c in L:
                                ln_rstd(pool, S, c, i, t, DP)

                @block.tensor
                def _(pe):
                    def mm(name, w, bank, src, i):
                        for c in L:
                            pe.wait_ge(*S.after(src[0], c, i))
                            nc.tensor.matmul(bank[c][:, 0:WD], W[w][:], src[1][c][:, 0:WD], start=True, stop=True).then_inc(S.did(name, c), 1)

                    def back(t, i):
                        for c in L:
                            pe.wait_ge(*S.after("norm" + t, c, i))
                            transposes(KA[c], R[c], rows=DP).then_inc(S.did("lnB" + t, c), 1)

                    def forth(t, i, z):
                        for c in L:
                            pe.wait_ge(*S.after(z, c, i))
                            for q in range(Q):
                                last = nc.tensor.transpose(KB[c][0:DP, q * D:(q + 1) * D], Z[c][:, q * DP:(q + 1) * DP], ident[:])
                            last.then_inc(S.did("lnT" + t, c), 1)

                    with pe.Fori(0, NI_) as i:
                        back("0", i)
                        for c in L:
                            lstm_gates(pe, S, c, i, X[c], "xf0", WD)
                        for c in L:
                            lstm_gate_o(pe, S, c, i, X[c], WD)
                        mm("r1", "L1_W1", KA, ("h", B1), i)
                        mm("y", "L1_W23", KB, ("ra1", B2), i)
                        forth("1", i, "z1")
                        back("1", i)
                        mm("u0", "W0x", KB, ("xf1", X), i)
                        mm("u1", "W1x", KA, ("ua0", B1), i)
                        mm("u2", "W2x", KB, ("ua1", B2), i)
                        forth("2", i, "z2")
                        back("2", i)
                        mm("v1", "L3_W1", KB, ("xf2", X), i)
                        mm("v2", "L3_W2", KA, ("va1", B1), i)
                        forth("3", i, "z3")

                @block.scalar
                def _(act):
                    def fn(name, src, bank, dst, f, b, i):
                        for c in L:
                            act.wait_ge(*S.after(src, c, i))
                            if b is None:
                                ins = nc.scalar.activation(dst[c][:, 0:WD], bank[c][:, 0:WD], f)
                            else:
                                ins = nc.scalar.activation(dst[c][:, 0:WD], bank[c][:, 0:WD], f, bias=B[b][:])
                            ins.then_inc(S.did(name, c), 1)

                    with act.Fori(0, NI_) as i:
                        fn("xf0", "lnB0", KA, X, ACT.Copy, None, i)
                        for c in L:
                            lstm_act_ig(act, S, c, i, WD)
                        for c in L:
                            lstm_act_oc(act, S, c, i, WD)
                        fn("ra1", "r1", KA, B2, ACT.Relu, "L1_b1", i)
                        fn("ya", "y", KB, B1, ACT.Relu, "L1_b23", i)
                        fn("xf1", "lnB1", KA, X, ACT.Copy, None, i)
                        fn("ua0", "u0", KB, B1, ACT.Relu, "L2_b0", i)
                        fn("ua1", "u1", KA, B2, ACT.Relu, "L2_b1", i)
                        fn("xf2", "lnB2", KA, X, ACT.Copy, None, i)
                        fn("va1", "v1", KB, B1, ACT.Relu, "L3_b1", i)
                        fn("va2", "v2", KA, B2, ACT.Relu, "L3_b2", i)

                @block.vector
                def _(dve):
                    with dve.Fori(0, NI_) as i:
                        for c in L:
                            dve.wait_ge(*arr["x"][c].after(i))
                            ln_stats(dve, S, c, i, "0", XR[c], None, DP)
                        for c in L:
                            ln_norm(dve, S, c, i, "0", XR[c], R[c], DP)
                        for c in L:
                            lstm_cell(dve, S, c, i, WD)
                        for c in L:
                            lstm_h(dve, S, c, i, WD)
                        for t, src, y in (("1", "ya", B1), ("2", "u2", None), ("3", "va2", B2)):
                            for c in L:
                                dve.wait_ge(*S.after(src, c, i))
                                if y is None:
                                    ins = nc.vector.scalar_tensor_tensor(Z[c][:, 0:WD], KB[c][:, 0:WD], B["L2_b2"][:, 0:1], X[c][:, 0:WD], ALU.add, ALU.add)
                                else:
                                    ins = nc.vector.tensor_tensor(Z[c][:, 0:WD], y[c][:, 0:WD], X[c][:, 0:WD], ALU.add)
                                ins.then_inc(S.did("z" + t, c), 1)
                            for c in L:
                                ln_stats(dve, S, c, i, t, KB[c], "lnT" + t, DP)
                            for c in L:
                                if t == "3":
                                    dve.wait_ge(*stored["v"][c].after(i - 1))
                                ln_norm(dve, S, c, i, t, KB[c], OV[c] if t == "3" else R[c], DP)
            S.close(NI_)
            for c in L:
                arr["x"][c].close(NI_)
                stored["v"][c].close(NI_)

        scan_ready, out_idx = sem("scan_ready"), sem("out_idx")
        out_dma = [sem(f"out_rows_written{c}") for c in range(LANES)]
        arr["x2"] = [Arrivals(sem(f"rows_arrived{c}")) for c in range(LANES)]
        scans = 0
        PLAN = [
            lambda: edge_stage(),
            lambda: slot_stage(lstm=True, post=1),
            lambda: sum_stage("L1_W1", (st_v, 1), C_SAMED, None, tab_f),
            lambda: slot_stage("L1_W1", "L1_b1", pre=1, post=1),
            lambda: sum_stage("L1_W23", (st_v, 1), C_SAMED, None, tab_f),
            lambda: slot_stage("L1_W23", "L1_b23", pre=1, resid=True, rows_to=True),
            lambda: sum_stage("W0f", (st_x, 1), C_SAMED, C_INVOUT, tab_f),
            lambda: sum_stage("W0b", "dst_in_s", C_SAMES, C_INVIN, tab_b),
            lambda: slot_stage("W0x", "L2_b0", two_way=True, v_from="x", rows_to=True),
            lambda: sum_stage("W1f", (st_v, 1), C_SAMED, C_INVOUT, tab_f),
            lambda: sum_stage("W1b", "dst_in_s", C_SAMES, C_INVIN, tab_b),
            lambda: slot_stage("W1x", "L2_b1", two_way=True, rows_to=True),
            lambda: sum_stage("W2f", (st_v, 1), C_SAMED, C_INVOUT, tab_f),
            lambda: sum_stage("W2b", "dst_in_s", C_SAMES, C_INVIN, tab_b),
            lambda: slot_stage("W2x", "L2_b2", relu=False, two_way=True, resid=True, post=3),
            lambda: sum_stage("L3_W1", (st_v, 1), C_SAMED, C_W, tab_f),
            lambda: slot_stage("L3_W1", "L3_b1", pre=3, post=3),
            lambda: sum_stage("L3_W2", (st_v, 1), C_SAMED, C_W, tab_f),
            lambda: dense_stage(),
            lambda: slot_stage("L3_W2", "L3_b2", pre=3, resid=True, final=True),
        ]
        for n, stage in enumerate(PLAN):
            if n < upto:
                before_n = scans
                stage()
                scans = before_n + (1 if n in SCANS else 0)



def kernel(**inputs):
    import concourse.bacc as bacc
    from concourse.bass_utils import run_bass_kernel_spmd

    nc = bacc.Bacc("TRN2", target_bir_lowering=False, num_devices=1)
    arrays, aps = {}, {}
    for name, x in inputs.items():
        x = np.ascontiguousarray(x)
        arrays["in_" + name] = x
        aps[name] = nc.dram_tensor("in_" + name, x.shape, mybir.dt.from_np(x.dtype), kind="ExternalInput").ap()
    out = nc.dram_tensor("out", (N, D), F32, kind="ExternalOutput").ap()
    build(nc, aps, out)
    r = run_bass_kernel_spmd(nc, [arrays], core_ids=[0])
    return r.results[0]["out"]
```

```python
from contextlib import ExitStack

import numpy as np

import concourse.bass as bass
import concourse.mybir as mybir

F32 = mybir.dt.float32
BF16 = mybir.dt.bfloat16
I32 = mybir.dt.int32
U32 = mybir.dt.uint32
ALU = mybir.AluOpType
ACT = mybir.ActivationFunctionType
AX = mybir.AxisListType.X

P = 128
N = 50000
E = 12500
D = 128
BLK = 512
Q = BLK // P
NB = 25
EP = NB * BLK
T = EP // P
HI, LO = 98, 512
PAD = HI * LO - 1
DP = 125
DB = N // (DP * Q)
LA, LB, NA, NBL, TA, TB, LM, D0, DE, D1, D2, D3, LNS, LNDA, LNDB, XA, XB = range(17)
EPS = 1e-5
PRIME = 64
SKIP = 60000
RANK_TILES = 4
DENSE_RANK, DENSE_RECORDS = T // RANK_TILES, 25
F_FULL, F_REST = E // P, E % P

N_ENDD, N_ENDS, N_DINV1, N_DINV3, N_INVOUT, N_INVIN, N_CNTD, NF = 0, 1, 2, 3, 4, 5, 6, 8
(R_DST, R_SRC, R_W, R_DINV1A, R_DINV3A, R_INVIN, R_ENDD_DST, R_ENDS_DST,
 R_DINV1B, R_DINV3B, R_INVOUT, R_ENDD_SRC, R_ENDS_SRC, R_CNTD_SRC, R_POSS) = range(15)
RF = 16
(C_SAMED, C_W, C_D1A, C_D1B, C_D3A, C_D3B, C_INVOUT, C_SAMES, C_INVIN) = range(9)
CF = 9


class Steps:

    def __init__(self, sems, base, lanes):
        self.sems, self.base = sems, base
        self.order, self.where = {}, {}
        for c, steps in lanes.items():
            for name, eng in steps:
                names = self.order.setdefault((eng, c), [])
                self.where[name, c] = (eng, len(names))
                names.append(name)
        self.next = {k: 0 for k in self.order}

    def after(self, name, c, i):
        eng, k = self.where[name, c]
        return self.sems[eng][c], i * len(self.order[eng, c]) + (self.base[eng][c] + k + 1)

    def did(self, name, c):
        eng, k = self.where[name, c]
        assert self.next[eng, c] % len(self.order[eng, c]) == k, (name, c)
        self.next[eng, c] += 1
        return self.sems[eng][c]

    def close(self, rounds):
        for (eng, c), names in self.order.items():
            self.base[eng][c] += rounds[c] * len(names)


class Arrivals:

    def __init__(self, sem, base=0):
        self.sem, self.base = sem, base

    def after(self, i, dmas=1):
        return self.sem, i * (16 * dmas) + (self.base + 16 * dmas)

    def close(self, n, dmas=1):
        self.base += 16 * dmas * n


def build(nc, a, out, upto=99, dbg=None):
    ctx = ExitStack()
    with ctx:
        def sb(name, shape, dt=F32):
            return ctx.enter_context(nc.sbuf_tensor(name, shape, dt))

        def sem(name):
            return ctx.enter_context(nc.semaphore(name))

        def dram(name, shape, dt=F32):
            return nc.dram_tensor(name, shape, dt).ap()

        node_tab = dram("node_tab", [HI * LO, NF])
        rec_d = dram("rec_d", [EP, RF])
        rec_s = dram("rec_s", [EP, RF])
        key_d = dram("key_d", [EP + P])
        key_s = dram("key_s", [EP + P])
        scal = dram("scal", [CF, NB, BLK])
        st_x = dram("st_x", [2, NB, P, BLK])
        st_v = dram("st_v", [2, NB, P, BLK])
        tab_f0, tab_f1 = dram("tab_f0", [EP + P, D]), dram("tab_f1", [EP + P, D])
        tab_b = dram("tab_b", [EP + P, D])
        no_block = dram("no_block", [DP, Q * D])
        tab_u = dram("tab_u", [EP, D])

        def rows_of(tab):
            return tab[0:EP, :].rearrange("(j q p) f -> j p q f", q=Q, p=P)

        pidx = sb("pidx", [P, 1])
        iota_i = sb("iota_i", [P, LO], I32)
        iot = sb("iot", [P, LO])
        ident = sb("ident", [P, P])
        identb = sb("identb", [P, P], BF16)
        before = sb("before", [P, P])
        above = sb("above", [P, P])
        ones = sb("ones", [P, LO])
        mhalf = sb("mhalf", [P, LO])
        zero = sb("zero", [P, LO])
        zerob = sb("zerob", [P, LO], BF16)
        minus1 = sb("minus1", [1, P])
        wnames = ["L0_W1", "L0_W2a", "L0_W2b", "L0_W3", "Wi", "Wg", "Wo", "L1_W1", "L1_W23",
                  "W0x", "W0f", "W0b", "W1x", "W1f", "W1b", "W2x", "W2f", "W2b", "L3_W1", "L3_W2"]
        W = {n: sb("w_" + n, [P, P]) for n in wnames}
        bnames = ["L0_b1", "L0_b2", "L0_b3", "bi", "bg", "bo", "L1_b1", "L1_b23",
                  "L2_b0", "L2_b1", "L2_b2", "L3_b1", "L3_b2"]
        B = {n: sb("b_" + n, [P, 1]) for n in bnames}
        IX = {n: sb("ix_" + n, [P, T], I32) for n in ["xa", "xb", "end_f", "end_bb", "end_ba", "dst_in_s", "out_a", "out_b"]}

        K = [ctx.enter_context(nc.psum_tensor(f"bank{k}", [P, BLK], F32)) for k in range(8)]

        names_of = {LA: "side_a", LB: "side_b", NA: "norm_a", NBL: "norm_b", TA: "lstm_a", TB: "lstm_b", LM: "messages",
                    D0: "dense_lstm", DE: "dense_gcn", D1: "dense_block2", D2: "dense_block3", D3: "dense_last",
                    LNS: "slot_rstd", LNDA: "dense_rstd_a", LNDB: "dense_rstd_b",
                    XA: "features_a", XB: "features_b"}
        uses = {"pe": (LA, LB, NA, NBL, XA, XB, TA, TB, LM, D0, DE, D1, D2, D3), "act": (LA, LB, NA, NBL, XA, XB, TA, TB, LM, D0, DE, D1, D2, D3),
                "dve": tuple(range(17)), "pool": (NA, NBL), "gather": (LA, LB)}
        lane_sems = {e: {c: sem(f"{e}_{names_of[c]}") for c in cs} for e, cs in uses.items()}
        lane_base = {e: {c: PRIME for c in cs} for e, cs in uses.items()}
        arr = {n: {c: Arrivals(sem(f"{n}_arrived_{names_of[c]}")) for c in cs}
               for n, cs in {"v": (LA, LB), "x": (LA, LB, D0), "s": (LA, LB, LM), "g1": (LA, LB), "g2": (LA, LB),
                             "same": (LA, LB, LM), "rows": (LA, LB)}.items()}
        stored = {n: {c: Arrivals(sem(f"{n}_stored_{names_of[c]}")) for c in cs}
                  for n, cs in {"v": (LA, LB), "x": (LA, LB), "r": (LA, LB, LM, D3)}.items()}
        setup_dma = Arrivals(sem("setup_dma"))
        table_dma = Arrivals(sem("table_dma"))
        pool_dma = Arrivals(sem("pool_dma"))
        s_pool, s_dve, s_pe, s_act = sem("pool_setup"), sem("dve_setup"), sem("pe_setup"), sem("act_setup")
        cnt = {"pool": 0, "dve": 0, "pe": 0, "act": 0}
        handle = {"pool": s_pool, "dve": s_dve, "pe": s_pe, "act": s_act}

        class Mark:

            def __init__(self, eng):
                cnt[eng] += 1
                self.sem, self.value = handle[eng], cnt[eng]

        pool_passed = sem("pool_passed")
        dve_passed = sem("dve_passed")
        sums_cleared, out_ids, carried = sem("sums_cleared"), sem("out_ids_ready"), sem("carried")
        out_dma = [sem(f"out_rows_written{k}") for k in range(2)]
        scans, carries = [0], [0]
        def per(cs, name, shape=(P, BLK), dt=F32):
            return {c: sb(f"{name}_{names_of[c]}", list(shape), dt) for c in cs}

        AB = (LA, LB)
        GI = [per(AB, f"row_ids{m}", (P, Q), I32) for m in range(2)]
        OI = per(AB, "out_ids", (P, Q), I32)
        B1 = per((D0, DE, D1, D2), "b1")
        B2 = per((D0, D1, D2), "b2")
        SO = per((D0,), "sig_o")
        Z = per((DE, D1, D2), "z")
        R = per((D0, D1, D2, D3), "out_rows")
        DX = per((D0, D1, D2), "dense_x")
        XR = sb("dense_rows", [P, BLK])
        H = sb("dense_h", [P, BLK])
        NORMED = (NA, NBL, D0, D1, D2, D3)
        ST = per(NORMED, "stats", (P, Q, 6))
        MV = per(NORMED, "mean_var", (P, Q, 2))
        NM = per(NORMED, "neg_mean", (P, Q))
        GROUP = {LNS: (NA, NBL), LNDA: (D0, D2), LNDB: (D1, D3)}
        VE = {g: sb(f"var_eps_{names_of[g]}", [P, Q * len(cs)]) for g, cs in GROUP.items()}
        RI = {g: sb(f"root_bits_{names_of[g]}", [P, Q * len(cs)], I32) for g, cs in GROUP.items()}
        RT = {g: sb(f"root_tmp_{names_of[g]}", [P, Q * len(cs)]) for g, cs in GROUP.items()}
        RR = {g: sb(f"root_{names_of[g]}", [P, Q * len(cs)]) for g, cs in GROUP.items()}
        WD = DP * Q

        def in_group(c):
            g = next(g for g, cs in GROUP.items() if c in cs)
            return g, GROUP[g].index(c) * Q

        def tile_cols(buf, q, w=P):
            return buf[:, q * w:(q + 1) * w]

        def transposes(dst, src, rows=P):
            for q in range(Q):
                last = nc.tensor.transpose(dst[:, q * rows:(q + 1) * rows], src[0:rows, q * D:(q + 1) * D], ident[0:rows, 0:rows])
            return last

        def to_rows(dst, src, rows=P):
            for q in range(Q):
                last = nc.tensor.transpose(dst[0:rows, q * D:(q + 1) * D], src[:, q * rows:(q + 1) * rows], ident[:])
            return last

        def bcast(c, j):
            return scal[c, j].partition_broadcast(P)

        def as_rows(buf):
            return buf[:].rearrange("p (q f) -> p q f", q=Q)

        LN = lambda t: [("lnT" + t, "pe")] + LN_IN(t)
        LN_IN = lambda t: [("stats" + t, "dve"), ("aggr" + t, "dve"), ("eps" + t, "dve"), ("neg" + t, "dve"), ("norm" + t, "act")]
        ROOT = [(f"root{k}", "dve") for k in range(11)]

        def ln_stats(dve, S, c, i, t, src, pp):
            g, o = in_group(c)
            if ("lnT" + t, c) in S.where:
                dve.wait_ge(*S.after("lnT" + t, c, i))
            for q in range(Q):
                last = nc.vector.bn_stats(ST[c][0:pp, q, :], src[0:pp, q * D:(q + 1) * D])
            last.then_inc(S.did("stats" + t, c), 1)

        def ln_aggr(dve, S, c, i, t, pp):
            g, o = in_group(c)
            dve.wait_ge(*S.after("stats" + t, c, i))
            dve.sem_inc(dve_passed, 1)
            for q in range(Q):
                last = nc.vector.bn_aggr(MV[c][0:pp, q, :], ST[c][0:pp, q, :])
            last.then_inc(S.did("aggr" + t, c), 1)

        def ln_eps(dve, S, c, i, t, pp):
            g, o = in_group(c)
            dve.wait_ge(*S.after("aggr" + t, c, i))
            nc.vector.tensor_scalar(VE[g][0:pp, o:o + Q], MV[c][0:pp, :, 1], EPS, None, ALU.add).then_inc(S.did("eps" + t, c), 1)

        def ln_root(dve, S, g, i, pp, ready):
            v, r, t, b = VE[g][0:pp, :], RR[g][0:pp, :], RT[g][0:pp, :], RI[g][0:pp, :]
            for c, tag in ready:
                dve.wait_ge(*S.after("eps" + tag, c, i))
            nc.vector.tensor_scalar(b, VE[g][0:pp, :].bitcast(I32), 1, None, ALU.arith_shift_right).then_inc(S.did("root0", g), 1)
            dve.wait_ge(*S.after("root0", g, i))
            nc.vector.tensor_scalar(RR[g][0:pp, :].bitcast(I32), b, -1.0, float(0x5F3759DF), ALU.mult, ALU.add).then_inc(S.did("root1", g), 1)
            for n in range(3):
                dve.wait_ge(*S.after(f"root{3 * n + 1}", g, i))
                nc.vector.scalar_tensor_tensor(t, r, -0.5, r, ALU.mult, ALU.mult).then_inc(S.did(f"root{3 * n + 2}", g), 1)
                dve.wait_ge(*S.after(f"root{3 * n + 2}", g, i))
                nc.vector.tensor_tensor(t, t, v, ALU.mult).then_inc(S.did(f"root{3 * n + 3}", g), 1)
                dve.wait_ge(*S.after(f"root{3 * n + 3}", g, i))
                nc.vector.scalar_tensor_tensor(r, t, 1.5, r, ALU.add, ALU.mult).then_inc(S.did(f"root{3 * n + 4}", g), 1)
            dve.wait_ge(*S.after("root10", g, i))

        def ln_neg(dve, S, c, i, pp):
            g, o = in_group(c)
            nc.vector.scalar_tensor_tensor(NM[c][0:pp, :], MV[c][0:pp, :, 0], -1.0, RR[g][0:pp, o:o + Q], ALU.mult, ALU.mult).then_inc(S.did("neg", c), 1)

        def ln_norm(act, S, c, i, src, dst, pp):
            g, o = in_group(c)
            act.wait_ge(*S.after("neg", c, i))
            for q in range(Q):
                last = nc.scalar.activation(dst[0:pp, q * D:(q + 1) * D], src[0:pp, q * D:(q + 1) * D], ACT.Identity,
                                            bias=NM[c][0:pp, q:q + 1], scale=RR[g][0:pp, o + q:o + q + 1])
            last.then_inc(S.did("norm", c), 1)

        def ln_group(dve, S, g, lanes_i, rows, pp):
            for c, i in lanes_i:
                ln_stats(dve, S, c, i, "", rows[c], pp)
            for c, i in lanes_i:
                ln_aggr(dve, S, c, i, "", pp)
            for c, i in lanes_i:
                ln_eps(dve, S, c, i, "", pp)
            n = lanes_i[0][1]
            ln_root(dve, S, g, n, pp, [(c, "") for c, _ in lanes_i])
            for c, i in lanes_i:
                ln_neg(dve, S, c, i, pp)

        LSTM = [("gate_i", "pe"), ("sig_i", "act"), ("gate_g", "pe"), ("tanh_g", "act"), ("cell", "dve"),
                ("gate_o", "pe"), ("sig_o", "act"), ("tanh_c", "act"), ("h", "dve")]

        def product(pe, S, c, i, name, weight, bank, src, before_, w):
            for b in before_:
                pe.wait_ge(*S.after(b, c, i))
            nc.tensor.matmul(bank[:, 0:w], W[weight][:], src[:, 0:w], start=True, stop=True).then_inc(S.did(name, c), 1)

        def function(act, S, c, i, name, f, bias, src, dst, before_, w):
            for b in before_:
                act.wait_ge(*S.after(b, c, i))
            if bias is None:
                ins = nc.scalar.activation(dst[:, 0:w], src[:, 0:w], f)
            else:
                ins = nc.scalar.activation(dst[:, 0:w], src[:, 0:w], f, bias=B[bias][:])
            ins.then_inc(S.did(name, c), 1)

        def cell(dve, S, c, i, b, t, w):
            dve.wait_ge(*S.after("tanh_g", c, i))
            nc.vector.tensor_tensor(b[:, 0:w], b[:, 0:w], t[:, 0:w], ALU.mult).then_inc(S.did("cell", c), 1)

        def hidden(dve, S, c, i, t, dst, w):
            dve.wait_ge(*S.after("tanh_c", c, i))
            nc.vector.tensor_tensor(dst[:, 0:w], t[:, 0:w], SO[c][:, 0:w], ALU.mult).then_inc(S.did("h", c), 1)

        def gather(pool, S, c, i, j, free, streams):
            pool.wait_ge(*S.after(free, c, i - 1))
            pool.sem_inc(pool_passed, 1)
            for m, (lst, tab, dst, stream) in enumerate(streams):
                last = nc.gpsimd.tensor_copy(GI[m][c][:], IX[lst][:, bass.ds(j * Q, Q)])
            last.then_inc(S.did("ids", c), 1)
            pool.wait_ge(*S.after("ids", c, i))
            pool.sem_inc(pool_passed, 1)
            for m, (lst, tab, dst, stream) in enumerate(streams):
                for q in range(Q):
                    nc.gpsimd.indirect_dma_start(out=dst[c][:, q * D:(q + 1) * D], out_offset=None, in_=tab,
                                                 in_offset=bass.IndirectOffsetOnAxis(ap=GI[m][c][:, q:q + 1].bitcast(U32), axis=0),
                                                 bounds_check=tab.shape[0] - 1, oob_is_err=False).then_inc(arr[stream][c].sem, 16)

        PAIRS = NB // 2
        TURNS = {LA: NB - PAIRS, LB: PAIRS}

        def in_turns(eng, body):
            with eng.Fori(0, PAIRS) as i:
                body(i, (LA, LB))
            body(PAIRS, (LA,))

        def loads_and_stores(sp, load, store, finish):
            load(0, (LA, LB))
            with sp.Fori(0, PAIRS - 1) as i:
                load(i + 1, (LA, LB))
                store(i, (LA, LB))
            load(PAIRS, (LA,))
            store(PAIRS - 1, (LA, LB))
            store(PAIRS, (LA,))
            finish()

        def start_sums(dve):
            for m in range(2):
                last = nc.vector.memset(ZM[m][:, BLK - 1:BLK], 0.0)
            last.then_inc(sums_cleared, 1)
            scans[0] += 1
            dve.wait_ge(sums_cleared, scans[0])

        DENSE = {D0: LN_IN("") + [("lnB", "pe"), ("xf", "act")] + LSTM,
                 DE: [("r1", "pe"), ("ra1", "act"), ("y", "pe"), ("ya", "act"), ("z", "dve")],
                 D1: [("u0", "pe"), ("ua0", "act"), ("u1", "pe"), ("ua1", "act"), ("u2", "pe"), ("z", "dve")] + LN("") + [("lnB", "pe"), ("xf", "act")],
                 D2: LN("") + [("lnB", "pe"), ("xf", "act"), ("v1", "pe"), ("va1", "act"), ("v2", "pe"), ("va2", "act"), ("z", "dve")],
                 D3: LN(""), LNDA: ROOT, LNDB: ROOT}
        LAG = 4
        x_in = a["x"].rearrange("(j p q) f -> j p (q f)", p=DP, q=Q)
        y_out = out.rearrange("(j p q) f -> j p (q f)", p=DP, q=Q)
        KD = {D0: K[4], DE: K[5], D3: K[5], D1: K[6], D2: K[7]}
        zin = {D1: Z[DE], D2: Z[D1], D3: Z[D2]}

        def dense_pe(pe, S, i, part):
            if part == 0:
                pe.wait_ge(*S.after("z", D1, i - 1))
                pe.wait_ge(*S.after("va2", D2, i - 1))
                to_rows(KD[D2], zin[D2], DP).then_inc(S.did("lnT", D2), 1)
                pe.wait_ge(*S.after("h", D0, i - 1))
                pe.wait_ge(*S.after("norm", D3, i - 1))
                nc.tensor.matmul(KD[DE][:, 0:WD], W["L1_W1"][:], H[:, 0:WD], start=True, stop=True).then_inc(S.did("r1", DE), 1)
                pe.wait_ge(*S.after("xf", D1, i - 1))
                nc.tensor.matmul(KD[D1][:, 0:WD], W["W0x"][:], DX[D1][:, 0:WD], start=True, stop=True).then_inc(S.did("u0", D1), 1)
            if part == 1:
                product(pe, S, DE, i, "y", "L1_W23", KD[DE], B1[DE], ["ra1"], WD)
                product(pe, S, D1, i, "u1", "W1x", KD[D1], B1[D1], ["ua0"], WD)
            if part == 2:
                product(pe, S, D1, i, "u2", "W2x", KD[D1], B2[D1], ["ua1"], WD)
                pe.wait_ge(*S.after("norm", D0, i))
                pe.wait_ge(*S.after("sig_o", D0, i - 1))
                transposes(KD[D0], R[D0], DP).then_inc(S.did("lnB", D0), 1)
            if part == 3:
                pe.wait_ge(*S.after("norm", D2, i))
                transposes(KD[D2], R[D2], DP).then_inc(S.did("lnB", D2), 1)
                pe.wait_ge(*S.after("z", DE, i))
                pe.wait_ge(*S.after("z", D1, i))
                to_rows(KD[D1], zin[D1], DP).then_inc(S.did("lnT", D1), 1)
                pe.wait_ge(*S.after("z", D2, i - 1))
                to_rows(KD[D3], zin[D3], DP).then_inc(S.did("lnT", D3), 1)
            if part == 4:
                product(pe, S, D0, i, "gate_i", "Wi", KD[D0], DX[D0], ["xf"], WD)
                product(pe, S, D2, i, "v1", "L3_W1", KD[D2], DX[D2], ["xf"], WD)
            if part == 5:
                product(pe, S, D0, i, "gate_g", "Wg", KD[D0], DX[D0], ["sig_i"], WD)
                product(pe, S, D2, i, "v2", "L3_W2", KD[D2], B1[D2], ["va1"], WD)
            if part == 6:
                product(pe, S, D0, i, "gate_o", "Wo", KD[D0], DX[D0], ["tanh_g"], WD)
            if part == 7:
                pe.wait_ge(*S.after("norm", D1, i))
                transposes(KD[D1], R[D1], DP).then_inc(S.did("lnB", D1), 1)

        def dense_act(act, S, i, part):
            if part == 0:
                function(act, S, DE, i, "ra1", ACT.Relu, "L1_b1", KD[DE], B1[DE], ["r1"], WD)
                function(act, S, D1, i, "ua0", ACT.Relu, "L2_b0", KD[D1], B1[D1], ["u0"], WD)
            if part == 1:
                function(act, S, DE, i, "ya", ACT.Relu, "L1_b23", KD[DE], B1[DE], ["y"], WD)
                function(act, S, D1, i, "ua1", ACT.Relu, "L2_b1", KD[D1], B2[D1], ["u1"], WD)
            if part == 2:
                ln_norm(act, S, D0, i, XR, R[D0], DP)
                ln_norm(act, S, D2, i, KD[D2], R[D2], DP)
            if part == 3:
                act.wait_ge(*S.after("z", DE, i))
                function(act, S, D0, i, "xf", ACT.Copy, None, KD[D0], DX[D0], ["lnB"], WD)
                function(act, S, D2, i, "xf", ACT.Copy, None, KD[D2], DX[D2], ["lnB"], WD)
            if part == 4:
                function(act, S, D0, i, "sig_i", ACT.Sigmoid, "bi", KD[D0], B1[D0], ["gate_i"], WD)
                function(act, S, D2, i, "va1", ACT.Relu, "L3_b1", KD[D2], B1[D2], ["v1"], WD)
            if part == 5:
                function(act, S, D0, i, "tanh_g", ACT.Tanh, "bg", KD[D0], B2[D0], ["gate_g"], WD)
                function(act, S, D2, i, "va2", ACT.Relu, "L3_b2", KD[D2], B2[D2], ["v2"], WD)
            if part == 6:
                function(act, S, D0, i, "sig_o", ACT.Sigmoid, "bo", KD[D0], SO[D0], ["gate_o"], WD)
                function(act, S, D0, i, "tanh_c", ACT.Tanh, None, B1[D0], B2[D0], ["cell"], WD)
            if part == 7:
                ln_norm(act, S, D1, i, KD[D1], R[D1], DP)
                act.wait_ge(*stored["r"][D3].after(i - 1))
                ln_norm(act, S, D3, i, KD[D3], R[D3], DP)
                function(act, S, D1, i, "xf", ACT.Copy, None, KD[D1], DX[D1], ["lnB"], WD)

        def dense_dve(dve, S, i, part):
            if part == 0:
                dve.wait_ge(*arr["x"][D0].after(i))
                dve.wait_ge(*S.after("norm", D0, i - 1))
                dve.wait_ge(*S.after("norm", D2, i - 1))
                ln_group(dve, S, LNDA, [(D0, i), (D2, i)], {D0: XR, D2: KD[D2]}, DP)
            if part == 2:
                dve.wait_ge(*S.after("ya", DE, i))
                nc.vector.tensor_tensor(Z[DE][:, 0:WD], B1[DE][:, 0:WD], DX[D0][:, 0:WD], ALU.add).then_inc(S.did("z", DE), 1)
                dve.wait_ge(*S.after("u2", D1, i))
                dve.wait_ge(*S.after("lnT", D2, i))
                nc.vector.scalar_tensor_tensor(Z[D1][:, 0:WD], KD[D1][:, 0:WD], B["L2_b2"][:, 0:1], DX[D1][:, 0:WD],
                                               ALU.add, ALU.add).then_inc(S.did("z", D1), 1)
            if part == 3:
                dve.wait_ge(*S.after("norm", D1, i - 1))
                dve.wait_ge(*S.after("norm", D3, i - 1))
                ln_group(dve, S, LNDB, [(D1, i), (D3, i)], {D1: KD[D1], D3: KD[D3]}, DP)
            if part == 5:
                cell(dve, S, D0, i, B1[D0], B2[D0], WD)
            if part == 6:
                dve.wait_ge(*S.after("va2", D2, i))
                dve.wait_ge(*S.after("lnT", D3, i))
                nc.vector.tensor_tensor(Z[D2][:, 0:WD], B2[D2][:, 0:WD], DX[D2][:, 0:WD], ALU.add).then_inc(S.did("z", D2), 1)
                dve.wait_ge(*S.after("r1", DE, i))
                hidden(dve, S, D0, i, B2[D0], H, WD)

        PARTS = range(8)

        def dense_load(sp, S, i, block_no):
            sp.wait_ge(*S.after("norm", D0, i - 1))
            sp.dma_start(XR[0:DP, :], x_in[block_no]).then_inc(arr["x"][D0].sem, 16)

        def dense_store(sp, S, i, block_no):
            sp.wait_ge(*S.after("norm", D3, i))
            sp.dma_start(no_block if block_no is None else y_out[block_no], R[D3][0:DP, :]).then_inc(stored["r"][D3].sem, 16)

        def dense_drain(first):
            S = Steps(lane_sems, lane_base, DENSE)
            with nc.Block() as block:
                @block.tensor
                def _(pe):
                    with pe.Fori(0, LAG) as i:
                        for part in PARTS:
                            dense_pe(pe, S, i, part)

                @block.scalar
                def _(act):
                    with act.Fori(0, LAG) as i:
                        for part in PARTS:
                            dense_act(act, S, i, part)

                @block.vector
                def _(dve):
                    with dve.Fori(0, LAG) as i:
                        for part in PARTS:
                            dense_dve(dve, S, i, part)

                @block.sync
                def _(sp):
                    for i in range(LAG):
                        if i + 1 < LAG:
                            dense_load(sp, S, i + 1, DB - 1)
                        dense_store(sp, S, i, first + i - LAG)
                    sp.wait_ge(*stored["r"][D3].after(LAG - 1))
            S.close({c: LAG for c in DENSE})
            arr["x"][D0].close(LAG)
            stored["r"][D3].close(LAG)


        def dense_sync(sp, S, first, rounds):
            head = LAG if first == 0 else 0
            if first == 0:
                dense_load(sp, S, 0, 0)
            for i in range(head):
                dense_load(sp, S, i + 1, i + 1)
                dense_store(sp, S, i, None)
            with sp.Fori(head, rounds - 1) as i:
                dense_load(sp, S, i + 1, i + (1 + first))
                dense_store(sp, S, i, i + (first - LAG))
            dense_load(sp, S, rounds, min(first + rounds, DB - 1))
            dense_store(sp, S, rounds - 1, first + rounds - 1 - LAG)
            sp.wait_ge(*stored["r"][D3].after(rounds - 1))

        def dense_close(S, rounds):
            S.close({c: rounds for c in DENSE})
            arr["x"][D0].close(rounds)
            stored["r"][D3].close(rounds)

        def setup():
            with ExitStack() as loc:
                def lb(name, shape, dt=F32):
                    return loc.enter_context(nc.sbuf_tensor(name, shape, dt))

                rows_i = lb("rows_i", [T, 2, P], I32)
                rows_h = lb("rows_h", [T, 2, P], I32)
                rows_l = lb("rows_l", [T, 2, P], I32)
                rows_f = lb("rows_f", [T, 7, P])
                cols = lb("cols", [P, 7, T])
                wraw = lb("wraw", [P, 6, P])
                wt = lb("wt", [P, 2, P])
                braw = lb("braw", [P, 6])
                b2s = lb("b2s", [P, 1])
                loads = sem_loads
                m_iota, m_one, m_mh, m_z = [Mark("pool") for _ in range(4)]
                with nc.Block() as block:
                    @block.gpsimd
                    def _(pool):
                        nc.gpsimd.iota(iota_i[:], pattern=[[1, LO]], base=0, channel_multiplier=0)
                        nc.gpsimd.iota(pidx_i[:], pattern=[[0, 1]], base=0, channel_multiplier=1).then_inc(s_pool, 1)
                        nc.gpsimd.memset(ones[:], 1.0).then_inc(s_pool, 1)
                        nc.gpsimd.memset(mhalf[:], -0.5).then_inc(s_pool, 1)
                        nc.gpsimd.memset(zero[:], 0.0).then_inc(s_pool, 1)
                        for e in ("pool", "gather"):
                            for c in uses[e]:
                                pool.sem_inc(lane_sems[e][c], PRIME)

                    dve_pad = Mark("dve")

                    @block.vector
                    def _(dve):
                        nc.vector.memset(rows_i[:], PAD)
                        nc.vector.memset(rows_f[:, 6, :], 0.0)
                        nc.vector.memset(minus1[:], -1.0)
                        for buf in (H, DX[D0], DX[D1], Z[DE], Z[D1], Z[D2]):
                            nc.vector.memset(buf[:], 0.0)
                        nc.vector.memset(zerob[:], 0.0).then_inc(s_dve, 1)
                        dve.wait_ge(s_pool, m_iota.value)
                        nc.vector.tensor_copy(pidx[:], pidx_i[:])
                        nc.vector.tensor_copy(iot[:], iota_i[:]).then_inc(s_dve, 1)
                        dve.wait_ge(s_dve, 2)
                        nc.vector.tensor_scalar(ident[:], iot[:, 0:P], pidx[:, 0:1], None, ALU.is_equal)
                        nc.vector.tensor_scalar(identb[:], iot[:, 0:P], pidx[:, 0:1], None, ALU.is_equal)
                        nc.vector.tensor_scalar(before[:], iot[:, 0:P], pidx[:, 0:1], None, ALU.is_lt)
                        nc.vector.tensor_scalar(above[:], iot[:, 0:P], pidx[:, 0:1], None, ALU.is_gt).then_inc(s_dve, 1)
                        dve.wait_ge(loads, 16 * 6)
                        nc.vector.tensor_scalar(rows_h[:], rows_i[:], 9, None, ALU.arith_shift_right)
                        nc.vector.tensor_scalar(rows_l[:], rows_i[:], LO - 1, None, ALU.bitwise_and)
                        nc.vector.tensor_copy(rows_f[:, 0:2, :], rows_i[:]).then_inc(s_dve, 1)
                        dve.wait_ge(s_dve, 4)
                        nc.vector.tensor_copy(rows_f[:, 2:4, :], rows_h[:])
                        nc.vector.tensor_copy(rows_f[:, 4:6, :], rows_l[:]).then_inc(s_dve, 1)
                        dve.wait_ge(s_pe, 1)
                        nc.vector.tensor_copy(cols[:, 0:4, :], K[0][:, 0:4 * T].rearrange("p (a b) -> p a b", b=T))
                        nc.vector.tensor_copy(cols[:, 4:7, :], K[1][:, 0:3 * T].rearrange("p (a b) -> p a b", b=T)).then_inc(s_dve, 1)
                        dve.wait_ge(s_pe, 2)
                        for k, n in enumerate(["Wi", "Wg", "Wo"]):
                            nc.vector.tensor_copy(W[n][:], K[2][:, k * P:(k + 1) * P])
                        nc.vector.tensor_copy(wt[:, 0, :], K[3][:, 0:P])
                        nc.vector.tensor_copy(wt[:, 1, :], K[3][:, P:2 * P]).then_inc(s_dve, 1)
                        nc.vector.tensor_tensor(braw[:, 0:3], braw[:, 0:3], braw[:, 3:6], ALU.add).then_inc(s_dve, 1)
                        dve.wait_ge(s_dve, 8)
                        dve.wait_ge(s_pe, 3)
                        nc.vector.tensor_copy(W["L1_W23"][:], K[4][:, 0:P])
                        nc.vector.tensor_tensor(B["L1_b23"][:], K[5][:, 0:1], b3raw[:], ALU.add)
                        for k, n in enumerate(["bi", "bg", "bo"]):
                            nc.vector.tensor_tensor(B[n][:], K[6][:, k:k + 1], braw[:, k:k + 1], ALU.add)
                        nc.vector.drain().then_inc(s_dve, 1)
                        for c in uses["dve"]:
                            dve.sem_inc(lane_sems["dve"][c], PRIME)

                    @block.sync
                    def _(sp):
                        sp.wait_ge(s_dve, 1)
                        for k, n in enumerate(["dst", "src"]):
                            sp.dma_start(rows_i[0:F_FULL, k, :], a[n][0:F_FULL * P].rearrange("(t p) -> t p", p=P)).then_inc(loads, 16)
                            sp.dma_start(rows_i[F_FULL:F_FULL + 1, k, 0:F_REST], a[n][F_FULL * P:E].rearrange("(t p) -> t p", t=1)).then_inc(loads, 16)
                        ew = a["edge_weight"]
                        sp.dma_start(rows_f[0:F_FULL, 6, :], ew[0:F_FULL * P].rearrange("(t p) -> t p", p=P)).then_inc(loads, 16)
                        sp.dma_start(rows_f[F_FULL:F_FULL + 1, 6, 0:F_REST], ew[F_FULL * P:E].rearrange("(t p) -> t p", t=1)).then_inc(loads, 16)
                        wih, whh = a["L1_gnn_W_ih"], a["L1_gnn_W_hh"]
                        for k, g in enumerate([0, 2, 3]):
                            sp.dma_start(wraw[:, k, :], wih[g * P:(g + 1) * P, :]).then_inc(loads2, 16)
                            sp.dma_start(whraw[:, k, :], whh[g * P:(g + 1) * P, :]).then_inc(loads2, 16)
                            sp.dma_start(braw[:, k:k + 1], a["L1_gnn_b_ih"][g * P:(g + 1) * P].unsqueeze(1)).then_inc(loads2, 16)
                            sp.dma_start(braw[:, 3 + k:4 + k], a["L1_gnn_b_hh"][g * P:(g + 1) * P].unsqueeze(1)).then_inc(loads2, 16)
                        sp.dma_start(wraw[:, 3, :], a["L1_gnn_W2"]).then_inc(loads2, 16)
                        sp.dma_start(wraw[:, 4, :], a["L1_gnn_W3"]).then_inc(loads2, 16)
                        sp.dma_start(b2s[:], a["L1_gnn_b2"].unsqueeze(1)).then_inc(loads2, 16)
                        sp.dma_start(b3raw[:], a["L1_gnn_b3"].unsqueeze(1)).then_inc(loads2, 16)
                        direct = [("L0_W1", a["L0_gnn_W1"]), ("L0_W2a", a["L0_gnn_W2"][0:P, :]), ("L0_W2b", a["L0_gnn_W2"][P:2 * P, :]),
                                  ("L0_W3", a["L0_gnn_W3"]), ("L1_W1", a["L1_gnn_W1"]), ("L3_W1", a["L3_gnn_W1"]), ("L3_W2", a["L3_gnn_W2"])]
                        for k in range(3):
                            for m, t in enumerate("xfb"):
                                direct.append((f"W{k}{t}", a[f"L2_gnn_W{k}"][m * P:(m + 1) * P, :]))
                        for n, src in direct:
                            sp.dma_start(W[n][:], src).then_inc(loads2, 16)
                        dbias = [("L0_b1", "L0_gnn_b1"), ("L0_b2", "L0_gnn_b2"), ("L0_b3", "L0_gnn_b3"), ("L1_b1", "L1_gnn_b1"),
                                 ("L2_b0", "L2_gnn_b0"), ("L2_b1", "L2_gnn_b1"), ("L2_b2", "L2_gnn_b2"), ("L3_b1", "L3_gnn_b1"), ("L3_b2", "L3_gnn_b2")]
                        for n, src in dbias:
                            sp.dma_start(B[n][:], a[src].unsqueeze(1)).then_inc(loads2, 16)
                        sp.wait_ge(loads2, 16 * N_LOADS2)
                        sp.wait_ge(s_pool, m_z.value)
                        spare = [tab[EP + 16 * m:EP + 16 * m + 16, :] for tab in (tab_f0, tab_f1, tab_b) for m in range(P // 16)]
                        for n, by_lane in stored.items():
                            for c in by_lane:
                                sp.dma_start(spare.pop(0), zero[0:16, 0:D]).then_inc(stored[n][c].sem, 16)
                        for rows in spare:
                            sp.dma_start(rows, zero[0:16, 0:D]).then_inc(setup_dma.sem, 16)
                        sp.dma_start(key_d[0:1].unsqueeze(0), minus1[0:1, 0:1]).then_inc(setup_dma.sem, 16)
                        sp.dma_start(key_s[0:1].unsqueeze(0), minus1[0:1, 0:1]).then_inc(setup_dma.sem, 16)
                        for n, by_lane in stored.items():
                            for c in by_lane:
                                sp.wait_ge(stored[n][c].sem, 16)
                                stored[n][c].base = 16
                        sp.wait_ge(setup_dma.sem, SD)

                    @block.tensor
                    def _(pe):
                        pe.wait_ge(s_dve, 5)
                        for k in range(7):
                            last = nc.tensor.transpose(K[k // 4][:, (k % 4) * T:(k % 4 + 1) * T], rows_f[:, k, :], ident[0:T, 0:T])
                        last.then_inc(s_pe, 1)
                        pe.wait_ge(loads2, 16 * N_LOADS2)
                        for k in range(3):
                            nc.tensor.transpose(K[2][:, k * P:(k + 1) * P], wraw[:, k, :], ident[:])
                        nc.tensor.transpose(K[3][:, 0:P], wraw[:, 3, :], ident[:])
                        nc.tensor.transpose(K[3][:, P:2 * P], wraw[:, 4, :], ident[:]).then_inc(s_pe, 1)
                        pe.wait_ge(s_dve, 7)
                        nc.tensor.matmul(K[4][:, 0:P], wt[:, 0, :], wt[:, 1, :], start=True, stop=True)
                        nc.tensor.matmul(K[5][:, 0:1], wt[:, 1, :], b2s[:], start=True, stop=True)
                        for k in range(3):
                            last = nc.tensor.transpose(K[7][:, k * P:(k + 1) * P], whraw[:, k, :], ident[:])
                        last.then_inc(s_pe2, 1)
                        pe.wait_ge(s_act, 1)
                        pe.wait_ge(s_pool, m_z.value)
                        for k in range(3):
                            last = nc.tensor.matmul(K[6][:, k:k + 1], whT[:, k, :], zero[:, 0:1], start=True, stop=True)
                        last.then_inc(s_pe, 1)
                        for c in uses["pe"]:
                            pe.sem_inc(lane_sems["pe"][c], PRIME)

                    @block.scalar
                    def _(act):
                        act.wait_ge(s_pe2, 1)
                        nc.scalar.activation(whT[:].rearrange("p a b -> p (a b)"), K[7][:, 0:3 * P], ACT.Copy).then_inc(s_act, 1)
                        for c in uses["act"]:
                            act.sem_inc(lane_sems["act"][c], PRIME)
                sort(cols, loc)

        def sort(cols, loc):
            def lb(name, shape, dt=F32):
                return loc.enter_context(nc.sbuf_tensor(name, shape, dt))

            oneh = [[lb(f"oneh{b}_{k}", [P, HI], BF16) for k in range(2)] for b in range(2)]
            onel = [[lb(f"onel{b}_{k}", [P, LO], BF16) for k in range(2)] for b in range(2)]
            onehf = [lb(f"onehf{b}", [P, HI]) for b in range(2)]
            onelw = [lb(f"onelw{b}", [P, LO]) for b in range(2)]
            hist = lb("hist", [HI, 3, LO])
            base = lb("base", [HI, 2, LO])
            rowtot = lb("rowtot", [HI, 2])
            rowbase = lb("rowbase", [HI, 2])
            nt = lb("nt", [HI, LO, NF])
            t1 = lb("t1", [HI, LO])
            t2 = lb("t2", [HI, LO])
            t3 = lb("t3", [HI, LO])
            t4 = lb("t4", [HI, LO])

            with nc.Block() as block:
                @block.vector
                def _(dve):
                    with dve.Fori(0, T // 2) as i:
                        for b in range(2):
                            t = i * 2 + b
                            dve.wait_ge(hist_done, t + 1)
                            for k in range(2):
                                nc.vector.tensor_scalar(oneh[b][k][:], iot[:, 0:HI], cols[:, 2 + k, bass.ds(t, 1)], None, ALU.is_equal)
                                nc.vector.tensor_scalar(onel[b][k][:], iot[:], cols[:, 4 + k, bass.ds(t, 1)], None, ALU.is_equal)
                            nc.vector.tensor_scalar(onehf[b][:], iot[:, 0:HI], cols[:, 2, bass.ds(t, 1)], None, ALU.is_equal)
                            nc.vector.tensor_scalar(onelw[b][:], iot[:], cols[:, 4, bass.ds(t, 1)], cols[:, 6, bass.ds(t, 1)],
                                                    ALU.is_equal, ALU.mult).then_inc(onehots_ready, 1)
                    dve.wait_ge(hist_done, T + 3)
                    for k in range(3):
                        last = nc.vector.tensor_copy(hist[:, k, :], K[k][0:HI, :])
                    last.then_inc(s_dve, 1)

                @block.tensor
                def _(pe):
                    for k in range(3):
                        last = nc.tensor.matmul(K[k][0:HI, :], zerob[:, 0:HI], zerob[:], start=True, stop=False)
                        if k:
                            last.then_inc(hist_done, 1)
                    with pe.Fori(0, T // 2) as i:
                        for b in range(2):
                            pe.wait_ge(onehots_ready, i * 2 + (b + 1))
                            for k in range(2):
                                nc.tensor.matmul(K[k][0:HI, :], oneh[b][k][:], onel[b][k][:], start=False, stop=False)
                            nc.tensor.matmul(K[2][0:HI, :], onehf[b][:], onelw[b][:], start=False, stop=False).then_inc(hist_done, 1)
                    for k in range(3):
                        last = nc.tensor.matmul(K[k][0:HI, :], zerob[:, 0:HI], zerob[:], start=False, stop=True)
                    last.then_inc(hist_done, 1)

            d0 = 10
            with nc.Block() as block:
                @block.vector
                def _(dve):
                    n = [d0]

                    def link(ins):
                        n[0] += 1
                        ins.then_inc(s_dve, 1)
                        dve.wait_ge(s_dve, n[0])

                    link(nc.vector.tensor_reduce(rowtot[:], hist[:, 0:2, :], AX, ALU.add))
                    dve.wait_ge(s_pe, 4)
                    link(nc.vector.tensor_copy(rowbase[:], K[3][0:HI, 0:2]))
                    for k in range(2):
                        link(nc.vector.tensor_tensor_scan(t1[:], ones[0:HI, :], hist[:, k, :], rowbase[:, k:k + 1], ALU.mult, ALU.add))
                        nc.vector.tensor_tensor(base[:, k, :], t1[:], hist[:, k, :], ALU.subtract)
                        link(nc.vector.tensor_scalar(t2[:], hist[:, k, :], 1.0, None, ALU.min))
                        link(nc.vector.scalar_tensor_tensor(t3[:], t1[:], float(-1 - EP), t2[:], ALU.add, ALU.mult))
                        link(nc.vector.tensor_scalar(nt[:, :, N_ENDD + k], t3[:], float(EP), None, ALU.add))
                        link(nc.vector.tensor_scalar(t4[:], hist[:, k, :], 1.0, None, ALU.max))
                        link(nc.vector.reciprocal(nt[:, :, N_INVIN if k == 0 else N_INVOUT], t4[:]))
                    nc.vector.tensor_copy(nt[:, :, N_CNTD], hist[:, 0, :])
                    nc.vector.tensor_scalar(nt[:, :, 7], hist[:, 0, :], 0.0, None, ALU.mult)
                    link(nc.vector.tensor_scalar(t1[:], hist[:, 0, :], 1.0, None, ALU.add))
                    link(nc.vector.tensor_scalar(t2[:], hist[:, 2, :], 1.0, None, ALU.add))
                    link(nc.vector.tensor_scalar(t3[:], t2[:], 0.0, None, ALU.is_gt))
                    link(nc.vector.tensor_scalar(t4[:], t3[:], -1.0, 1.0, ALU.mult, ALU.add))
                    link(nc.vector.tensor_tensor(t2[:], t2[:], t3[:], ALU.mult))
                    link(nc.vector.tensor_tensor(t2[:], t2[:], t4[:], ALU.add))
                    dve.sem_inc(degrees_ready, 1)
                    dve.wait_ge(s_pool, 6)
                    nc.vector.tensor_copy(nt[:, :, N_DINV1], hist[:, 0, :])
                    link(nc.vector.tensor_tensor(nt[:, :, N_DINV3], hist[:, 1, :], t3[:], ALU.mult))

                @block.gpsimd
                def _(pool):
                    pool.wait_ge(degrees_ready, 1)
                    nc.gpsimd.tensor_tensor(hist[:, 0, :], t1[:], mhalf[0:HI, :], ALU.pow).then_inc(s_pool, 1)
                    nc.gpsimd.tensor_tensor(hist[:, 1, :], t2[:], mhalf[0:HI, :], ALU.pow).then_inc(s_pool, 1)

                @block.tensor
                def _(pe):
                    pe.wait_ge(s_dve, d0 + 1)
                    nc.tensor.matmul(K[3][0:HI, 0:2], above[0:HI, 0:HI], rowtot[:], start=True, stop=True).then_inc(s_pe, 1)

                @block.sync
                def _(sp):
                    sp.wait_ge(s_dve, d0 + 2 + 2 * 6 + 7)
                    sp.dma_start(node_tab.rearrange("(h l) f -> h (l f)", h=HI), nt[:].rearrange("h l f -> h (l f)")).then_inc(setup_dma.sem, 16)
                    sp.wait_ge(setup_dma.sem, SD + 16)

            pos = lb("pos", [P, 2, T])
            pair = [dict(onehf=[lb(f"onehf_b{b}k{k}", [P, HI]) for k in range(2)], kbc=[lb(f"kbc_b{b}k{k}", [P, P]) for k in range(2)],
                         keys=lb(f"keys_b{b}", [P, 2, 1]), ohT=lb(f"ohT_b{b}", [HI, 2, P])) for b in range(2)]
            pick = [lb(f"pick{k}", [P, LO]) for k in range(2)]
            tie = [lb(f"tie{k}", [P, P]) for k in range(2)]
            acc = [lb(f"acc{k}", [P, 2]) for k in range(2)]
            place = [("look", "pe"), ("outer", "pe"), ("tie", "dve"), ("base", "dve"), ("pick", "dve"), ("pos", "dve")]
            S = Steps(lane_sems, lane_base, {LA: place, LB: place, NA: [("hots", "dve"), ("trans", "pe"), ("ohT", "act")]})
            dense1 = Steps(lane_sems, lane_base, DENSE)
            keys_T, looked, outer = K[0], (K[1], K[2]), K[3]
            ROUNDS = T // RANK_TILES

            def tiles(eng, ahead, now, dense_part):
                def body(i, more):
                    for u in range(RANK_TILES):
                        t = i * RANK_TILES + u
                        dense_part(i, 2 * u)
                        now(t, u % 2, lambda: ahead(t + 1, (u + 1) % 2) if more or u < RANK_TILES - 1 else None,
                            lambda: dense_part(i, 2 * u + 1))
                ahead(0, 0)
                with eng.Fori(0, ROUNDS - 1) as i:
                    body(i, True)
                body(ROUNDS - 1, False)

            with nc.Block() as block:
                @block.vector
                def _(dve):
                    def ahead(t, b):
                        for k in range(2):
                            dve.wait_ge(*S.after("outer", k, t - 2))
                        dve.wait_ge(*S.after("trans", NA, t - 2))
                        for k in range(2):
                            nc.vector.tensor_scalar(pair[b]["onehf"][k][:], iot[:, 0:HI], cols[:, 2 + k, bass.ds(t, 1)], None, ALU.is_equal)
                            nc.vector.tensor_scalar(oneh[b][k][:], iot[:, 0:HI], cols[:, 2 + k, bass.ds(t, 1)], None, ALU.is_equal)
                            nc.vector.tensor_scalar(onel[b][k][:], iot[:], cols[:, 4 + k, bass.ds(t, 1)], None, ALU.is_equal)
                            nc.vector.tensor_scalar(pair[b]["kbc"][k][:], ones[:, 0:P], cols[:, k, bass.ds(t, 1)], None, ALU.mult)
                        nc.vector.tensor_copy(pair[b]["keys"][:], cols[:, 0:2, bass.ds(t, 1)]).then_inc(S.did("hots", NA), 1)

                    def now(t, b, prepare, between):
                        dve.wait_ge(*S.after("hots", NA, t))
                        dve.wait_ge(*S.after("ohT", NA, t))
                        for k in range(2):
                            dve.wait_ge(*S.after("pos", k, t - 1))
                            nc.vector.scalar_tensor_tensor(tie[k][:], keys_T[:, (2 * k + 1) * P:(2 * k + 2) * P], pair[b]["keys"][:, k, :], before[:],
                                                           ALU.is_equal, ALU.mult, accum_out=acc[k][:, 0:1]).then_inc(S.did("tie", k), 1)
                        prepare()
                        between()
                        for k in range(2):
                            dve.wait_ge(*S.after("outer", k, t))
                            dve.wait_ge(*S.after("look", k, t))
                            nc.vector.tensor_tensor(base[:, k, :], base[:, k, :], outer[0:HI, :], ALU.add).then_inc(S.did("base", k), 1)
                        for k in range(2):
                            nc.vector.scalar_tensor_tensor(pick[k][:], looked[k][:], 1.0, onel[b][k][:], ALU.mult, ALU.mult,
                                                           accum_out=acc[k][:, 1:2]).then_inc(S.did("pick", k), 1)
                        for k in range(2):
                            dve.wait_ge(*S.after("pick", k, t))
                            nc.vector.tensor_tensor(pos[:, k, bass.ds(t, 1)], acc[k][:, 0:1], acc[k][:, 1:2], ALU.add).then_inc(S.did("pos", k), 1)
                    tiles(dve, ahead, now, lambda i, part: dense_dve(dve, dense1, i, part))

                @block.tensor
                def _(pe):
                    def ahead(t, b):
                        pe.wait_ge(*S.after("hots", NA, t))
                        pe.wait_ge(*S.after("ohT", NA, t - 1))
                        for k in range(2):
                            pe.wait_ge(*S.after("tie", k, t - 1))
                        for k in range(2):
                            nc.tensor.transpose(keys_T[0:HI, 2 * k * P:(2 * k + 1) * P], pair[b]["onehf"][k][:], ident[:])
                            last = nc.tensor.transpose(keys_T[:, (2 * k + 1) * P:(2 * k + 2) * P], pair[b]["kbc"][k][:], ident[:])
                        last.then_inc(S.did("trans", NA), 1)

                    def now(t, b, prepare, between):
                        pe.wait_ge(*S.after("ohT", NA, t))
                        for k in range(2):
                            pe.wait_ge(*S.after("base", k, t - 1))
                            pe.wait_ge(*S.after("pick", k, t - 1))
                            nc.tensor.matmul(looked[k][:], pair[b]["ohT"][:, k, :], base[:, k, :], start=True, stop=True).then_inc(S.did("look", k), 1)
                        nc.tensor.matmul(outer[0:HI, :], oneh[b][0][:], onel[b][0][:], start=True, stop=True).then_inc(S.did("outer", 0), 1)
                        prepare()
                        between()
                        pe.wait_ge(*S.after("base", 0, t))
                        nc.tensor.matmul(outer[0:HI, :], oneh[b][1][:], onel[b][1][:], start=True, stop=True).then_inc(S.did("outer", 1), 1)
                    tiles(pe, ahead, now, lambda i, part: dense_pe(pe, dense1, i, part))

                @block.scalar
                def _(act):
                    def ahead(t, b):
                        act.wait_ge(*S.after("trans", NA, t))
                        for k in range(2):
                            act.wait_ge(*S.after("look", k, t - 2))
                        nc.scalar.activation(pair[b]["ohT"][:], keys_T[0:HI, :].rearrange("h (k m) -> h k m", k=2)[:, :, 0:P],
                                             ACT.Copy).then_inc(S.did("ohT", NA), 1)

                    def now(t, b, prepare, between):
                        prepare()
                        between()
                    tiles(act, ahead, now, lambda i, part: dense_act(act, dense1, i, part))

                @block.sync
                def _(sp):
                    dense_sync(sp, dense1, 0, DENSE_RANK)
            S.close({LA: T, LB: T, NA: T})
            dense_close(dense1, DENSE_RANK)
            records(cols, pos, loc)

        def records(cols, pos, loc):
            def lb(name, shape, dt=F32):
                return loc.enter_context(nc.sbuf_tensor(name, shape, dt))

            G = 10
            idx_i = lb("idx_i", [P, 4, T], I32)
            rec = lb("rec", [P, T, RF])
            idx_g = lb("idx_g", [P, 2, G], I32)
            got = [lb(f"got{k}", [P, G, NF]) for k in range(2)]
            part = lb("part", [P, G, RF])
            m0 = {"dve": d0 + 2 + 2 * 6 + 7 + 1, "pool": 6}
            rd_c = lb("rd_c", [P, T, RF])
            rs_c = lb("rs_c", [P, T, RF])
            dense2 = Steps(lane_sems, lane_base, DENSE)
            with nc.Block() as block:
                @block.vector
                def _(dve):
                    nc.vector.tensor_copy(idx_i[:, 0:2, :], cols[:, 0:2, :])
                    nc.vector.tensor_copy(idx_i[:, 2:4, :], pos[:])
                    nc.vector.tensor_copy(rec[:, :, R_DST], cols[:, 0, :])
                    nc.vector.tensor_copy(rec[:, :, R_SRC], cols[:, 1, :])
                    nc.vector.tensor_copy(rec[:, :, R_W], cols[:, 6, :])
                    nc.vector.tensor_copy(rec[:, :, R_POSS], pos[:, 1, :])
                    nc.vector.tensor_scalar(rec[:, :, 15], pos[:, 1, :], 0.0, None, ALU.mult).then_inc(rec_ready, 1)
                    with dve.Fori(0, DENSE_RECORDS) as i:
                        for part in PARTS:
                            dense_dve(dve, dense2, i, part)

                @block.tensor
                def _(pe):
                    with pe.Fori(0, DENSE_RECORDS) as i:
                        for part in PARTS:
                            dense_pe(pe, dense2, i, part)

                @block.scalar
                def _(act):
                    with act.Fori(0, DENSE_RECORDS) as i:
                        for part in PARTS:
                            dense_act(act, dense2, i, part)

                @block.sync
                def _(sp):
                    dense_sync(sp, dense2, DENSE_RANK, DENSE_RECORDS)

                @block.gpsimd
                def _(pool):
                    pool.wait_ge(rec_ready, 1)
                    pool.sem_inc(copied, 1)
                    with pool.Fori(0, T // G) as r:
                        pool.wait_ge(copied, r * 3 + 1)
                        pool.sem_inc(pool_passed, 1)
                        nc.gpsimd.tensor_copy(idx_g[:], idx_i[:, 0:2, bass.ds(r * G, G)]).then_inc(copied, 1)
                        pool.wait_ge(copied, r * 3 + 2)
                        pool.sem_inc(pool_passed, 1)
                        for k in range(2):
                            for g in range(G):
                                nc.gpsimd.indirect_dma_start(
                                    out=got[k][:, g, :], out_offset=None, in_=node_tab,
                                    in_offset=bass.IndirectOffsetOnAxis(ap=idx_g[:, k, g:g + 1].bitcast(U32), axis=0),
                                    bounds_check=HI * LO - 1, oob_is_err=False).then_inc(pool_dma.sem, 16)
                        pool.wait_ge(pool_dma.sem, r * (32 * G) + 32 * G)
                        pool.sem_inc(pool_passed, 1)
                        view = rec[:, bass.ds(r * G, G), :]
                        for dst, side, src in ((R_DINV1A, 0, N_DINV1), (R_DINV3A, 0, N_DINV3), (R_INVIN, 0, N_INVIN),
                                               (R_ENDD_DST, 0, N_ENDD), (R_ENDS_DST, 0, N_ENDS),
                                               (R_DINV1B, 1, N_DINV1), (R_DINV3B, 1, N_DINV3), (R_INVOUT, 1, N_INVOUT),
                                               (R_ENDD_SRC, 1, N_ENDD), (R_ENDS_SRC, 1, N_ENDS)):
                            nc.gpsimd.tensor_copy(view[:, :, dst:dst + 1], got[side][:, :, src:src + 1])
                        nc.gpsimd.tensor_copy(view[:, :, R_CNTD_SRC:R_CNTD_SRC + 1], got[1][:, :, N_CNTD:N_CNTD + 1]).then_inc(copied, 1)
                        pool.wait_ge(copied, r * 3 + 3)
                        pool.sem_inc(copied, 1)
                    pool.wait_ge(copied, (T // G) * 3 + 1)
                    with pool.Fori(0, T // G) as r:
                        nc.gpsimd.tensor_copy(part[:], rec[:, bass.ds(r * G, G), :])
                        nc.gpsimd.tensor_copy(idx_g[:], idx_i[:, 2:4, bass.ds(r * G, G)]).then_inc(copied, 1)
                        pool.wait_ge(copied, r + ((T // G) * 3 + 2))
                        pool.sem_inc(pool_passed, 1)
                        for k, tab in enumerate((rec_d, rec_s)):
                            for g in range(G):
                                nc.gpsimd.indirect_dma_start(
                                    out=tab, out_offset=bass.IndirectOffsetOnAxis(ap=idx_g[:, k, g:g + 1].bitcast(U32), axis=0),
                                    in_=part[:, g, :], in_offset=None, bounds_check=EP - 1, oob_is_err=False).then_inc(pool_dma.sem, 16)
                        pool.wait_ge(pool_dma.sem, r * (32 * G) + (T // G + 1) * 32 * G)
                        pool.sem_inc(pool_passed, 1)
                    pool_dma.base = 2 * (T // G) * 32 * G
            dense_close(dense2, DENSE_RECORDS)

            sd_r = lb("sd_r", [T, 12, P])
            prev = lb("prev", [T, 2, P])
            e_pos = lb("e_pos", [P, T])
            e_pos_i = lb("e_pos_i", [P, T], I32)
            u1 = lb("u1", [P, T])
            u2 = lb("u2", [P, T])
            u3 = lb("u3", [P, T])
            with nc.Block() as block:
                @block.sync
                def _(sp):
                    sp.dma_start(rd_c[:], rec_d.rearrange("(t p) f -> p t f", p=P)).then_inc(setup_dma.sem, 16)
                    sp.dma_start(rs_c[:], rec_s.rearrange("(t p) f -> p t f", p=P)).then_inc(setup_dma.sem, 16)
                    sp.wait_ge(rows_done, 3)
                    sp.dma_start(key_d[1:1 + EP].rearrange("(t p) -> t p", p=P), sd_r[:, 0, :]).then_inc(setup_dma.sem, 16)
                    sp.dma_start(key_s[1:1 + EP].rearrange("(t p) -> t p", p=P), sd_r[:, 7, :]).then_inc(setup_dma.sem, 16)
                    sp.wait_ge(setup_dma.sem, SD + 16 + 64)
                    sp.dma_start(prev[:, 0, :], key_d[0:EP].rearrange("(t p) -> t p", p=P)).then_inc(setup_dma.sem, 16)
                    sp.dma_start(prev[:, 1, :], key_s[0:EP].rearrange("(t p) -> t p", p=P)).then_inc(setup_dma.sem, 16)
                    sp.wait_ge(same_done, 1)
                    sc = scal.rearrange("c j b -> c (j b)").rearrange("c (t p) -> c t p", p=P)
                    for c, row in ((C_SAMED, 9), (C_W, 1), (C_D1A, 2), (C_D1B, 3), (C_D3A, 4), (C_D3B, 5), (C_INVOUT, 6),
                                   (C_SAMES, 10), (C_INVIN, 8)):
                        sp.dma_start(sc[c], sd_r[:, row, :]).then_inc(setup_dma.sem, 16)
                    sp.wait_ge(setup_dma.sem, SD + 16 + 64 + 32 + 16 * CF)
                    setup_dma.base = 0

                @block.tensor
                def _(pe):
                    pe.wait_ge(setup_dma.sem, SD + 16 + 32)
                    fields = [(rd_c, R_DST), (rd_c, R_W), (rd_c, R_DINV1A), (rd_c, R_DINV1B), (rd_c, R_DINV3A), (rd_c, R_DINV3B),
                              (rd_c, R_INVOUT), (rs_c, R_SRC), (rs_c, R_INVIN)]
                    for n, (src, f) in enumerate(fields):
                        last = nc.tensor.transpose(K[n // 4][0:T, (n % 4) * P:(n % 4 + 1) * P], src[:, :, f], ident[:])
                        if n % 4 == 3 or n == 8:
                            last.then_inc(rows_T, 1)

                @block.scalar
                def _(act):
                    for n in range(3):
                        w = 4 if n < 2 else 1
                        act.wait_ge(rows_T, n + 1)
                        nc.scalar.activation(sd_r[:, 4 * n:4 * n + w, :].rearrange("t a b -> t (a b)"), K[n][0:T, 0:w * P], ACT.Copy).then_inc(rows_done, 1)

                @block.gpsimd
                def _(pool):
                    nc.gpsimd.iota(e_pos_i[:], pattern=[[P, T]], base=0, channel_multiplier=1).then_inc(copied, 1)

                @block.vector
                def _(dve):
                    n = [0]

                    def link(ins):
                        n[0] += 1
                        ins.then_inc(lists_dve, 1)
                        dve.wait_ge(lists_dve, n[0])

                    dve.wait_ge(setup_dma.sem, SD + 16 + 32)
                    dve.wait_ge(copied, (T // G) * 4 + 2)
                    nc.vector.tensor_copy(e_pos[:], e_pos_i[:])
                    nc.vector.tensor_scalar(IX["xa"][:], rd_c[:, :, R_DST], float(N - 1), None, ALU.min)
                    nc.vector.tensor_scalar(IX["xb"][:], rd_c[:, :, R_SRC], float(N - 1), None, ALU.min)
                    nc.vector.tensor_copy(IX["end_f"][:], rd_c[:, :, R_ENDD_SRC])
                    nc.vector.tensor_copy(IX["end_bb"][:], rd_c[:, :, R_ENDS_SRC])
                    nc.vector.tensor_copy(IX["end_ba"][:], rd_c[:, :, R_ENDS_DST])
                    nc.vector.tensor_copy(IX["dst_in_s"][:], rs_c[:, :, R_ENDD_DST])
                    link(nc.vector.tensor_scalar(u1[:], rd_c[:, :, R_DST], float(N - 1), None, ALU.is_le))
                    link(nc.vector.tensor_tensor(u2[:], e_pos[:], rd_c[:, :, R_ENDD_DST], ALU.is_equal))
                    link(nc.vector.tensor_tensor(u1[:], u1[:], u2[:], ALU.mult))
                    link(nc.vector.scalar_tensor_tensor(u3[:], rd_c[:, :, R_DST], float(-SKIP), u1[:], ALU.add, ALU.mult))
                    link(nc.vector.tensor_scalar(IX["out_a"][:], u3[:], float(SKIP), None, ALU.add))
                    link(nc.vector.tensor_scalar(u1[:], rd_c[:, :, R_SRC], float(N - 1), None, ALU.is_le))
                    link(nc.vector.tensor_tensor(u2[:], rd_c[:, :, R_POSS], rd_c[:, :, R_ENDS_SRC], ALU.is_equal))
                    link(nc.vector.tensor_tensor(u1[:], u1[:], u2[:], ALU.mult))
                    link(nc.vector.tensor_scalar(u2[:], rd_c[:, :, R_CNTD_SRC], 0.0, None, ALU.is_equal))
                    link(nc.vector.tensor_tensor(u1[:], u1[:], u2[:], ALU.mult))
                    link(nc.vector.scalar_tensor_tensor(u3[:], rd_c[:, :, R_SRC], float(-SKIP), u1[:], ALU.add, ALU.mult))
                    link(nc.vector.tensor_scalar(IX["out_b"][:], u3[:], float(SKIP), None, ALU.add))
                    dve.wait_ge(setup_dma.sem, SD + 16 + 64 + 32)
                    dve.wait_ge(rows_done, 3)
                    nc.vector.tensor_tensor(sd_r[:, 9, :], sd_r[:, 0, :], prev[:, 0, :], ALU.is_equal)
                    nc.vector.tensor_tensor(sd_r[:, 10, :], sd_r[:, 7, :], prev[:, 1, :], ALU.is_equal).then_inc(same_done, 1)

        pidx_i = sb("pidx_i", [P, 1], I32)
        whraw = sb("whraw", [P, 3, P])
        whT = sb("whT", [P, 3, P])
        b3raw = sb("b3raw", [P, 1])
        sem_loads, loads2 = sem("edges_loaded"), sem("weights_loaded")
        N_LOADS2 = 12 + 4 + 16 + 9
        s_pe2 = sem("whh_transposed")
        hist_done, onehots_ready = sem("hist_done"), sem("onehots_ready")
        degrees_ready, rec_ready, copied = sem("degrees_ready"), sem("rec_ready"), sem("copied")
        rows_T, rows_done, same_done, lists_dve = sem("rows_T"), sem("rows_done"), sem("same_done"), sem("lists_dve")
        d0 = 10
        SD = 16 * (3 * P // 16 - 8 + 2)
        setup()
        if upto <= 0:
            return
        LV, LX, LS = per(AB, "in_v"), per(AB, "in_x"), per((LA, LB, LM), "in_scale")
        LT = per((LA, LB, LM), "in_same")
        G1, G2 = per(AB, "rows1"), per(AB, "rows2")
        B1.update(per((LA, LB, LM), "b1"))
        B2.update(per(AB, "b2"))
        BT, CT = per((TA, TB), "cell"), per((TA, TB), "tanh")
        SO.update(per((TA, TB), "sig_o"))
        Z.update(per(AB, "z"))
        ZM = [sb(f"sums{m}", [P, BLK]) for m in range(2)]
        OX, OV = per(AB, "out_x"), per(AB, "out_v")
        R.update(per((LA, LB, NA, NBL, LM), "out_rows"))

        def edge_stage(tab):
            steps = [("ids", "gather"), ("inT", "pe"), ("xa", "act"), ("xb", "dve"), ("proj", "pe"), ("hi", "act"), ("d", "dve"), ("mlp1", "pe"),
                     ("m1", "act"), ("mlp2", "pe"), ("m2", "act"), ("scan", "dve"), ("rowsT", "pe"), ("rows", "act")]
            S = Steps(lane_sems, lane_base, {LA: steps, LB: steps})
            KK = [[K[4 * c + m] for m in range(4)] for c in range(2)]
            with nc.Block() as block:
                @block.gpsimd
                def _(pool):
                    def body(i, cs):
                        for c in cs:
                            gather(pool, S, c, i, i * 2 + c, "inT", [("xa", a["x"], G1, "g1"), ("xb", a["x"], G2, "g2")])
                    in_turns(pool, body)

                @block.sync
                def _(sp):
                    def load(i, cs):
                        for c in cs:
                            sp.wait_ge(*S.after("scan", c, i - 1))
                            sp.dma_start(LT[c][:], bcast(C_SAMED, i * 2 + c)).then_inc(arr["same"][c].sem, 16)

                    def store(i, cs):
                        for c in cs:
                            j = i * 2 + c
                            sp.wait_ge(*S.after("xa", c, i))
                            sp.dma_start(st_x[0, j], OX[c][:]).then_inc(stored["x"][c].sem, 16)
                            sp.wait_ge(*S.after("xb", c, i))
                            sp.dma_start(st_x[1, j], OV[c][:]).then_inc(stored["v"][c].sem, 16)
                            sp.wait_ge(*S.after("rows", c, i))
                            sp.dma_start(rows_of(tab)[j], as_rows(R[c])).then_inc(stored["r"][c].sem, 16)

                    def finish():
                        for c in AB:
                            for n in ("x", "v", "r"):
                                sp.wait_ge(*stored[n][c].after(TURNS[c] - 1))

                    loads_and_stores(sp, load, store, finish)

                @block.tensor
                def _(pe):
                    def body(i, cs):
                        for c in cs:
                            pe.wait_ge(*arr["g1"][c].after(i, Q))
                            pe.wait_ge(*S.after("rows", c, i - 1))
                            transposes(KK[c][0], G1[c])
                            pe.wait_ge(*arr["g2"][c].after(i, Q))
                            transposes(KK[c][1], G2[c]).then_inc(S.did("inT", c), 1)
                        for c in cs:
                            pe.wait_ge(*S.after("xa", c, i))
                            nc.tensor.matmul(KK[c][2][:], W["L0_W1"][:], OX[c][:], start=True, stop=True)
                            pe.wait_ge(*S.after("xb", c, i))
                            nc.tensor.matmul(KK[c][3][:], W["L0_W1"][:], OV[c][:], start=True, stop=True).then_inc(S.did("proj", c), 1)
                        for c in cs:
                            pe.wait_ge(*S.after("hi", c, i))
                            nc.tensor.matmul(KK[c][0][:], W["L0_W2a"][:], B1[c][:], start=True, stop=False)
                            pe.wait_ge(*S.after("d", c, i))
                            nc.tensor.matmul(KK[c][0][:], W["L0_W2b"][:], B2[c][:], start=False, stop=True).then_inc(S.did("mlp1", c), 1)
                        for c in cs:
                            product(pe, S, c, i, "mlp2", "L0_W3", KK[c][1], LV[c], ["m1"], BLK)
                        for c in cs:
                            pe.wait_ge(*S.after("scan", c, i))
                            to_rows(KK[c][2], ZM[c]).then_inc(S.did("rowsT", c), 1)
                    in_turns(pe, body)

                @block.scalar
                def _(act):
                    def body(i, cs):
                        for c in cs:
                            act.wait_ge(*stored["x"][c].after(i - 1))
                            function(act, S, c, i, "xa", ACT.Copy, None, KK[c][0], OX[c], ["inT"], BLK)
                        for c in cs:
                            function(act, S, c, i, "hi", ACT.Identity, "L0_b1", KK[c][2], B1[c], ["proj"], BLK)
                        for c in cs:
                            function(act, S, c, i, "m1", ACT.Relu, "L0_b2", KK[c][0], LV[c], ["mlp1"], BLK)
                        for c in cs:
                            function(act, S, c, i, "m2", ACT.Relu, "L0_b3", KK[c][1], LX[c], ["mlp2"], BLK)
                        for c in cs:
                            act.wait_ge(*stored["r"][c].after(i - 1))
                            function(act, S, c, i, "rows", ACT.Copy, None, KK[c][2], R[c], ["rowsT"], BLK)
                    in_turns(act, body)

                @block.vector
                def _(dve):
                    def body(i, cs):
                        for c in cs:
                            dve.wait_ge(*S.after("inT", c, i))
                            dve.wait_ge(*stored["v"][c].after(i - 1))
                            nc.vector.tensor_copy(OV[c][:], KK[c][1][:]).then_inc(S.did("xb", c), 1)
                        for c in cs:
                            dve.wait_ge(*S.after("hi", c, i))
                            nc.vector.scalar_tensor_tensor(B2[c][:], KK[c][3][:], B["L0_b1"][:, 0:1], B1[c][:], ALU.add, ALU.subtract).then_inc(S.did("d", c), 1)
                        for c in cs:
                            dve.wait_ge(*S.after("m2", c, i))
                            dve.wait_ge(*arr["same"][c].after(i))
                            if c == LB:
                                dve.wait_ge(*S.after("scan", LA, i))
                            else:
                                dve.wait_ge(*S.after("scan", LB, i - 1))
                            dve.wait_ge(*S.after("rowsT", c, i - 1))
                            nc.vector.tensor_tensor_scan(ZM[c][:], LT[c][:], LX[c][:], ZM[1 - c][:, BLK - 1:BLK], ALU.mult, ALU.max).then_inc(S.did("scan", c), 1)
                    start_sums(dve)
                    in_turns(dve, body)
            S.close(TURNS)
            for c in AB:
                for n in ("g1", "g2"):
                    arr[n][c].close(TURNS[c], Q)
                arr["same"][c].close(TURNS[c])
                for n in ("x", "v", "r"):
                    stored[n][c].close(TURNS[c])

        def back_stage(wname):
            steps = [("ids", "gather"), ("inT", "pe"), ("in", "act"), ("msg", "pe"), ("scaled", "dve"), ("scan", "dve"), ("rowsT", "pe"), ("rows", "act")]
            S = Steps(lane_sems, lane_base, {LA: steps, LB: steps})
            KK = [[K[4 * c + m] for m in range(4)] for c in range(2)]
            with nc.Block() as block:
                @block.gpsimd
                def _(pool):
                    def body(i, cs):
                        for c in cs:
                            gather(pool, S, c, i, i * 2 + c, "inT", [("dst_in_s", tab_u, G1, "g1")])
                    in_turns(pool, body)

                @block.sync
                def _(sp):
                    def load(i, cs):
                        for c in cs:
                            sp.wait_ge(*S.after("scan", c, i - 1))
                            sp.dma_start(LT[c][:], bcast(C_SAMES, i * 2 + c)).then_inc(arr["same"][c].sem, 16)
                            sp.dma_start(LS[c][:], bcast(C_INVIN, i * 2 + c)).then_inc(arr["s"][c].sem, 16)

                    def store(i, cs):
                        for c in cs:
                            sp.wait_ge(*S.after("rows", c, i))
                            sp.dma_start(rows_of(tab_b)[i * 2 + c], as_rows(R[c])).then_inc(stored["r"][c].sem, 16)

                    def finish():
                        for c in AB:
                            sp.wait_ge(*stored["r"][c].after(TURNS[c] - 1))

                    loads_and_stores(sp, load, store, finish)

                @block.tensor
                def _(pe):
                    def body(i, cs):
                        for c in cs:
                            pe.wait_ge(*arr["g1"][c].after(i, Q))
                            pe.wait_ge(*S.after("in", c, i - 1))
                            transposes(KK[c][0], G1[c]).then_inc(S.did("inT", c), 1)
                        for c in cs:
                            pe.wait_ge(*S.after("scaled", c, i - 1))
                            product(pe, S, c, i, "msg", wname, KK[c][1], LV[c], ["in"], BLK)
                        for c in cs:
                            pe.wait_ge(*S.after("scan", c, i))
                            pe.wait_ge(*S.after("rows", c, i - 1))
                            to_rows(KK[c][2], ZM[c]).then_inc(S.did("rowsT", c), 1)
                    in_turns(pe, body)

                @block.scalar
                def _(act):
                    def body(i, cs):
                        for c in cs:
                            act.wait_ge(*S.after("msg", c, i - 1))
                            function(act, S, c, i, "in", ACT.Copy, None, KK[c][0], LV[c], ["inT"], BLK)
                        for c in cs:
                            act.wait_ge(*stored["r"][c].after(i - 1))
                            function(act, S, c, i, "rows", ACT.Copy, None, KK[c][2], R[c], ["rowsT"], BLK)
                    in_turns(act, body)

                @block.vector
                def _(dve):
                    def body(i, cs):
                        for c in cs:
                            dve.wait_ge(*S.after("msg", c, i))
                            dve.wait_ge(*S.after("scan", c, i - 1))
                            dve.wait_ge(*arr["s"][c].after(i))
                            nc.vector.tensor_tensor(B1[c][:], KK[c][1][:], LS[c][:], ALU.mult).then_inc(S.did("scaled", c), 1)
                            dve.wait_ge(*S.after("scaled", c, i))
                            dve.wait_ge(*arr["same"][c].after(i))
                            if c == LB:
                                dve.wait_ge(*S.after("scan", LA, i))
                            else:
                                dve.wait_ge(*S.after("scan", LB, i - 1))
                            dve.wait_ge(*S.after("rowsT", c, i - 1))
                            nc.vector.tensor_tensor_scan(ZM[c][:], LT[c][:], B1[c][:], ZM[1 - c][:, BLK - 1:BLK], ALU.mult, ALU.add).then_inc(S.did("scan", c), 1)
                    start_sums(dve)
                    in_turns(dve, body)
            S.close(TURNS)
            for c in AB:
                arr["g1"][c].close(TURNS[c], Q)
                arr["same"][c].close(TURNS[c])
                arr["s"][c].close(TURNS[c])
                stored["r"][c].close(TURNS[c])

        def slot_stage(tab, weight=None, bias=None, relu=True, two_way=False, v_from="v", pre=None, post=None,
                       resid=False, lstm=False, rows_to=False, final=False, msg=None, dense=None):
            norm = resid or lstm
            NS_, XS_, TS_ = (NA, NBL), (XA, XB), (TA, TB)
            agg = []
            if weight:
                agg += ([("rowsum", "dve")] if two_way else []) + [("pre", "pe")] + ([("scaled", "dve")] if pre else []) + [("act", "act")]
            else:
                agg += [("pre", "pe")]
            if norm:
                agg += [("z", "dve")]
            elif post:
                agg += [("v", "dve")]
            uT = [("uT", "pe"), ("uR", "act")] if rows_to and not norm else []
            lanes = {LA: [("ids", "gather")] * (two_way) + agg + uT, LB: [("ids", "gather")] * (not final) + agg}
            lag = {LA: 0, LB: 0}
            if norm:
                for c in NS_:
                    lanes[c] = LN("") + ([("scattered", "pool")] if final else [])
                    lag[c] = 1
                if not final:
                    for c in XS_:
                        lanes[c] = [("lnB", "pe"), ("xf", "act")] + ([("v", "dve")] if post and not lstm else [])
                        lag[c] = 2
                lanes[LNS] = ROOT
                lag[LNS] = 1
            if lstm:
                for c in TS_:
                    lanes[c] = LSTM + [("v", "dve")]
                    lag[c] = 2
            maker = TS_ if lstm else XS_ if norm else AB
            v_step = "v" if post else None if norm else "act"
            out_step = v_step or "xf"
            if msg:
                lanes[LM] = [("msg", "pe")] + ([("scaled", "dve")] if msg[1] is not None else []) + \
                    [("scan", "dve"), ("rowsT", "pe"), ("rows", "act")]
                lag[LM] = lag[maker[0]] + 1
            if dense is not None:
                lanes.update(DENSE)
            S = Steps(lane_sems, lane_base, lanes)
            LAST = max(lag.values())
            out_buf = OV[LB] if v_step else OX[LB]
            KG, KN, KM = K[0], {NA: K[1], NBL: K[2]}, K[3]
            KX = {XA: K[7], XB: K[7] if lstm else K[5]}
            KA = {LA: KG, LB: KG if dense is not None else K[4]}
            KT = {TA: KM, TB: KM} if dense is not None else {TA: K[5], TB: K[6]}
            fetch = {LA: [("end_ba", tab_b, G2, "g2")] * two_way,
                     LB: [("end_f", tab, G1, "g1")] * (not final) + [("end_bb", tab_b, G2, "g2")] * two_way}
            scale_row = {LA: C_D1A if 1 in (pre, post) else C_D3A, LB: C_D1B if 1 in (pre, post) else C_D3B}
            agg_free = {c: ("uR" if uT and c == LA else "scaled" if pre else "act" if weight else "z") for c in AB}
            scaler = {c: (maker[c] if post else c) for c in AB}
            scale_used = "v" if post else "scaled"

            def rounds(eng, body):
                for i in range(LAST):
                    body(i)
                with eng.Fori(LAST, NB) as i:
                    body(i)
                for i in range(NB, NB + LAST):
                    body(i)

            def on(i, c):
                return c in lanes and (not isinstance(i, int) or lag[c] <= i < NB + lag[c])

            def at(i, c):
                return i - lag[c] if lag[c] else i

            def dense_on(i):
                return dense is not None and (not isinstance(i, int) or i < NB)

            with nc.Block() as block:
                @block.gpsimd
                def _(pool):
                    def get(i):
                        for c in AB:
                            if fetch[c]:
                                gather(pool, S, c, i, i, "pre", fetch[c])

                    def put(i):
                        for c in AB:
                            nc.gpsimd.tensor_copy(OI[c][:], IX["out_a" if c == LA else "out_b"][:, bass.ds(i * Q, Q)]).then_inc(out_ids, 1)
                        pool.wait_ge(out_ids, i * 2 + 2)
                        pool.sem_inc(pool_passed, 1)
                        for c, n in zip(AB, NS_):
                            pool.wait_ge(*S.after("norm", n, i))
                            pool.sem_inc(pool_passed, 1)
                            for q in range(Q):
                                nc.gpsimd.indirect_dma_start(
                                    out=out, out_offset=bass.IndirectOffsetOnAxis(ap=OI[c][:, q:q + 1].bitcast(U32), axis=0),
                                    in_=R[n][:, q * D:(q + 1) * D], in_offset=None, bounds_check=N - 1, oob_is_err=False).then_inc(out_dma[c], 16)
                        for c, n in zip(AB, NS_):
                            pool.wait_ge(out_dma[c], i * (16 * Q) + 16 * Q)
                            pool.sem_inc(S.did("scattered", n), 1)
                    with pool.Fori(0, NB) as i:
                        put(i) if final else get(i)

                @block.sync
                def _(sp):
                    def load_start(i):
                        for c in AB:
                            if weight:
                                sp.wait_ge(*S.after("pre", c, i - 1))
                                sp.dma_start(LV[c][:], (st_v if v_from == "v" else st_x)[c, i]).then_inc(arr["v"][c].sem, 16)
                        sp.wait_ge(*S.after("pre", LA, i - 1))
                        sp.dma_start(as_rows(G1[LA]), rows_of(tab)[i]).then_inc(arr["rows"][LA].sem, 16)
                        for c in AB:
                            if norm:
                                sp.wait_ge(*S.after("z", c, i - 1))
                                sp.dma_start(LX[c][:], st_x[c, i]).then_inc(arr["x"][c].sem, 16)
                            if pre:
                                sp.wait_ge(*S.after("v" if post else "scaled", c, i - 1))
                                sp.dma_start(LS[c][:], bcast(scale_row[c], i)).then_inc(arr["s"][c].sem, 16)

                    def load_scale(n):
                        for c in AB:
                            sp.wait_ge(*S.after("v", maker[c], n - 1))
                            sp.dma_start(LS[c][:], bcast(scale_row[c], n)).then_inc(arr["s"][c].sem, 16)

                    def load_msg(n):
                        sp.wait_ge(*S.after("scan", LM, n - 1))
                        sp.dma_start(LT[LM][:], bcast(C_SAMED, n)).then_inc(arr["same"][LM].sem, 16)
                        if msg[1] is not None:
                            sp.dma_start(LS[LM][:], bcast(msg[1], n)).then_inc(arr["s"][LM].sem, 16)

                    late_scale = bool(post and not pre)

                    def loads(i):
                        if on(i, LA):
                            load_start(i)
                        if late_scale and on(i, maker[0]):
                            load_scale(at(i, maker[0]))
                        if msg and on(i, LM):
                            load_msg(at(i, LM))

                    def stores(i):
                        if rows_to and not norm and on(i, LA):
                            sp.wait_ge(*S.after("uR", LA, i))
                            sp.dma_start(rows_of(tab_u)[i], as_rows(R[LA])).then_inc(stored["r"][LA].sem, 16)
                        if norm and rows_to and on(i, NA):
                            n = at(i, NA)
                            sp.wait_ge(*S.after("norm", NA, n))
                            sp.dma_start(rows_of(tab_u)[n], as_rows(R[NA])).then_inc(stored["r"][LA].sem, 16)
                        if norm and not final and on(i, XA):
                            n = at(i, XA)
                            for c in AB:
                                sp.wait_ge(*S.after("xf", XS_[c], n))
                                sp.dma_start(st_x[c, n], OX[c][:]).then_inc(stored["x"][c].sem, 16)
                        if msg and on(i, LM):
                            sp.wait_ge(*S.after("rows", LM, at(i, LM)))
                            sp.dma_start(rows_of(msg[2])[at(i, LM)], as_rows(R[LM])).then_inc(stored["r"][LM].sem, 16)
                        if v_step and on(i, maker[0]):
                            n = at(i, maker[0])
                            for c in AB:
                                sp.wait_ge(*S.after(v_step, maker[c], n))
                                sp.dma_start(st_v[c, n], OV[c][:]).then_inc(stored["v"][c].sem, 16)

                    def dense_in(i):
                        if dense_on(i - 1) or i is NB:
                            n = i + dense
                            dense_load(sp, S, i, min(n, DB - 1) if isinstance(i, int) else n)

                    def dense_out(i):
                        if dense_on(i):
                            fill = isinstance(i, int) and i + dense < LAG
                            dense_store(sp, S, i, None if fill else i + (dense - LAG))

                    head = max(LAST, LAG if dense == 0 else 0)
                    loads(0)
                    if dense == 0:
                        dense_load(sp, S, 0, 0)
                    for i in range(head):
                        loads(i + 1)
                        dense_in(i + 1)
                        stores(i)
                        dense_out(i)
                    with sp.Fori(head, NB - 1) as i:
                        loads(i + 1)
                        dense_in(i + 1)
                        stores(i)
                        dense_out(i)
                    for i in range(NB - 1, NB + LAST):
                        if i + 1 < NB + LAST:
                            loads(i + 1)
                        if i == NB - 1 and dense is not None:
                            dense_load(sp, S, NB, min(NB + dense, DB - 1))
                        stores(i)
                        dense_out(i)
                    if rows_to:
                        sp.wait_ge(*stored["r"][LA].after(NB - 1))
                    for c in AB:
                        if norm and not final:
                            sp.wait_ge(*stored["x"][c].after(NB - 1))
                        if v_step:
                            sp.wait_ge(*stored["v"][c].after(NB - 1))
                    if msg:
                        sp.wait_ge(*stored["r"][LM].after(NB - 1))
                    if dense is not None:
                        sp.wait_ge(*stored["r"][D3].after(NB - 1))

                @block.tensor
                def _(pe):
                    def aggregate(i, c):
                        if c == LA:
                            pe.wait_ge(*arr["rows"][c].after(i))
                            pe.wait_ge(*S.after(agg_free[KA[LA] is KA[LB] and LB or LA], KA[LA] is KA[LB] and LB or LA, i - 1))
                        elif KA[LA] is KA[LB]:
                            pe.wait_ge(*S.after("scaled" if pre else "act" if weight else "z", LA, i))
                        else:
                            pe.wait_ge(*S.after(agg_free[c], c, i - 1))
                        for _, _, _, stream in fetch[c]:
                            pe.wait_ge(*arr[stream][c].after(i, Q))
                        rows = G1[c] if (c == LA or not final) else None
                        if weight:
                            if two_way:
                                pe.wait_ge(*S.after("rowsum", c, i))
                            pe.wait_ge(*arr["v"][c].after(i))
                            last = nc.tensor.matmul(KA[c][:], W[weight][:], LV[c][:], start=True, stop=rows is None)
                            if rows is not None:
                                for q in range(Q):
                                    last = nc.tensor.matmul(tile_cols(KA[c], q), tile_cols(rows, q), ident[:], start=False, stop=(q == Q - 1))
                        else:
                            last = transposes(KA[c], rows)
                        last.then_inc(S.did("pre", c), 1)

                    def body(i):
                        def dense_part(part):
                            if dense_on(i):
                                dense_pe(pe, S, i, part)

                        dense_part(0)
                        if norm and on(i, NA):
                            n = at(i, NA)
                            for k, c in enumerate(NS_):
                                pe.wait_ge(*S.after("z", k, n))
                                pe.wait_ge(*S.after("norm", c, n - 1))
                                to_rows(KN[c], Z[k]).then_inc(S.did("lnT", c), 1)

                        def features(k):
                            if norm and not final and on(i, XA):
                                n = at(i, XA)
                                pe.wait_ge(*S.after("norm", NS_[k], n))
                                if KX[XA] is KX[XB]:
                                    pe.wait_ge(*(S.after("xf", XA, n) if k else S.after("xf", XB, n - 1)))
                                else:
                                    pe.wait_ge(*S.after("xf", XS_[k], n - 1))
                                transposes(KX[XS_[k]], R[NS_[k]]).then_inc(S.did("lnB", XS_[k]), 1)
                        features(0)
                        if msg and on(i, LM):
                            n = at(i, LM)
                            pe.wait_ge(*S.after(out_step, maker[1], n))
                            pe.wait_ge(*S.after("rows", LM, n - 1))
                            nc.tensor.matmul(KM[:], W[msg[0]][:], out_buf[:], start=True, stop=True).then_inc(S.did("msg", LM), 1)
                        dense_part(1)
                        if on(i, LA):
                            aggregate(i, LA)
                        features(1)
                        dense_part(2)
                        if msg and on(i, LM):
                            pe.wait_ge(*S.after("scan", LM, at(i, LM)))
                            to_rows(KM, ZM[0]).then_inc(S.did("rowsT", LM), 1)
                        dense_part(3)
                        if on(i, LA):
                            aggregate(i, LB)
                        gates = lstm and on(i, TA)
                        m = at(i, TA) if gates else None
                        shared = KT[TA] is KT[TB]

                        def first_gate(k):
                            c = TS_[k]
                            if shared:
                                if k == 0:
                                    pe.wait_ge(*S.after("rows", LM, m - 1))
                                else:
                                    pe.wait_ge(*S.after("sig_o", TA, m))
                            else:
                                pe.wait_ge(*S.after("sig_o", c, m - 1))
                            pe.wait_ge(*S.after("xf", XS_[k], m))
                            product(pe, S, c, m, "gate_i", "Wi", KT[c], OX[k], [], BLK)

                        dense_part(4)
                        if gates:
                            first_gate(0)
                            if not shared:
                                first_gate(1)
                        dense_part(5)
                        if gates:
                            product(pe, S, TA, m, "gate_g", "Wg", KT[TA], OX[LA], ["sig_i"], BLK)
                            if not shared:
                                product(pe, S, TB, m, "gate_g", "Wg", KT[TB], OX[LB], ["sig_i"], BLK)
                        dense_part(6)
                        if gates:
                            product(pe, S, TA, m, "gate_o", "Wo", KT[TA], OX[LA], ["tanh_g"], BLK)
                            if not shared:
                                product(pe, S, TB, m, "gate_o", "Wo", KT[TB], OX[LB], ["tanh_g"], BLK)
                            else:
                                first_gate(1)
                        dense_part(7)
                        if gates and shared:
                            product(pe, S, TB, m, "gate_g", "Wg", KT[TB], OX[LB], ["sig_i"], BLK)
                            product(pe, S, TB, m, "gate_o", "Wo", KT[TB], OX[LB], ["tanh_g"], BLK)
                        if uT and on(i, LA):
                            pe.wait_ge(*S.after("act", LA, i))
                            if KA[LA] is KA[LB]:
                                pe.wait_ge(*S.after("scaled" if pre else "act", LB, i))
                            to_rows(KA[LA], OV[LA]).then_inc(S.did("uT", LA), 1)
                    rounds(pe, body)

                @block.scalar
                def _(act):
                    def activate(i, c):
                        if v_step == "act":
                            act.wait_ge(*stored["v"][c].after(i - 1))
                            if msg and c == LB:
                                act.wait_ge(*S.after("msg", LM, i - 1))
                        else:
                            act.wait_ge(*S.after("z" if norm else "v", c, i - 1))
                        function(act, S, c, i, "act", ACT.Relu if relu else ACT.Identity, bias, B1[c] if pre else KA[c],
                                 OV[c] if v_step == "act" else B2[c], ["scaled" if pre else "pre"], BLK)

                    def body(i):
                        def dense_part(part):
                            if dense_on(i):
                                dense_act(act, S, i, part)

                        gates = lstm and on(i, TA)
                        m = at(i, TA) if gates else None

                        def gate_acts(k, which):
                            c = TS_[k]
                            if which == 0:
                                function(act, S, c, m, "sig_i", ACT.Sigmoid, "bi", KT[c], BT[c], ["gate_i"], BLK)
                            if which == 1:
                                function(act, S, c, m, "tanh_g", ACT.Tanh, "bg", KT[c], CT[c], ["gate_g"], BLK)
                            if which == 2:
                                function(act, S, c, m, "sig_o", ACT.Sigmoid, "bo", KT[c], SO[c], ["gate_o"], BLK)
                                function(act, S, c, m, "tanh_c", ACT.Tanh, None, BT[c], CT[c], ["cell"], BLK)

                        shared = KT[TA] is KT[TB]

                        def features(k):
                            if norm and not final and on(i, XA):
                                n, c = at(i, XA), XS_[k]
                                act.wait_ge(*stored["x"][k].after(n - 1))
                                if lstm:
                                    act.wait_ge(*S.after("gate_o", TS_[k], n - 1))
                                elif post:
                                    act.wait_ge(*S.after("v", c, n - 1))
                                if msg and k == 1 and not v_step:
                                    act.wait_ge(*S.after("msg", LM, n - 1))
                                function(act, S, c, n, "xf", ACT.Copy, None, KX[c], OX[k], ["lnB"], BLK)

                        def norms():
                            if norm and on(i, NA):
                                n = at(i, NA)
                                for k, c in enumerate(NS_):
                                    if rows_to and c == NA:
                                        act.wait_ge(*stored["r"][LA].after(n - 1))
                                    act.wait_ge(*(S.after("scattered", c, n - 1) if final else S.after("lnB", XS_[k], n - 1)))
                                    ln_norm(act, S, c, n, KN[c], R[c], P)
                        dense_part(0)
                        features(0)
                        dense_part(1)
                        if weight and on(i, LA):
                            activate(i, LA)
                        features(1)
                        if not lstm:
                            norms()
                        dense_part(2)
                        if msg and on(i, LM):
                            act.wait_ge(*stored["r"][LM].after(at(i, LM) - 1))
                            function(act, S, LM, at(i, LM), "rows", ACT.Copy, None, KM, R[LM], ["rowsT"], BLK)
                        dense_part(3)
                        if weight and on(i, LA):
                            activate(i, LB)
                        dense_part(4)
                        if gates:
                            gate_acts(0, 0)
                            if not shared:
                                gate_acts(1, 0)
                        dense_part(5)
                        if gates:
                            gate_acts(0, 1)
                            if not shared:
                                gate_acts(1, 1)
                        if lstm:
                            norms()
                        dense_part(6)
                        if gates:
                            gate_acts(0, 2)
                            if shared:
                                gate_acts(1, 0)
                            else:
                                gate_acts(1, 2)
                        dense_part(7)
                        if gates and shared:
                            gate_acts(1, 1)
                            gate_acts(1, 2)
                        if uT and on(i, LA):
                            act.wait_ge(*stored["r"][LA].after(i - 1))
                            function(act, S, LA, i, "uR", ACT.Copy, None, KA[LA], R[LA], ["uT"], BLK)
                    rounds(act, body)

                @block.vector
                def _(dve):
                    def add_ways(i, c):
                        if c == LA:
                            dve.wait_ge(*arr["rows"][c].after(i))
                        for _, _, _, stream in fetch[c]:
                            dve.wait_ge(*arr[stream][c].after(i, Q))
                        nc.vector.tensor_tensor(G1[c][:], G1[c][:], G2[c][:], ALU.add).then_inc(S.did("rowsum", c), 1)

                    def scale(i, c):
                        dve.wait_ge(*S.after("pre", c, i))
                        dve.wait_ge(*arr["s"][c].after(i))
                        dve.wait_ge(*S.after("act", c, i - 1))
                        nc.vector.tensor_tensor(B1[c][:], KA[c][:], LS[c][:], ALU.mult).then_inc(S.did("scaled", c), 1)

                    def add_residual(i, c):
                        dve.wait_ge(*S.after("act" if weight else "pre", c, i))
                        dve.wait_ge(*arr["x"][c].after(i))
                        if True:
                            dve.wait_ge(*S.after("lnT", NS_[c], i - 1))
                        nc.vector.tensor_tensor(Z[c][:], B2[c][:] if weight else KA[c][:], LX[c][:], ALU.add).then_inc(S.did("z", c), 1)

                    def keep(i):
                        if post and on(i, maker[0]):
                            n = at(i, maker[0])
                            for k, c in enumerate(maker):
                                dve.wait_ge(*S.after("h" if lstm else "xf" if norm else "act", c, n))
                                dve.wait_ge(*stored["v"][k].after(n - 1))
                                if msg and k == 1:
                                    dve.wait_ge(*S.after("msg", LM, n - 1))
                                dve.wait_ge(*arr["s"][k].after(n))
                                src = BT[c] if lstm else OX[k] if norm else B2[k]
                                nc.vector.tensor_tensor(OV[k][:], src[:], LS[k][:], ALU.mult).then_inc(S.did("v", c), 1)

                    def body(i):
                        def dense_part(part):
                            if dense_on(i):
                                dense_dve(dve, S, i, part)

                        gates = lstm and on(i, TA)
                        m = at(i, TA) if gates else None
                        shared = KT[TA] is KT[TB]
                        def messages():
                            if msg and on(i, LM):
                                n = at(i, LM)
                                dve.wait_ge(*S.after("msg", LM, n))
                                src = KM
                                if msg[1] is not None:
                                    dve.wait_ge(*arr["s"][LM].after(n))
                                    nc.vector.tensor_tensor(B1[LM][:], KM[:], LS[LM][:], ALU.mult).then_inc(S.did("scaled", LM), 1)
                                    dve.wait_ge(*S.after("scaled", LM, n))
                                    src = B1[LM]
                                dve.wait_ge(*arr["same"][LM].after(n))
                                dve.wait_ge(*S.after("rowsT", LM, n - 1))
                                nc.vector.tensor_tensor_scan(ZM[0][:], LT[LM][:], src[:], ZM[1][:, BLK - 1:BLK], ALU.mult, ALU.add).then_inc(S.did("scan", LM), 1)
                                dve.wait_ge(*S.after("scan", LM, n))
                                nc.vector.tensor_copy(ZM[1][:, BLK - 1:BLK], ZM[0][:, BLK - 1:BLK]).then_inc(carried, 1)
                                dve.wait_ge(carried, n + (carries[0] + 1))
                        if not norm:
                            messages()
                        if two_way and on(i, LA):
                            add_ways(i, LA)
                        dense_part(0)
                        if norm and on(i, NA):
                            n = at(i, NA)
                            for c in NS_:
                                dve.wait_ge(*S.after("norm", c, n - 1))
                            ln_group(dve, S, LNS, [(c, n) for c in NS_], KN, P)
                        if norm:
                            messages()
                        dense_part(1)
                        if on(i, LA):
                            if weight and pre:
                                scale(i, LA)
                            if norm:
                                add_residual(i, LA)
                        dense_part(2)
                        if two_way and on(i, LA):
                            add_ways(i, LB)
                        if on(i, LA):
                            if weight and pre:
                                scale(i, LB)
                            if norm:
                                add_residual(i, LB)
                        dense_part(3)
                        dense_part(4)
                        dense_part(5)
                        if gates:
                            cell(dve, S, TA, m, BT[TA], CT[TA], BLK)
                            if not shared:
                                cell(dve, S, TB, m, BT[TB], CT[TB], BLK)
                        dense_part(6)
                        if gates:
                            hidden(dve, S, TA, m, CT[TA], BT[TA], BLK)
                            if not shared:
                                hidden(dve, S, TB, m, CT[TB], BT[TB], BLK)
                        dense_part(7)
                        if gates and shared:
                            cell(dve, S, TB, m, BT[TB], CT[TB], BLK)
                            hidden(dve, S, TB, m, CT[TB], BT[TB], BLK)
                        keep(i)

                    if msg:
                        start_sums(dve)
                    rounds(dve, body)
            S.close({c: NB for c in lanes})
            for c in AB:
                if weight:
                    arr["v"][c].close(NB)
                if norm:
                    arr["x"][c].close(NB)
                if pre or post:
                    arr["s"][c].close(NB)
                for _, _, _, stream in fetch[c]:
                    arr[stream][c].close(NB, Q)
                if norm and not final:
                    stored["x"][c].close(NB)
                if v_step:
                    stored["v"][c].close(NB)
            arr["rows"][LA].close(NB)
            if rows_to:
                stored["r"][LA].close(NB)
            if msg:
                carries[0] += NB
                arr["same"][LM].close(NB)
                if msg[1] is not None:
                    arr["s"][LM].close(NB)
                stored["r"][LM].close(NB)
            if dense is not None:
                arr["x"][D0].close(NB)
                stored["r"][D3].close(NB)



        NS = NB
        PLAN = [
            lambda: edge_stage(tab_f0),
            lambda: slot_stage(tab_f0, lstm=True, post=1, msg=("L1_W1", None, tab_f1)),
            lambda: slot_stage(tab_f1, "L1_W1", "L1_b1", pre=1, post=1, msg=("L1_W23", None, tab_f0)),
            lambda: slot_stage(tab_f0, "L1_W23", "L1_b23", pre=1, resid=True, rows_to=True, msg=("W0f", C_INVOUT, tab_f1)),
            lambda: back_stage("W0b"),
            lambda: slot_stage(tab_f1, "W0x", "L2_b0", two_way=True, v_from="x", rows_to=True, msg=("W1f", C_INVOUT, tab_f0), dense=2 * NS),
            lambda: back_stage("W1b"),
            lambda: slot_stage(tab_f0, "W1x", "L2_b1", two_way=True, rows_to=True, msg=("W2f", C_INVOUT, tab_f1), dense=3 * NS),
            lambda: dense_drain(4 * NS),
            lambda: back_stage("W2b"),
            lambda: slot_stage(tab_f1, "W2x", "L2_b2", relu=False, two_way=True, resid=True, post=3, msg=("L3_W1", C_W, tab_f0)),
            lambda: slot_stage(tab_f0, "L3_W1", "L3_b1", pre=3, post=3, msg=("L3_W2", C_W, tab_f1)),
            lambda: slot_stage(tab_f1, "L3_W2", "L3_b2", pre=3, resid=True, final=True),
        ]
        for stage in PLAN[:upto]:
            stage()

def kernel(**inputs):
    import concourse.bacc as bacc
    from concourse.bass_utils import run_bass_kernel_spmd

    nc = bacc.Bacc("TRN2", target_bir_lowering=False, num_devices=1)
    arrays, aps = {}, {}
    for name, x in inputs.items():
        x = np.ascontiguousarray(x)
        arrays["in_" + name] = x
        aps[name] = nc.dram_tensor("in_" + name, x.shape, mybir.dt.from_np(x.dtype), kind="ExternalInput").ap()
    out = nc.dram_tensor("out", (N, D), F32, kind="ExternalOutput").ap()
    build(nc, aps, out)
    r = run_bass_kernel_spmd(nc, [arrays], core_ids=[0])
    return r.results[0]["out"]
```

```python
from contextlib import ExitStack

import numpy as np

import concourse.bass as bass
import concourse.mybir as mybir

F32 = mybir.dt.float32
BF16 = mybir.dt.bfloat16
I32 = mybir.dt.int32
U32 = mybir.dt.uint32
ALU = mybir.AluOpType
ACT = mybir.ActivationFunctionType
AX = mybir.AxisListType.X

P = 128
N = 50000
E = 12500
D = 128
BLK = 512
Q = BLK // P
NB = 25
EP = NB * BLK
T = EP // P
HI, LO = 98, 512
PAD = HI * LO - 1
DP = 125
DB = N // (DP * Q)
LA, LB, NA, NBL, TA, TB, LM, D0, DE, D1, D2, D3, LNS, LNDA, LNDB, XA, XB = range(17)
EPS = 1e-5
PRIME = 64
SKIP = 60000
RANK_TILES = 4
TURNS_BACK = 3
LAG = 4
DENSE_RANK, DENSE_BACK = T // RANK_TILES, NB // 2 // TURNS_BACK
DENSE_RECORDS = DB + LAG - DENSE_RANK - 3 * DENSE_BACK - 2 * NB
F_FULL, F_REST = E // P, E % P

N_ENDD, N_ENDS, N_DINV1, N_DINV3, N_INVOUT, N_INVIN, N_CNTD, NF = 0, 1, 2, 3, 4, 5, 6, 8
(R_DST, R_SRC, R_W, R_DINV1A, R_DINV3A, R_INVIN, R_ENDD_DST, R_ENDS_DST,
 R_DINV1B, R_DINV3B, R_INVOUT, R_ENDD_SRC, R_ENDS_SRC, R_CNTD_SRC, R_POSS) = range(15)
RF = 16
(C_SAMED, C_W, C_D1A, C_D1B, C_D3A, C_D3B, C_INVOUT, C_SAMES, C_INVIN) = range(9)
CF = 9


class Steps:

    def __init__(self, sems, base, lanes):
        self.sems, self.base = sems, base
        self.order, self.where = {}, {}
        for c, steps in lanes.items():
            for name, eng in steps:
                names = self.order.setdefault((eng, c), [])
                self.where[name, c] = (eng, len(names))
                names.append(name)
        self.next = {k: 0 for k in self.order}

    def after(self, name, c, i):
        eng, k = self.where[name, c]
        return self.sems[eng][c], i * len(self.order[eng, c]) + (self.base[eng][c] + k + 1)

    def did(self, name, c):
        eng, k = self.where[name, c]
        assert self.next[eng, c] % len(self.order[eng, c]) == k, (name, c)
        self.next[eng, c] += 1
        return self.sems[eng][c]

    def close(self, rounds):
        for (eng, c), names in self.order.items():
            self.base[eng][c] += rounds[c] * len(names)


class Arrivals:

    def __init__(self, sem, base=0):
        self.sem, self.base = sem, base

    def after(self, i, dmas=1):
        return self.sem, i * (16 * dmas) + (self.base + 16 * dmas)

    def close(self, n, dmas=1):
        self.base += 16 * dmas * n


class PairArrivals:

    def __init__(self, sems):
        self.sems, self.base = sems, [0, 0]

    def after(self, i, place, dmas=1):
        return self.sems[place], i * (8 * dmas) + (self.base[place] + (16 - 8 * place) * dmas)

    def close(self, n, dmas=1):
        for place in range(2):
            self.base[place] += 16 * dmas * ((n + 1 - place) // 2)


def build(nc, a, out):
    ctx = ExitStack()
    with ctx:
        def sb(name, shape, dt=F32):
            return ctx.enter_context(nc.sbuf_tensor(name, shape, dt))

        def sem(name):
            return ctx.enter_context(nc.semaphore(name))

        def dram(name, shape, dt=F32):
            return nc.dram_tensor(name, shape, dt).ap()

        node_tab = dram("node_tab", [HI * LO, NF])
        rec_d = dram("rec_d", [EP, RF])
        rec_s = dram("rec_s", [EP, RF])
        key_d = dram("key_d", [EP + P])
        key_s = dram("key_s", [EP + P])
        scal = dram("scal", [CF, NB, BLK])
        st_x = dram("st_x", [2, NB, P, BLK])
        st_v = dram("st_v", [2, NB, P, BLK])
        tab_f0, tab_f1 = dram("tab_f0", [EP + P, D]), dram("tab_f1", [EP + P, D])
        tab_b = dram("tab_b", [EP + P, D])
        no_block = dram("no_block", [DP, Q * D])
        tab_u = dram("tab_u", [EP, D])

        def rows_of(tab):
            return tab[0:EP, :].rearrange("(j q p) f -> j p q f", q=Q, p=P)

        pidx = sb("pidx", [P, 1])
        iota_i = sb("iota_i", [P, LO], I32)
        iot = sb("iot", [P, LO])
        ident = sb("ident", [P, P])
        identb = sb("identb", [P, P], BF16)
        before = sb("before", [P, P])
        above = sb("above", [P, P])
        ones = sb("ones", [P, LO])
        zero = sb("zero", [P, LO])
        zerob = sb("zerob", [P, LO], BF16)
        minus1 = sb("minus1", [1, P])
        wnames = ["L0_W1", "L0_W2a", "L0_W2b", "L0_W3", "Wi", "Wg", "Wo", "L1_W1", "L1_W23",
                  "W0x", "W0f", "W0b", "W1x", "W1f", "W1b", "W2x", "W2f", "W2b", "L3_W1", "L3_W2"]
        W = {n: sb("w_" + n, [P, P]) for n in wnames}
        bnames = ["L0_b1", "L0_b2", "L0_b3", "bi", "bg", "bo", "L1_b1", "L1_b23",
                  "L2_b0", "L2_b1", "L2_b2", "L3_b1", "L3_b2"]
        B = {n: sb("b_" + n, [P, 1]) for n in bnames}
        IX = {n: sb("ix_" + n, [P, T], I32) for n in ["xa", "xb", "end_f", "end_bb", "end_ba", "dst_in_s", "out_a", "out_b"]}

        K = [ctx.enter_context(nc.psum_tensor(f"bank{k}", [P, BLK], F32)) for k in range(8)]

        AB = (LA, LB)
        names_of = {LA: "side_a", LB: "side_b", NA: "norm_a", NBL: "norm_b", TA: "lstm_a", TB: "lstm_b", LM: "messages",
                    D0: "dense_lstm", DE: "dense_gcn", D1: "dense_block2", D2: "dense_block3", D3: "dense_last",
                    LNS: "slot_rstd", LNDA: "dense_rstd_a", LNDB: "dense_rstd_b",
                    XA: "features_a", XB: "features_b"}
        uses = {"pe": (LA, LB, NA, NBL, XA, XB, TA, TB, LM, D0, DE, D1, D2, D3), "act": (LA, LB, NA, NBL, XA, XB, TA, TB, LM, D0, DE, D1, D2, D3),
                "dve": tuple(range(17)), "pool": (NA, NBL), "gather": (LA, LB)}
        lane_sems = {e: {c: sem(f"{e}_{names_of[c]}") for c in cs} for e, cs in uses.items()}
        lane_base = {e: {c: PRIME for c in cs} for e, cs in uses.items()}
        arr = {n: {c: Arrivals(sem(f"{n}_arrived_{names_of[c]}")) for c in cs}
               for n, cs in {"x": (D0,), "s": AB, "g1": AB, "g2": AB, "same": AB}.items()}
        pairs = {n: {c: PairArrivals([sem(f"{n}_in_place{b}_{names_of[c]}") for b in range(2)]) for c in cs}
                 for n, cs in {"v": AB, "x": AB, "s": (LA, LB, LM), "g1": (LB,), "g2": AB, "same": (LM,), "rows": (LA,)}.items()}
        stored = {n: {c: Arrivals(sem(f"{n}_stored_{names_of[c]}")) for c in cs}
                  for n, cs in {"v": (LA, LB), "x": (LA, LB), "r": (LA, LB, LM, D3)}.items()}
        setup_dma = Arrivals(sem("setup_dma"))
        pool_dma = Arrivals(sem("pool_dma"))
        s_pool, s_dve, s_pe, s_act = sem("pool_setup"), sem("dve_setup"), sem("pe_setup"), sem("act_setup")
        pool_passed = sem("pool_passed")
        sp_passed = sem("sp_passed")
        dve_passed = sem("dve_passed")
        sums_cleared, out_ids, carried = sem("sums_cleared"), sem("out_ids_ready"), sem("carried")
        out_dma = [PairArrivals([sem(f"out_rows_written{b}_{names_of[c]}") for b in range(2)]) for c in AB]
        scans, carries = [0], [0]
        def per(cs, name, shape=(P, BLK), dt=F32):
            return {c: sb(f"{name}_{names_of[c]}", list(shape), dt) for c in cs}

        GI = [[per(AB, f"row_ids{m}_{b}", (P, Q), I32) for m in range(2)] for b in range(2)]
        OI = [per(AB, f"out_ids{b}", (P, Q), I32) for b in range(2)]
        B1 = per((D0, DE, D1, D2), "b1")
        B2 = per((D0, D1, D2), "b2")
        SO = per((D0,), "sig_o")
        Z = per((DE, D1, D2), "z")
        R = per((D0, D1, D2, D3), "out_rows")
        DX = per((D0, D1, D2), "dense_x")
        XR = sb("dense_rows", [P, BLK])
        H = sb("dense_h", [P, BLK])
        NORMED = (NA, NBL, D0, D1, D2, D3)
        ST = per(NORMED, "stats", (P, Q, 6))
        MV = per(NORMED, "mean_var", (P, Q, 2))
        NM = per(NORMED, "neg_mean", (P, Q))
        GROUP = {LNS: (NA, NBL), LNDA: (D0, D2), LNDB: (D1, D3)}
        VE = {g: sb(f"var_eps_{names_of[g]}", [P, Q * len(cs)]) for g, cs in GROUP.items()}
        RI = {g: sb(f"root_bits_{names_of[g]}", [P, Q * len(cs)], I32) for g, cs in GROUP.items()}
        RT = {g: sb(f"root_tmp_{names_of[g]}", [P, Q * len(cs)]) for g, cs in GROUP.items()}
        RR = {g: sb(f"root_{names_of[g]}", [P, Q * len(cs)]) for g, cs in GROUP.items()}
        WD = DP * Q

        def in_group(c):
            g = next(g for g, cs in GROUP.items() if c in cs)
            return g, GROUP[g].index(c) * Q

        def tile_cols(buf, q, w=P):
            return buf[:, q * w:(q + 1) * w]

        def transposes(dst, src, rows=P):
            for q in range(Q):
                last = nc.tensor.transpose(dst[:, q * rows:(q + 1) * rows], src[0:rows, q * D:(q + 1) * D], ident[0:rows, 0:rows])
            return last

        def to_rows(dst, src, rows=P):
            for q in range(Q):
                last = nc.tensor.transpose(dst[0:rows, q * D:(q + 1) * D], src[:, q * rows:(q + 1) * rows], ident[:])
            return last

        def bcast(c, j):
            return scal[c, j].partition_broadcast(P)

        def as_rows(buf):
            return buf[:].rearrange("p (q f) -> p q f", q=Q)

        LN_ROWS = [("stats", "dve"), ("aggr", "dve"), ("eps", "dve"), ("neg", "dve"), ("norm", "act")]
        LN = [("lnT", "pe")] + LN_ROWS
        ROOT = [(f"root{k}", "dve") for k in range(11)]

        def ln_stats(dve, S, c, i, src, pp):
            if ("lnT", c) in S.where:
                dve.wait_ge(*S.after("lnT", c, i))
            for q in range(Q):
                last = nc.vector.bn_stats(ST[c][0:pp, q, :], src[0:pp, q * D:(q + 1) * D])
            last.then_inc(S.did("stats", c), 1)

        def ln_aggr(dve, S, c, i, pp):
            dve.wait_ge(*S.after("stats", c, i))
            dve.sem_inc(dve_passed, 1)
            for q in range(Q):
                last = nc.vector.bn_aggr(MV[c][0:pp, q, :], ST[c][0:pp, q, :])
            last.then_inc(S.did("aggr", c), 1)

        def ln_eps(dve, S, c, i, pp):
            g, o = in_group(c)
            dve.wait_ge(*S.after("aggr", c, i))
            nc.vector.tensor_scalar(VE[g][0:pp, o:o + Q], MV[c][0:pp, :, 1], EPS, None, ALU.add).then_inc(S.did("eps", c), 1)

        def ln_root(dve, S, g, i, pp, ready):
            v, r, t, b = VE[g][0:pp, :], RR[g][0:pp, :], RT[g][0:pp, :], RI[g][0:pp, :]
            for c in ready:
                dve.wait_ge(*S.after("eps", c, i))
            nc.vector.tensor_scalar(b, VE[g][0:pp, :].bitcast(I32), 1, None, ALU.arith_shift_right).then_inc(S.did("root0", g), 1)
            dve.wait_ge(*S.after("root0", g, i))
            nc.vector.tensor_scalar(RR[g][0:pp, :].bitcast(I32), b, -1.0, float(0x5F3759DF), ALU.mult, ALU.add).then_inc(S.did("root1", g), 1)
            for n in range(3):
                dve.wait_ge(*S.after(f"root{3 * n + 1}", g, i))
                nc.vector.scalar_tensor_tensor(t, r, -0.5, r, ALU.mult, ALU.mult).then_inc(S.did(f"root{3 * n + 2}", g), 1)
                dve.wait_ge(*S.after(f"root{3 * n + 2}", g, i))
                nc.vector.tensor_tensor(t, t, v, ALU.mult).then_inc(S.did(f"root{3 * n + 3}", g), 1)
                dve.wait_ge(*S.after(f"root{3 * n + 3}", g, i))
                nc.vector.scalar_tensor_tensor(r, t, 1.5, r, ALU.add, ALU.mult).then_inc(S.did(f"root{3 * n + 4}", g), 1)
            dve.wait_ge(*S.after("root10", g, i))

        def ln_neg(dve, S, c, i, pp):
            g, o = in_group(c)
            nc.vector.scalar_tensor_tensor(NM[c][0:pp, :], MV[c][0:pp, :, 0], -1.0, RR[g][0:pp, o:o + Q], ALU.mult, ALU.mult).then_inc(S.did("neg", c), 1)

        def ln_norm(act, S, c, i, src, dst, pp):
            g, o = in_group(c)
            act.wait_ge(*S.after("neg", c, i))
            for q in range(Q):
                last = nc.scalar.activation(dst[0:pp, q * D:(q + 1) * D], src[0:pp, q * D:(q + 1) * D], ACT.Identity,
                                            bias=NM[c][0:pp, q:q + 1], scale=RR[g][0:pp, o + q:o + q + 1])
            last.then_inc(S.did("norm", c), 1)

        def ln_group(dve, S, g, lanes_i, rows, pp):
            ln_sums(dve, S, g, lanes_i, rows, pp)
            ln_roots(dve, S, g, lanes_i, pp)

        def ln_sums(dve, S, g, lanes_i, rows, pp):
            for c, i in lanes_i:
                ln_stats(dve, S, c, i, rows[c], pp)
            for c, i in lanes_i:
                ln_aggr(dve, S, c, i, pp)
            for c, i in lanes_i:
                ln_eps(dve, S, c, i, pp)

        def ln_roots(dve, S, g, lanes_i, pp):
            n = lanes_i[0][1]
            ln_root(dve, S, g, n, pp, [c for c, _ in lanes_i])
            for c, i in lanes_i:
                ln_neg(dve, S, c, i, pp)

        LSTM = [("gate_i", "pe"), ("sig_i", "act"), ("gate_g", "pe"), ("tanh_g", "act"), ("cell", "dve"),
                ("gate_o", "pe"), ("sig_o", "act"), ("tanh_c", "act"), ("h", "dve")]

        def product(pe, S, c, i, name, weight, bank, src, before_, w):
            for b in before_:
                pe.wait_ge(*S.after(b, c, i))
            nc.tensor.matmul(bank[:, 0:w], W[weight][:], src[:, 0:w], start=True, stop=True).then_inc(S.did(name, c), 1)

        def function(act, S, c, i, name, f, bias, src, dst, before_, w):
            for b in before_:
                act.wait_ge(*S.after(b, c, i))
            if bias is None:
                ins = nc.scalar.activation(dst[:, 0:w], src[:, 0:w], f)
            else:
                ins = nc.scalar.activation(dst[:, 0:w], src[:, 0:w], f, bias=B[bias][:])
            ins.then_inc(S.did(name, c), 1)

        def cell(dve, S, c, i, b, t, w):
            dve.wait_ge(*S.after("tanh_g", c, i))
            nc.vector.tensor_tensor(b[:, 0:w], b[:, 0:w], t[:, 0:w], ALU.mult).then_inc(S.did("cell", c), 1)

        def hidden(dve, S, c, i, t, dst, w):
            dve.wait_ge(*S.after("tanh_c", c, i))
            nc.vector.tensor_tensor(dst[:, 0:w], t[:, 0:w], SO[c][:, 0:w], ALU.mult).then_inc(S.did("h", c), 1)

        def gather(pool, S, c, i, j, free, streams, b=0, ahead=1):
            pool.wait_ge(*S.after(free, c, i - ahead))
            pool.sem_inc(pool_passed, 1)
            for m, (lst, tab, dst, stream) in enumerate(streams):
                last = nc.gpsimd.tensor_copy(GI[b][m][c][:], IX[lst][:, bass.ds(j * Q, Q)])
            last.then_inc(S.did("ids", c), 1)
            pool.wait_ge(*S.after("ids", c, i))
            pool.sem_inc(pool_passed, 1)
            for m, (lst, tab, dst, stream) in enumerate(streams):
                for q in range(Q):
                    nc.gpsimd.indirect_dma_start(out=dst[:, q * D:(q + 1) * D], out_offset=None, in_=tab,
                                                 in_offset=bass.IndirectOffsetOnAxis(ap=GI[b][m][c][:, q:q + 1].bitcast(U32), axis=0),
                                                 bounds_check=tab.shape[0] - 1, oob_is_err=False).then_inc(stream, 16)

        def in_pairs(eng, start, stop, body):
            with eng.Fori(0, (stop - start) // 2) as r:
                for u in range(2):
                    body(r * 2 + (start + u), (start + u) % 2)
            if (stop - start) % 2:
                body(stop - 1, (stop - 1) % 2)

        PAIRS = NB // 2
        TURNS = {LA: NB - PAIRS, LB: PAIRS}

        def in_turns(eng, body):
            with eng.Fori(0, PAIRS) as i:
                body(i, (LA, LB))
            body(PAIRS, (LA,))

        def loads_and_stores(sp, load, store, finish):
            load(0, (LA, LB))
            with sp.Fori(0, PAIRS - 1) as i:
                load(i + 1, (LA, LB))
                store(i, (LA, LB))
            load(PAIRS, (LA,))
            store(PAIRS - 1, (LA, LB))
            store(PAIRS, (LA,))
            finish()

        def start_sums(dve):
            for m in range(2):
                last = nc.vector.memset(ZM[m][:, BLK - 1:BLK], 0.0)
            last.then_inc(sums_cleared, 1)
            scans[0] += 1
            dve.wait_ge(sums_cleared, scans[0])

        DENSE = {D0: LN_ROWS + [("lnB", "pe"), ("xf", "act")] + LSTM,
                 DE: [("r1", "pe"), ("ra1", "act"), ("y", "pe"), ("ya", "act"), ("z", "dve")],
                 D1: [("u0", "pe"), ("ua0", "act"), ("u1", "pe"), ("ua1", "act"), ("u2", "pe"), ("z", "dve")] + LN + [("lnB", "pe"), ("xf", "act")],
                 D2: LN + [("lnB", "pe"), ("xf", "act"), ("v1", "pe"), ("va1", "act"), ("v2", "pe"), ("va2", "act"), ("z", "dve")],
                 D3: LN, LNDA: ROOT, LNDB: ROOT}
        x_in = a["x"].rearrange("(j p q) f -> j p (q f)", p=DP, q=Q)
        y_out = out.rearrange("(j p q) f -> j p (q f)", p=DP, q=Q)
        KD = {D0: K[4], DE: K[5], D3: K[5], D1: K[6], D2: K[7]}
        zin = {D1: Z[DE], D2: Z[D1], D3: Z[D2]}

        def dense_pe(pe, S, i, part):
            if part == 0:
                pe.wait_ge(*S.after("z", D1, i - 1))
                pe.wait_ge(*S.after("va2", D2, i - 1))
                to_rows(KD[D2], zin[D2], DP).then_inc(S.did("lnT", D2), 1)
                pe.wait_ge(*S.after("xf", D1, i - 1))
                nc.tensor.matmul(KD[D1][:, 0:WD], W["W0x"][:], DX[D1][:, 0:WD], start=True, stop=True).then_inc(S.did("u0", D1), 1)
                pe.wait_ge(*S.after("h", D0, i - 1))
                pe.wait_ge(*S.after("norm", D3, i - 1))
                nc.tensor.matmul(KD[DE][:, 0:WD], W["L1_W1"][:], H[:, 0:WD], start=True, stop=True).then_inc(S.did("r1", DE), 1)
            if part == 1:
                product(pe, S, D1, i, "u1", "W1x", KD[D1], B1[D1], ["ua0"], WD)
                product(pe, S, DE, i, "y", "L1_W23", KD[DE], B1[DE], ["ra1"], WD)
                product(pe, S, D1, i, "u2", "W2x", KD[D1], B2[D1], ["ua1"], WD)
            if part == 2:
                pe.wait_ge(*S.after("z", D1, i))
                pe.wait_ge(*S.after("z", DE, i))
                to_rows(KD[D1], zin[D1], DP).then_inc(S.did("lnT", D1), 1)
                pe.wait_ge(*S.after("z", D2, i - 1))
                to_rows(KD[D3], zin[D3], DP).then_inc(S.did("lnT", D3), 1)
            if part == 3:
                pe.wait_ge(*S.after("norm", D0, i))
                pe.wait_ge(*S.after("sig_o", D0, i - 1))
                transposes(KD[D0], R[D0], DP).then_inc(S.did("lnB", D0), 1)
                pe.wait_ge(*S.after("norm", D2, i))
                transposes(KD[D2], R[D2], DP).then_inc(S.did("lnB", D2), 1)
            if part == 4:
                product(pe, S, D0, i, "gate_i", "Wi", KD[D0], DX[D0], ["xf"], WD)
                product(pe, S, D2, i, "v1", "L3_W1", KD[D2], DX[D2], ["xf"], WD)
            if part == 5:
                product(pe, S, D0, i, "gate_g", "Wg", KD[D0], DX[D0], ["sig_i"], WD)
                product(pe, S, D2, i, "v2", "L3_W2", KD[D2], B1[D2], ["va1"], WD)
            if part == 6:
                product(pe, S, D0, i, "gate_o", "Wo", KD[D0], DX[D0], ["tanh_g"], WD)
            if part == 7:
                pe.wait_ge(*S.after("norm", D1, i))
                transposes(KD[D1], R[D1], DP).then_inc(S.did("lnB", D1), 1)

        def dense_act(act, S, i, part):
            if part == 0:
                function(act, S, D1, i, "ua0", ACT.Relu, "L2_b0", KD[D1], B1[D1], ["u0"], WD)
                function(act, S, DE, i, "ra1", ACT.Relu, "L1_b1", KD[DE], B1[DE], ["r1"], WD)
            if part == 1:
                function(act, S, D1, i, "ua1", ACT.Relu, "L2_b1", KD[D1], B2[D1], ["u1"], WD)
                function(act, S, DE, i, "ya", ACT.Relu, "L1_b23", KD[DE], B1[DE], ["y"], WD)
            if part == 2:
                ln_norm(act, S, D0, i, XR, R[D0], DP)
                ln_norm(act, S, D2, i, KD[D2], R[D2], DP)
            if part == 3:
                act.wait_ge(*S.after("z", DE, i))
                function(act, S, D0, i, "xf", ACT.Copy, None, KD[D0], DX[D0], ["lnB"], WD)
                function(act, S, D2, i, "xf", ACT.Copy, None, KD[D2], DX[D2], ["lnB"], WD)
            if part == 4:
                function(act, S, D0, i, "sig_i", ACT.Sigmoid, "bi", KD[D0], B1[D0], ["gate_i"], WD)
                function(act, S, D2, i, "va1", ACT.Relu, "L3_b1", KD[D2], B1[D2], ["v1"], WD)
            if part == 5:
                function(act, S, D0, i, "tanh_g", ACT.Tanh, "bg", KD[D0], B2[D0], ["gate_g"], WD)
                ln_norm(act, S, D1, i, KD[D1], R[D1], DP)
                function(act, S, D2, i, "va2", ACT.Relu, "L3_b2", KD[D2], B2[D2], ["v2"], WD)
            if part == 6:
                function(act, S, D0, i, "sig_o", ACT.Sigmoid, "bo", KD[D0], SO[D0], ["gate_o"], WD)
                function(act, S, D0, i, "tanh_c", ACT.Tanh, None, B1[D0], B2[D0], ["cell"], WD)
            if part == 7:
                function(act, S, D1, i, "xf", ACT.Copy, None, KD[D1], DX[D1], ["lnB"], WD)
                act.wait_ge(*stored["r"][D3].after(i - 1))
                ln_norm(act, S, D3, i, KD[D3], R[D3], DP)

        def dense_dve(dve, S, i, part):
            if part == 0:
                dve.wait_ge(*arr["x"][D0].after(i))
                dve.wait_ge(*S.after("norm", D0, i - 1))
                dve.wait_ge(*S.after("norm", D2, i - 1))
                ln_sums(dve, S, LNDA, [(D0, i), (D2, i)], {D0: XR, D2: KD[D2]}, DP)
                ln_roots(dve, S, LNDA, [(D0, i), (D2, i)], DP)
            if part == 1:
                dve.wait_ge(*S.after("u2", D1, i))
                dve.wait_ge(*S.after("lnT", D2, i))
                nc.vector.scalar_tensor_tensor(Z[D1][:, 0:WD], KD[D1][:, 0:WD], B["L2_b2"][:, 0:1], DX[D1][:, 0:WD],
                                               ALU.add, ALU.add).then_inc(S.did("z", D1), 1)
                dve.wait_ge(*S.after("ya", DE, i))
                nc.vector.tensor_tensor(Z[DE][:, 0:WD], B1[DE][:, 0:WD], DX[D0][:, 0:WD], ALU.add).then_inc(S.did("z", DE), 1)
            if part == 3:
                dve.wait_ge(*S.after("norm", D1, i - 1))
                dve.wait_ge(*S.after("norm", D3, i - 1))
                ln_sums(dve, S, LNDB, [(D1, i), (D3, i)], {D1: KD[D1], D3: KD[D3]}, DP)
            if part == 4:
                ln_roots(dve, S, LNDB, [(D1, i), (D3, i)], DP)
            if part == 5:
                cell(dve, S, D0, i, B1[D0], B2[D0], WD)
            if part == 6:
                dve.wait_ge(*S.after("va2", D2, i))
                dve.wait_ge(*S.after("lnT", D3, i))
                nc.vector.tensor_tensor(Z[D2][:, 0:WD], B2[D2][:, 0:WD], DX[D2][:, 0:WD], ALU.add).then_inc(S.did("z", D2), 1)
                dve.wait_ge(*S.after("r1", DE, i))
                hidden(dve, S, D0, i, B2[D0], H, WD)

        PARTS = range(8)

        def dense_load(sp, S, i, block_no):
            sp.wait_ge(*S.after("norm", D0, i - 1))
            sp.dma_start(XR[0:DP, :], x_in[block_no]).then_inc(arr["x"][D0].sem, 16)

        def dense_store(sp, S, i, block_no):
            sp.wait_ge(*S.after("norm", D3, i))
            sp.dma_start(no_block if block_no is None else y_out[block_no], R[D3][0:DP, :]).then_inc(stored["r"][D3].sem, 16)

        def dense_sync(sp, S, first, rounds):
            head = LAG if first == 0 else 0
            if first == 0:
                dense_load(sp, S, 0, 0)
            for i in range(head):
                dense_load(sp, S, i + 1, i + 1)
                dense_store(sp, S, i, None)
            with sp.Fori(head, rounds - 1) as i:
                dense_load(sp, S, i + 1, i + (1 + first))
                dense_store(sp, S, i, i + (first - LAG))
            dense_load(sp, S, rounds, min(first + rounds, DB - 1))
            dense_store(sp, S, rounds - 1, first + rounds - 1 - LAG)
            sp.wait_ge(*stored["r"][D3].after(rounds - 1))

        def dense_close(S, rounds):
            S.close({c: rounds for c in DENSE})
            arr["x"][D0].close(rounds)
            stored["r"][D3].close(rounds)

        def setup():
            with ExitStack() as loc:
                def lb(name, shape, dt=F32):
                    return loc.enter_context(nc.sbuf_tensor(name, shape, dt))

                rows_i = lb("rows_i", [T, 2, P], I32)
                rows_h = lb("rows_h", [T, 2, P], I32)
                rows_l = lb("rows_l", [T, 2, P], I32)
                rows_f = lb("rows_f", [T, 7, P])
                cols = lb("cols", [P, 7, T])
                wraw = lb("wraw", [P, 5, P])
                wt = lb("wt", [P, 2, P])
                braw = lb("braw", [P, 6])
                b2s = lb("b2s", [P, 1])
                loads = sem_loads
                iota_made, ones_made, zero_made = 1, 2, 3
                with nc.Block() as block:
                    @block.gpsimd
                    def _(pool):
                        nc.gpsimd.iota(iota_i[:], pattern=[[1, LO]], base=0, channel_multiplier=0)
                        nc.gpsimd.iota(pidx_i[:], pattern=[[0, 1]], base=0, channel_multiplier=1).then_inc(s_pool, 1)
                        nc.gpsimd.memset(ones[:], 1.0).then_inc(s_pool, 1)
                        nc.gpsimd.memset(zero[:], 0.0).then_inc(s_pool, 1)
                        for e in ("pool", "gather"):
                            for c in uses[e]:
                                pool.sem_inc(lane_sems[e][c], PRIME)

                    @block.vector
                    def _(dve):
                        nc.vector.memset(rows_i[:], PAD)
                        nc.vector.memset(rows_f[:, 6, :], 0.0)
                        nc.vector.memset(minus1[:], -1.0)
                        for buf in (H, DX[D0], DX[D1], Z[DE], Z[D1], Z[D2]):
                            nc.vector.memset(buf[:], 0.0)
                        nc.vector.memset(zerob[:], 0.0).then_inc(s_dve, 1)
                        dve.wait_ge(s_pool, iota_made)
                        nc.vector.tensor_copy(pidx[:], pidx_i[:])
                        nc.vector.tensor_copy(iot[:], iota_i[:]).then_inc(s_dve, 1)
                        dve.wait_ge(s_dve, 2)
                        nc.vector.tensor_scalar(ident[:], iot[:, 0:P], pidx[:, 0:1], None, ALU.is_equal)
                        nc.vector.tensor_scalar(identb[:], iot[:, 0:P], pidx[:, 0:1], None, ALU.is_equal)
                        nc.vector.tensor_scalar(before[:], iot[:, 0:P], pidx[:, 0:1], None, ALU.is_lt)
                        nc.vector.tensor_scalar(above[:], iot[:, 0:P], pidx[:, 0:1], None, ALU.is_gt).then_inc(s_dve, 1)
                        dve.wait_ge(loads, 16 * 6)
                        nc.vector.tensor_scalar(rows_h[:], rows_i[:], 9, None, ALU.arith_shift_right)
                        nc.vector.tensor_scalar(rows_l[:], rows_i[:], LO - 1, None, ALU.bitwise_and)
                        nc.vector.tensor_copy(rows_f[:, 0:2, :], rows_i[:]).then_inc(s_dve, 1)
                        dve.wait_ge(s_dve, 4)
                        nc.vector.tensor_copy(rows_f[:, 2:4, :], rows_h[:])
                        nc.vector.tensor_copy(rows_f[:, 4:6, :], rows_l[:]).then_inc(s_dve, 1)
                        dve.wait_ge(s_pe, 1)
                        nc.vector.tensor_copy(cols[:, 0:4, :], K[0][:, 0:4 * T].rearrange("p (a b) -> p a b", b=T))
                        nc.vector.tensor_copy(cols[:, 4:7, :], K[1][:, 0:3 * T].rearrange("p (a b) -> p a b", b=T)).then_inc(s_dve, 1)
                        dve.wait_ge(s_pe, 2)
                        for k, n in enumerate(["Wi", "Wg", "Wo"]):
                            nc.vector.tensor_copy(W[n][:], K[2][:, k * P:(k + 1) * P])
                        nc.vector.tensor_copy(wt[:, 0, :], K[3][:, 0:P])
                        nc.vector.tensor_copy(wt[:, 1, :], K[3][:, P:2 * P]).then_inc(s_dve, 1)
                        nc.vector.tensor_tensor(braw[:, 0:3], braw[:, 0:3], braw[:, 3:6], ALU.add).then_inc(s_dve, 1)
                        dve.wait_ge(s_dve, 8)
                        dve.wait_ge(s_pe, 3)
                        nc.vector.tensor_copy(W["L1_W23"][:], K[4][:, 0:P])
                        nc.vector.tensor_tensor(B["L1_b23"][:], K[5][:, 0:1], b3raw[:], ALU.add)
                        for k, n in enumerate(["bi", "bg", "bo"]):
                            nc.vector.tensor_tensor(B[n][:], K[6][:, k:k + 1], braw[:, k:k + 1], ALU.add)
                        nc.vector.drain().then_inc(s_dve, 1)
                        for c in uses["dve"]:
                            dve.sem_inc(lane_sems["dve"][c], PRIME)

                    @block.sync
                    def _(sp):
                        sp.wait_ge(s_dve, 1)
                        for k, n in enumerate(["dst", "src"]):
                            sp.dma_start(rows_i[0:F_FULL, k, :], a[n][0:F_FULL * P].rearrange("(t p) -> t p", p=P)).then_inc(loads, 16)
                            sp.dma_start(rows_i[F_FULL:F_FULL + 1, k, 0:F_REST], a[n][F_FULL * P:E].rearrange("(t p) -> t p", t=1)).then_inc(loads, 16)
                        ew = a["edge_weight"]
                        sp.dma_start(rows_f[0:F_FULL, 6, :], ew[0:F_FULL * P].rearrange("(t p) -> t p", p=P)).then_inc(loads, 16)
                        sp.dma_start(rows_f[F_FULL:F_FULL + 1, 6, 0:F_REST], ew[F_FULL * P:E].rearrange("(t p) -> t p", t=1)).then_inc(loads, 16)
                        wih, whh = a["L1_gnn_W_ih"], a["L1_gnn_W_hh"]
                        for k, g in enumerate([0, 2, 3]):
                            sp.dma_start(wraw[:, k, :], wih[g * P:(g + 1) * P, :]).then_inc(loads2, 16)
                            sp.dma_start(whraw[:, k, :], whh[g * P:(g + 1) * P, :]).then_inc(loads2, 16)
                            sp.dma_start(braw[:, k:k + 1], a["L1_gnn_b_ih"][g * P:(g + 1) * P].unsqueeze(1)).then_inc(loads2, 16)
                            sp.dma_start(braw[:, 3 + k:4 + k], a["L1_gnn_b_hh"][g * P:(g + 1) * P].unsqueeze(1)).then_inc(loads2, 16)
                        sp.dma_start(wraw[:, 3, :], a["L1_gnn_W2"]).then_inc(loads2, 16)
                        sp.dma_start(wraw[:, 4, :], a["L1_gnn_W3"]).then_inc(loads2, 16)
                        sp.dma_start(b2s[:], a["L1_gnn_b2"].unsqueeze(1)).then_inc(loads2, 16)
                        sp.dma_start(b3raw[:], a["L1_gnn_b3"].unsqueeze(1)).then_inc(loads2, 16)
                        direct = [("L0_W1", a["L0_gnn_W1"]), ("L0_W2a", a["L0_gnn_W2"][0:P, :]), ("L0_W2b", a["L0_gnn_W2"][P:2 * P, :]),
                                  ("L0_W3", a["L0_gnn_W3"]), ("L1_W1", a["L1_gnn_W1"]), ("L3_W1", a["L3_gnn_W1"]), ("L3_W2", a["L3_gnn_W2"])]
                        for k in range(3):
                            for m, t in enumerate("xfb"):
                                direct.append((f"W{k}{t}", a[f"L2_gnn_W{k}"][m * P:(m + 1) * P, :]))
                        for n, src in direct:
                            sp.dma_start(W[n][:], src).then_inc(loads2, 16)
                        dbias = [("L0_b1", "L0_gnn_b1"), ("L0_b2", "L0_gnn_b2"), ("L0_b3", "L0_gnn_b3"), ("L1_b1", "L1_gnn_b1"),
                                 ("L2_b0", "L2_gnn_b0"), ("L2_b1", "L2_gnn_b1"), ("L2_b2", "L2_gnn_b2"), ("L3_b1", "L3_gnn_b1"), ("L3_b2", "L3_gnn_b2")]
                        for n, src in dbias:
                            sp.dma_start(B[n][:], a[src].unsqueeze(1)).then_inc(loads2, 16)
                        sp.wait_ge(loads2, 16 * N_LOADS2)
                        sp.wait_ge(s_pool, zero_made)
                        spare = [tab[EP + 16 * m:EP + 16 * m + 16, :] for tab in (tab_f0, tab_f1, tab_b) for m in range(P // 16)]
                        for n, by_lane in stored.items():
                            for c in by_lane:
                                sp.dma_start(spare.pop(0), zero[0:16, 0:D]).then_inc(stored[n][c].sem, 16)
                        for rows in spare:
                            sp.dma_start(rows, zero[0:16, 0:D]).then_inc(setup_dma.sem, 16)
                        sp.dma_start(key_d[0:1].unsqueeze(0), minus1[0:1, 0:1]).then_inc(setup_dma.sem, 16)
                        sp.dma_start(key_s[0:1].unsqueeze(0), minus1[0:1, 0:1]).then_inc(setup_dma.sem, 16)
                        for n, by_lane in stored.items():
                            for c in by_lane:
                                sp.wait_ge(stored[n][c].sem, 16)
                                stored[n][c].base = 16
                        sp.wait_ge(setup_dma.sem, SD)

                    @block.tensor
                    def _(pe):
                        pe.wait_ge(s_dve, 5)
                        for k in range(7):
                            last = nc.tensor.transpose(K[k // 4][:, (k % 4) * T:(k % 4 + 1) * T], rows_f[:, k, :], ident[0:T, 0:T])
                        last.then_inc(s_pe, 1)
                        pe.wait_ge(loads2, 16 * N_LOADS2)
                        for k in range(3):
                            nc.tensor.transpose(K[2][:, k * P:(k + 1) * P], wraw[:, k, :], ident[:])
                        nc.tensor.transpose(K[3][:, 0:P], wraw[:, 3, :], ident[:])
                        nc.tensor.transpose(K[3][:, P:2 * P], wraw[:, 4, :], ident[:]).then_inc(s_pe, 1)
                        pe.wait_ge(s_dve, 7)
                        nc.tensor.matmul(K[4][:, 0:P], wt[:, 0, :], wt[:, 1, :], start=True, stop=True)
                        nc.tensor.matmul(K[5][:, 0:1], wt[:, 1, :], b2s[:], start=True, stop=True)
                        for k in range(3):
                            last = nc.tensor.transpose(K[7][:, k * P:(k + 1) * P], whraw[:, k, :], ident[:])
                        last.then_inc(s_pe2, 1)
                        pe.wait_ge(s_act, 1)
                        pe.wait_ge(s_pool, zero_made)
                        for k in range(3):
                            last = nc.tensor.matmul(K[6][:, k:k + 1], whT[:, k, :], zero[:, 0:1], start=True, stop=True)
                        last.then_inc(s_pe, 1)
                        for c in uses["pe"]:
                            pe.sem_inc(lane_sems["pe"][c], PRIME)

                    @block.scalar
                    def _(act):
                        act.wait_ge(s_pe2, 1)
                        nc.scalar.activation(whT[:].rearrange("p a b -> p (a b)"), K[7][:, 0:3 * P], ACT.Copy).then_inc(s_act, 1)
                        for c in uses["act"]:
                            act.sem_inc(lane_sems["act"][c], PRIME)
                sort(cols, loc)

        def sort(cols, loc):
            def lb(name, shape, dt=F32):
                return loc.enter_context(nc.sbuf_tensor(name, shape, dt))

            HB = 4
            oneh = [[lb(f"oneh{b}_{k}", [P, HI], BF16) for k in range(2)] for b in range(HB)]
            onel = [[lb(f"onel{b}_{k}", [P, LO], BF16) for k in range(2)] for b in range(HB)]
            onehf = [lb(f"onehf{b}", [P, HI]) for b in range(HB)]
            onelw = [lb(f"onelw{b}", [P, LO]) for b in range(HB)]
            wcol = [lb(f"weight_col{b}", [P, 1]) for b in range(HB)]
            hist = lb("hist", [HI, 3, LO])
            base = lb("base", [HI, 2, LO])
            rowtot = lb("rowtot", [HI, 2])
            rowbase = lb("rowbase", [HI, 2])
            nt = lb("nt", [HI, LO, NF])
            t1 = lb("t1", [HI, LO])
            t2 = lb("t2", [HI, LO])
            t3 = lb("t3", [HI, LO])
            t4 = lb("t4", [HI, LO])
            degree, root, step = [lb(n, [HI, 2, LO]) for n in ("degree", "degree_root", "degree_step")]
            bits = lb("degree_bits", [HI, 2, LO], I32)

            with nc.Block() as block:
                @block.vector
                def _(dve):
                    with dve.Fori(0, T // HB) as i:
                        for b in range(HB):
                            t = i * HB + b
                            dve.wait_ge(hist_done, t + 1)
                            for k in range(2):
                                nc.vector.tensor_scalar(oneh[b][k][:], iot[:, 0:HI], cols[:, 2 + k, bass.ds(t, 1)], None, ALU.is_equal)
                                last = nc.vector.tensor_scalar(onel[b][k][:], iot[:], cols[:, 4 + k, bass.ds(t, 1)], None, ALU.is_equal)
                                if k == 0:
                                    nc.vector.tensor_copy(wcol[b][:], cols[:, 6, bass.ds(t, 1)]).then_inc(dst_ready, 1)
                            last.then_inc(onehots_ready, 1)
                    dve.wait_ge(hist_done, T + HB + 1)
                    for k in range(3):
                        last = nc.vector.tensor_copy(hist[:, k, :], K[k][0:HI, :])
                    last.then_inc(s_dve, 1)

                @block.tensor
                def _(pe):
                    for k in range(3):
                        last = nc.tensor.matmul(K[k][0:HI, :], zerob[:, 0:HI], zerob[:], start=True, stop=False)
                    last.then_inc(hist_done, HB)
                    with pe.Fori(0, T // HB) as i:
                        for b in range(HB):
                            pe.wait_ge(onehots_ready, i * HB + (b + 1))
                            for k in range(2):
                                nc.tensor.matmul(K[k][0:HI, :], oneh[b][k][:], onel[b][k][:], start=False, stop=False)
                            pe.wait_ge(weighted_ready, i * HB + (b + 1))
                            nc.tensor.matmul(K[2][0:HI, :], onehf[b][:], onelw[b][:], start=False, stop=False).then_inc(hist_done, 1)
                    for k in range(3):
                        last = nc.tensor.matmul(K[k][0:HI, :], zerob[:, 0:HI], zerob[:], start=False, stop=True)
                    last.then_inc(hist_done, 1)

                @block.scalar
                def _(act):
                    with act.Fori(0, T // HB) as i:
                        for b in range(HB):
                            act.wait_ge(dst_ready, i * HB + (b + 1))
                            nc.scalar.activation(onehf[b][:], oneh[b][0][:], ACT.Copy)
                            nc.scalar.activation(onelw[b][:], onel[b][0][:], ACT.Identity, bias=zero[:, 0:1],
                                                 scale=wcol[b][:, 0:1]).then_inc(weighted_ready, 1)

            d0 = 10
            with nc.Block() as block:
                @block.vector
                def _(dve):
                    n = [d0]

                    def link(ins):
                        n[0] += 1
                        ins.then_inc(s_dve, 1)
                        dve.wait_ge(s_dve, n[0])

                    link(nc.vector.tensor_reduce(rowtot[:], hist[:, 0:2, :], AX, ALU.add))
                    dve.wait_ge(s_pe, 4)
                    link(nc.vector.tensor_copy(rowbase[:], K[3][0:HI, 0:2]))
                    for k in range(2):
                        link(nc.vector.tensor_tensor_scan(t1[:], ones[0:HI, :], hist[:, k, :], rowbase[:, k:k + 1], ALU.mult, ALU.add))
                        nc.vector.tensor_tensor(base[:, k, :], t1[:], hist[:, k, :], ALU.subtract)
                        link(nc.vector.tensor_scalar(t2[:], hist[:, k, :], 1.0, None, ALU.min))
                        link(nc.vector.scalar_tensor_tensor(t3[:], t1[:], float(-1 - EP), t2[:], ALU.add, ALU.mult))
                        link(nc.vector.tensor_scalar(nt[:, :, N_ENDD + k], t3[:], float(EP), None, ALU.add))
                        link(nc.vector.tensor_scalar(t4[:], hist[:, k, :], 1.0, None, ALU.max))
                        link(nc.vector.reciprocal(nt[:, :, N_INVIN if k == 0 else N_INVOUT], t4[:]))
                    nc.vector.tensor_copy(nt[:, :, N_CNTD], hist[:, 0, :])
                    nc.vector.tensor_scalar(nt[:, :, 7], hist[:, 0, :], 0.0, None, ALU.mult)
                    link(nc.vector.tensor_scalar(degree[:, 0, :], hist[:, 0, :], 1.0, None, ALU.add))
                    link(nc.vector.tensor_scalar(degree[:, 1, :], hist[:, 2, :], 1.0, None, ALU.add))
                    link(nc.vector.tensor_scalar(t3[:], degree[:, 1, :], 0.0, None, ALU.is_gt))
                    link(nc.vector.tensor_scalar(t4[:], t3[:], -1.0, 1.0, ALU.mult, ALU.add))
                    link(nc.vector.tensor_tensor(degree[:, 1, :], degree[:, 1, :], t3[:], ALU.mult))
                    link(nc.vector.tensor_tensor(degree[:, 1, :], degree[:, 1, :], t4[:], ALU.add))
                    link(nc.vector.tensor_scalar(bits[:], degree[:].bitcast(I32), 1, None, ALU.arith_shift_right))
                    link(nc.vector.tensor_scalar(root[:].bitcast(I32), bits[:], -1.0, float(0x5F3759DF), ALU.mult, ALU.add))
                    for _ in range(3):
                        link(nc.vector.scalar_tensor_tensor(step[:], root[:], -0.5, root[:], ALU.mult, ALU.mult))
                        link(nc.vector.tensor_tensor(step[:], step[:], degree[:], ALU.mult))
                        link(nc.vector.scalar_tensor_tensor(root[:], step[:], 1.5, root[:], ALU.add, ALU.mult))
                    nc.vector.tensor_copy(nt[:, :, N_DINV1], root[:, 0, :])
                    link(nc.vector.tensor_tensor(nt[:, :, N_DINV3], root[:, 1, :], t3[:], ALU.mult))

                @block.tensor
                def _(pe):
                    pe.wait_ge(s_dve, d0 + 1)
                    nc.tensor.matmul(K[3][0:HI, 0:2], above[0:HI, 0:HI], rowtot[:], start=True, stop=True).then_inc(s_pe, 1)

                @block.sync
                def _(sp):
                    sp.wait_ge(s_dve, d0 + 2 + 2 * 6 + 7 + 11)
                    sp.dma_start(node_tab.rearrange("(h l) f -> h (l f)", h=HI), nt[:].rearrange("h l f -> h (l f)")).then_inc(setup_dma.sem, 16)
                    sp.wait_ge(setup_dma.sem, SD + 16)

            pos = lb("pos", [P, 2, T])
            pair = [dict(onehf=[lb(f"onehf_b{b}k{k}", [P, HI]) for k in range(2)], kbc=[lb(f"kbc_b{b}k{k}", [P, P]) for k in range(2)],
                         keys=lb(f"keys_b{b}", [P, 2, 1]), ohT=lb(f"ohT_b{b}", [HI, 2, P])) for b in range(2)]
            pick = [lb(f"pick{k}", [P, LO]) for k in range(2)]
            tie = [lb(f"tie{k}", [P, P]) for k in range(2)]
            acc = [lb(f"acc{k}", [P, 2]) for k in range(2)]
            place = [("look", "pe"), ("outer", "pe"), ("tie", "dve"), ("base", "dve"), ("pick", "dve"), ("pos", "dve")]
            S = Steps(lane_sems, lane_base, {LA: place, LB: place, NA: [("hots", "dve"), ("trans", "pe"), ("ohT", "act")]})
            dense1 = Steps(lane_sems, lane_base, DENSE)
            G = T // 10
            idx_i = lb("idx_i", [P, 4, T], I32)
            rec = lb("rec", [P, T, RF])
            idx_g = lb("idx_g", [P, 2, G], I32)
            got = [lb(f"got{k}", [P, G, NF]) for k in range(2)]
            part = lb("part", [P, G, RF])
            keys_T, looked, outer = K[0], (K[1], K[2]), K[3]
            ROUNDS = T // RANK_TILES

            def tiles(eng, ahead, now, dense_part):
                def body(i, more):
                    for u in range(RANK_TILES):
                        t = i * RANK_TILES + u
                        dense_part(i, 2 * u)
                        now(t, u % 2, lambda: ahead(t + 1, (u + 1) % 2) if more or u < RANK_TILES - 1 else None,
                            lambda: dense_part(i, 2 * u + 1))
                ahead(0, 0)
                with eng.Fori(0, ROUNDS - 1) as i:
                    body(i, True)
                body(ROUNDS - 1, False)

            with nc.Block() as block:
                @block.vector
                def _(dve):
                    def ahead(t, b):
                        for k in range(2):
                            dve.wait_ge(*S.after("outer", k, t - 2))
                        dve.wait_ge(*S.after("trans", NA, t - 2))
                        for k in range(2):
                            nc.vector.tensor_scalar(pair[b]["onehf"][k][:], iot[:, 0:HI], cols[:, 2 + k, bass.ds(t, 1)], None, ALU.is_equal)
                            nc.vector.tensor_scalar(oneh[b][k][:], iot[:, 0:HI], cols[:, 2 + k, bass.ds(t, 1)], None, ALU.is_equal)
                            nc.vector.tensor_scalar(onel[b][k][:], iot[:], cols[:, 4 + k, bass.ds(t, 1)], None, ALU.is_equal)
                            nc.vector.tensor_scalar(pair[b]["kbc"][k][:], ones[:, 0:P], cols[:, k, bass.ds(t, 1)], None, ALU.mult)
                        nc.vector.tensor_copy(pair[b]["keys"][:], cols[:, 0:2, bass.ds(t, 1)]).then_inc(S.did("hots", NA), 1)

                    def now(t, b, prepare, between):
                        dve.wait_ge(*S.after("hots", NA, t))
                        dve.wait_ge(*S.after("ohT", NA, t))
                        for k in range(2):
                            dve.wait_ge(*S.after("pos", k, t - 1))
                            nc.vector.scalar_tensor_tensor(tie[k][:], keys_T[:, (2 * k + 1) * P:(2 * k + 2) * P], pair[b]["keys"][:, k, :], before[:],
                                                           ALU.is_equal, ALU.mult, accum_out=acc[k][:, 0:1]).then_inc(S.did("tie", k), 1)
                        for k in range(2):
                            dve.wait_ge(*S.after("outer", k, t))
                            dve.wait_ge(*S.after("look", k, t))
                            nc.vector.tensor_tensor(base[:, k, :], base[:, k, :], outer[0:HI, :], ALU.add).then_inc(S.did("base", k), 1)
                            if k == 0:
                                prepare()
                        between()
                        for k in range(2):
                            nc.vector.scalar_tensor_tensor(pick[k][:], looked[k][:], 1.0, onel[b][k][:], ALU.mult, ALU.mult,
                                                           accum_out=acc[k][:, 1:2]).then_inc(S.did("pick", k), 1)
                        for k in range(2):
                            dve.wait_ge(*S.after("pick", k, t))
                            nc.vector.tensor_tensor(pos[:, k, bass.ds(t, 1)], acc[k][:, 0:1], acc[k][:, 1:2], ALU.add).then_inc(S.did("pos", k), 1)
                    nc.vector.tensor_copy(idx_i[:, 0:2, :], cols[:, 0:2, :]).then_inc(rec_ready, 1)
                    nc.vector.tensor_copy(rec[:, :, R_DST], cols[:, 0, :])
                    nc.vector.tensor_copy(rec[:, :, R_SRC], cols[:, 1, :])
                    nc.vector.tensor_copy(rec[:, :, R_W], cols[:, 6, :])
                    nc.vector.tensor_scalar(rec[:, :, 15], cols[:, 0, :], 0.0, None, ALU.mult)
                    tiles(dve, ahead, now, lambda i, part: dense_dve(dve, dense1, i, part))

                @block.tensor
                def _(pe):
                    def ahead(t, b):
                        pe.wait_ge(*S.after("hots", NA, t))
                        pe.wait_ge(*S.after("ohT", NA, t - 1))
                        for k in range(2):
                            pe.wait_ge(*S.after("tie", k, t - 1))
                        for k in range(2):
                            nc.tensor.transpose(keys_T[0:HI, 2 * k * P:(2 * k + 1) * P], pair[b]["onehf"][k][:], ident[:])
                            last = nc.tensor.transpose(keys_T[:, (2 * k + 1) * P:(2 * k + 2) * P], pair[b]["kbc"][k][:], ident[:])
                        last.then_inc(S.did("trans", NA), 1)

                    def now(t, b, prepare, between):
                        pe.wait_ge(*S.after("ohT", NA, t))
                        for k in range(2):
                            pe.wait_ge(*S.after("base", k, t - 1))
                            pe.wait_ge(*S.after("pick", k, t - 1))
                            nc.tensor.matmul(looked[k][:], pair[b]["ohT"][:, k, :], base[:, k, :], start=True, stop=True).then_inc(S.did("look", k), 1)
                            if k:
                                between()
                            pe.wait_ge(*(S.after("base", 0, t) if k else S.after("base", 1, t - 1)))
                            nc.tensor.matmul(outer[0:HI, :], oneh[b][k][:], onel[b][k][:], start=True, stop=True).then_inc(S.did("outer", k), 1)
                        prepare()
                    tiles(pe, ahead, now, lambda i, part: dense_pe(pe, dense1, i, part))

                @block.scalar
                def _(act):
                    def ahead(t, b):
                        act.wait_ge(*S.after("trans", NA, t))
                        for k in range(2):
                            act.wait_ge(*S.after("look", k, t - 2))
                        nc.scalar.activation(pair[b]["ohT"][:], keys_T[0:HI, :].rearrange("h (k m) -> h k m", k=2)[:, :, 0:P],
                                             ACT.Copy).then_inc(S.did("ohT", NA), 1)

                    def now(t, b, prepare, between):
                        between()
                        prepare()
                    tiles(act, ahead, now, lambda i, part: dense_act(act, dense1, i, part))

                @block.gpsimd
                def _(pool):
                    pool.wait_ge(rec_ready, 1)
                    pool.sem_inc(copied, 1)
                    with pool.Fori(0, T // G) as r:
                        pool.wait_ge(copied, r * 3 + 1)
                        pool.sem_inc(pool_passed, 1)
                        nc.gpsimd.tensor_copy(idx_g[:], idx_i[:, 0:2, bass.ds(r * G, G)]).then_inc(copied, 1)
                        pool.wait_ge(copied, r * 3 + 2)
                        pool.sem_inc(pool_passed, 1)
                        for k in range(2):
                            for g in range(G):
                                nc.gpsimd.indirect_dma_start(
                                    out=got[k][:, g, :], out_offset=None, in_=node_tab,
                                    in_offset=bass.IndirectOffsetOnAxis(ap=idx_g[:, k, g:g + 1].bitcast(U32), axis=0),
                                    bounds_check=HI * LO - 1, oob_is_err=False).then_inc(pool_dma.sem, 16)
                        pool.wait_ge(pool_dma.sem, r * (32 * G) + 32 * G)
                        pool.sem_inc(pool_passed, 1)
                        view = rec[:, bass.ds(r * G, G), :]
                        for dst, side, src in ((R_DINV1A, 0, N_DINV1), (R_DINV3A, 0, N_DINV3), (R_INVIN, 0, N_INVIN),
                                               (R_ENDD_DST, 0, N_ENDD), (R_ENDS_DST, 0, N_ENDS),
                                               (R_DINV1B, 1, N_DINV1), (R_DINV3B, 1, N_DINV3), (R_INVOUT, 1, N_INVOUT),
                                               (R_ENDD_SRC, 1, N_ENDD), (R_ENDS_SRC, 1, N_ENDS)):
                            nc.gpsimd.tensor_copy(view[:, :, dst:dst + 1], got[side][:, :, src:src + 1])
                        nc.gpsimd.tensor_copy(view[:, :, R_CNTD_SRC:R_CNTD_SRC + 1], got[1][:, :, N_CNTD:N_CNTD + 1]).then_inc(copied, 1)
                        pool.wait_ge(copied, r * 3 + 3)
                        pool.sem_inc(copied, 1)

                @block.sync
                def _(sp):
                    dense_sync(sp, dense1, 0, DENSE_RANK)
            S.close({LA: T, LB: T, NA: T})
            dense_close(dense1, DENSE_RANK)
            records(cols, pos, loc, (idx_i, rec, idx_g, part))

        def records(cols, pos, loc, rec_bufs):
            def lb(name, shape, dt=F32):
                return loc.enter_context(nc.sbuf_tensor(name, shape, dt))

            G = T // 10
            idx_i, rec, idx_g, part = rec_bufs
            rd_c = lb("rd_c", [P, T, RF])
            rs_c = lb("rs_c", [P, T, RF])
            dense2 = Steps(lane_sems, lane_base, DENSE)
            with nc.Block() as block:
                @block.vector
                def _(dve):
                    nc.vector.tensor_copy(idx_i[:, 2:4, :], pos[:])
                    nc.vector.tensor_copy(rec[:, :, R_POSS], pos[:, 1, :]).then_inc(rec_ready, 1)
                    with dve.Fori(0, DENSE_RECORDS) as i:
                        for part in PARTS:
                            dense_dve(dve, dense2, i, part)

                @block.tensor
                def _(pe):
                    with pe.Fori(0, DENSE_RECORDS) as i:
                        for part in PARTS:
                            dense_pe(pe, dense2, i, part)

                @block.scalar
                def _(act):
                    with act.Fori(0, DENSE_RECORDS) as i:
                        for part in PARTS:
                            dense_act(act, dense2, i, part)

                @block.sync
                def _(sp):
                    dense_sync(sp, dense2, DENSE_RANK, DENSE_RECORDS)

                @block.gpsimd
                def _(pool):
                    pool.wait_ge(rec_ready, 2)
                    pool.wait_ge(copied, (T // G) * 3 + 1)
                    with pool.Fori(0, T // G) as r:
                        nc.gpsimd.tensor_copy(part[:], rec[:, bass.ds(r * G, G), :])
                        nc.gpsimd.tensor_copy(idx_g[:], idx_i[:, 2:4, bass.ds(r * G, G)]).then_inc(copied, 1)
                        pool.wait_ge(copied, r + ((T // G) * 3 + 2))
                        pool.sem_inc(pool_passed, 1)
                        for k, tab in enumerate((rec_d, rec_s)):
                            for g in range(G):
                                nc.gpsimd.indirect_dma_start(
                                    out=tab, out_offset=bass.IndirectOffsetOnAxis(ap=idx_g[:, k, g:g + 1].bitcast(U32), axis=0),
                                    in_=part[:, g, :], in_offset=None, bounds_check=EP - 1, oob_is_err=False).then_inc(pool_dma.sem, 16)
                        pool.wait_ge(pool_dma.sem, r * (32 * G) + (T // G + 1) * 32 * G)
                        pool.sem_inc(pool_passed, 1)
                    pool_dma.base = 2 * (T // G) * 32 * G
            dense_close(dense2, DENSE_RECORDS)

            sd_r = lb("sd_r", [T, 12, P])
            prev = lb("prev", [T, 2, P])
            e_pos = lb("e_pos", [P, T])
            e_pos_i = lb("e_pos_i", [P, T], I32)
            u1 = lb("u1", [P, T])
            u2 = lb("u2", [P, T])
            u3 = lb("u3", [P, T])
            with nc.Block() as block:
                @block.sync
                def _(sp):
                    sp.dma_start(rd_c[:], rec_d.rearrange("(t p) f -> p t f", p=P)).then_inc(setup_dma.sem, 16)
                    sp.dma_start(rs_c[:], rec_s.rearrange("(t p) f -> p t f", p=P)).then_inc(setup_dma.sem, 16)
                    sp.wait_ge(rows_done, 3)
                    sp.dma_start(key_d[1:1 + EP].rearrange("(t p) -> t p", p=P), sd_r[:, 0, :]).then_inc(setup_dma.sem, 16)
                    sp.dma_start(key_s[1:1 + EP].rearrange("(t p) -> t p", p=P), sd_r[:, 7, :]).then_inc(setup_dma.sem, 16)
                    sp.wait_ge(setup_dma.sem, SD + 16 + 64)
                    sp.dma_start(prev[:, 0, :], key_d[0:EP].rearrange("(t p) -> t p", p=P)).then_inc(setup_dma.sem, 16)
                    sp.dma_start(prev[:, 1, :], key_s[0:EP].rearrange("(t p) -> t p", p=P)).then_inc(setup_dma.sem, 16)
                    sp.wait_ge(same_done, 1)
                    sc = scal.rearrange("c j b -> c (j b)").rearrange("c (t p) -> c t p", p=P)
                    for c, row in ((C_SAMED, 9), (C_W, 1), (C_D1A, 2), (C_D1B, 3), (C_D3A, 4), (C_D3B, 5), (C_INVOUT, 6),
                                   (C_SAMES, 10), (C_INVIN, 8)):
                        sp.dma_start(sc[c], sd_r[:, row, :]).then_inc(setup_dma.sem, 16)
                    sp.wait_ge(setup_dma.sem, SD + 16 + 64 + 32 + 16 * CF)
                    setup_dma.base = 0

                @block.tensor
                def _(pe):
                    pe.wait_ge(setup_dma.sem, SD + 16 + 32)
                    fields = [(rd_c, R_DST), (rd_c, R_W), (rd_c, R_DINV1A), (rd_c, R_DINV1B), (rd_c, R_DINV3A), (rd_c, R_DINV3B),
                              (rd_c, R_INVOUT), (rs_c, R_SRC), (rs_c, R_INVIN)]
                    for n, (src, f) in enumerate(fields):
                        last = nc.tensor.transpose(K[n // 4][0:T, (n % 4) * P:(n % 4 + 1) * P], src[:, :, f], ident[:])
                        if n % 4 == 3 or n == 8:
                            last.then_inc(rows_T, 1)

                @block.scalar
                def _(act):
                    for n in range(3):
                        w = 4 if n < 2 else 1
                        act.wait_ge(rows_T, n + 1)
                        nc.scalar.activation(sd_r[:, 4 * n:4 * n + w, :].rearrange("t a b -> t (a b)"), K[n][0:T, 0:w * P], ACT.Copy).then_inc(rows_done, 1)

                @block.gpsimd
                def _(pool):
                    nc.gpsimd.iota(e_pos_i[:], pattern=[[P, T]], base=0, channel_multiplier=1).then_inc(copied, 1)

                @block.vector
                def _(dve):
                    n = [0]

                    def link(ins):
                        n[0] += 1
                        ins.then_inc(lists_dve, 1)
                        dve.wait_ge(lists_dve, n[0])

                    dve.wait_ge(setup_dma.sem, SD + 16 + 32)
                    dve.wait_ge(copied, (T // G) * 4 + 2)
                    nc.vector.tensor_copy(e_pos[:], e_pos_i[:])
                    nc.vector.tensor_scalar(IX["xa"][:], rd_c[:, :, R_DST], float(N - 1), None, ALU.min)
                    nc.vector.tensor_scalar(IX["xb"][:], rd_c[:, :, R_SRC], float(N - 1), None, ALU.min)
                    nc.vector.tensor_copy(IX["end_f"][:], rd_c[:, :, R_ENDD_SRC])
                    nc.vector.tensor_copy(IX["end_bb"][:], rd_c[:, :, R_ENDS_SRC])
                    nc.vector.tensor_copy(IX["end_ba"][:], rd_c[:, :, R_ENDS_DST])
                    nc.vector.tensor_copy(IX["dst_in_s"][:], rs_c[:, :, R_ENDD_DST])
                    link(nc.vector.tensor_scalar(u1[:], rd_c[:, :, R_DST], float(N - 1), None, ALU.is_le))
                    link(nc.vector.tensor_tensor(u2[:], e_pos[:], rd_c[:, :, R_ENDD_DST], ALU.is_equal))
                    link(nc.vector.tensor_tensor(u1[:], u1[:], u2[:], ALU.mult))
                    link(nc.vector.scalar_tensor_tensor(u3[:], rd_c[:, :, R_DST], float(-SKIP), u1[:], ALU.add, ALU.mult))
                    link(nc.vector.tensor_scalar(IX["out_a"][:], u3[:], float(SKIP), None, ALU.add))
                    link(nc.vector.tensor_scalar(u1[:], rd_c[:, :, R_SRC], float(N - 1), None, ALU.is_le))
                    link(nc.vector.tensor_tensor(u2[:], rd_c[:, :, R_POSS], rd_c[:, :, R_ENDS_SRC], ALU.is_equal))
                    link(nc.vector.tensor_tensor(u1[:], u1[:], u2[:], ALU.mult))
                    link(nc.vector.tensor_scalar(u2[:], rd_c[:, :, R_CNTD_SRC], 0.0, None, ALU.is_equal))
                    link(nc.vector.tensor_tensor(u1[:], u1[:], u2[:], ALU.mult))
                    link(nc.vector.scalar_tensor_tensor(u3[:], rd_c[:, :, R_SRC], float(-SKIP), u1[:], ALU.add, ALU.mult))
                    link(nc.vector.tensor_scalar(IX["out_b"][:], u3[:], float(SKIP), None, ALU.add))
                    dve.wait_ge(setup_dma.sem, SD + 16 + 64 + 32)
                    dve.wait_ge(rows_done, 3)
                    nc.vector.tensor_tensor(sd_r[:, 9, :], sd_r[:, 0, :], prev[:, 0, :], ALU.is_equal)
                    nc.vector.tensor_tensor(sd_r[:, 10, :], sd_r[:, 7, :], prev[:, 1, :], ALU.is_equal).then_inc(same_done, 1)

        pidx_i = sb("pidx_i", [P, 1], I32)
        whraw = sb("whraw", [P, 3, P])
        whT = sb("whT", [P, 3, P])
        b3raw = sb("b3raw", [P, 1])
        sem_loads, loads2 = sem("edges_loaded"), sem("weights_loaded")
        N_LOADS2 = 12 + 4 + 16 + 9
        s_pe2 = sem("whh_transposed")
        hist_done, onehots_ready = sem("hist_done"), sem("onehots_ready")
        dst_ready, weighted_ready = sem("dst_onehots_ready"), sem("weighted_onehots_ready")
        rec_ready, copied = sem("rec_ready"), sem("copied")
        rows_T, rows_done, same_done, lists_dve = sem("rows_T"), sem("rows_done"), sem("same_done"), sem("lists_dve")
        SD = 16 * (3 * P // 16 - sum(map(len, stored.values())) + 2)
        setup()
        LV, LX, LS = per(AB, "in_v"), per(AB, "in_x"), per((LA, LB, LM), "in_scale")
        LT = per((LA, LB, LM), "in_same")
        G1, G2 = per(AB, "rows1"), per(AB, "rows2")
        B1.update(per((LA, LB, LM), "b1"))
        B2.update(per(AB, "b2"))
        BT, CT = per((TA, TB), "cell"), per((TA, TB), "tanh")
        SO.update(per((TA, TB), "sig_o"))
        Z.update(per(AB, "z"))
        ZM = [sb(f"sums{m}", [P, BLK]) for m in range(2)]
        OX, OV = per(AB, "out_x"), per(AB, "out_v")
        R.update(per((LA, LB, NA, NBL, LM), "out_rows"))
        OUT_ROWS = {c: (R[c], sb(f"out_rows1_{names_of[c]}", [P, BLK])) for c in (NA, NBL)}
        V_IN = {c: (LV[c], sb(f"in_v1_{names_of[c]}", [P, BLK])) for c in AB}
        X_IN = {c: (LX[c], sb(f"in_x1_{names_of[c]}", [P, BLK])) for c in AB}
        S_IN = {c: (LS[c], sb(f"in_scale1_{names_of[c]}", [P, BLK])) for c in (LA, LB, LM)}
        SAME = {c: (LT[c], sb(f"in_same1_{names_of[c]}", [P, BLK])) for c in (LM,)}
        ROWS1 = {c: (G1[c], sb(f"rows1b_{names_of[c]}", [P, BLK])) for c in AB}
        ROWS2 = {c: (G2[c], sb(f"rows2b_{names_of[c]}", [P, BLK])) for c in AB}

        def edge_stage(tab):
            steps = [("ids", "gather"), ("inT", "pe"), ("xa", "act"), ("xb", "dve"), ("proj", "pe"), ("hi", "act"), ("d", "dve"), ("mlp1", "pe"),
                     ("m1", "act"), ("mlp2", "pe"), ("m2", "act"), ("scan", "dve"), ("rowsT", "pe"), ("rows", "act")]
            S = Steps(lane_sems, lane_base, {LA: steps, LB: steps})
            KK = [[K[4 * c + m] for m in range(4)] for c in range(2)]
            with nc.Block() as block:
                @block.gpsimd
                def _(pool):
                    def body(i, cs):
                        for c in cs:
                            gather(pool, S, c, i, i * 2 + c, "inT", [("xa", a["x"], G1[c], arr["g1"][c].sem), ("xb", a["x"], G2[c], arr["g2"][c].sem)])
                    in_turns(pool, body)

                @block.sync
                def _(sp):
                    def load(i, cs):
                        for c in cs:
                            sp.wait_ge(*S.after("scan", c, i - 1))
                            sp.dma_start(LT[c][:], bcast(C_SAMED, i * 2 + c)).then_inc(arr["same"][c].sem, 16)

                    def store(i, cs):
                        for c in cs:
                            j = i * 2 + c
                            sp.wait_ge(*S.after("xa", c, i))
                            sp.dma_start(st_x[0, j], OX[c][:]).then_inc(stored["x"][c].sem, 16)
                            sp.wait_ge(*S.after("xb", c, i))
                            sp.dma_start(st_x[1, j], OV[c][:]).then_inc(stored["v"][c].sem, 16)
                            sp.wait_ge(*S.after("rows", c, i))
                            sp.dma_start(rows_of(tab)[j], as_rows(R[c])).then_inc(stored["r"][c].sem, 16)

                    def finish():
                        for c in AB:
                            for n in ("x", "v", "r"):
                                sp.wait_ge(*stored[n][c].after(TURNS[c] - 1))

                    loads_and_stores(sp, load, store, finish)

                @block.tensor
                def _(pe):
                    def body(i, cs):
                        for c in cs:
                            pe.wait_ge(*arr["g1"][c].after(i, Q))
                            pe.wait_ge(*S.after("rows", c, i - 1))
                            transposes(KK[c][0], G1[c])
                            pe.wait_ge(*arr["g2"][c].after(i, Q))
                            transposes(KK[c][1], G2[c]).then_inc(S.did("inT", c), 1)
                        for c in cs:
                            pe.wait_ge(*S.after("xa", c, i))
                            nc.tensor.matmul(KK[c][2][:], W["L0_W1"][:], OX[c][:], start=True, stop=True)
                            pe.wait_ge(*S.after("xb", c, i))
                            nc.tensor.matmul(KK[c][3][:], W["L0_W1"][:], OV[c][:], start=True, stop=True).then_inc(S.did("proj", c), 1)
                        for c in cs:
                            pe.wait_ge(*S.after("hi", c, i))
                            nc.tensor.matmul(KK[c][0][:], W["L0_W2a"][:], B1[c][:], start=True, stop=False)
                            pe.wait_ge(*S.after("d", c, i))
                            nc.tensor.matmul(KK[c][0][:], W["L0_W2b"][:], B2[c][:], start=False, stop=True).then_inc(S.did("mlp1", c), 1)
                        for c in cs:
                            product(pe, S, c, i, "mlp2", "L0_W3", KK[c][1], LV[c], ["m1"], BLK)
                        for c in cs:
                            pe.wait_ge(*S.after("scan", c, i))
                            to_rows(KK[c][2], ZM[c]).then_inc(S.did("rowsT", c), 1)
                    in_turns(pe, body)

                @block.scalar
                def _(act):
                    def body(i, cs):
                        for c in cs:
                            act.wait_ge(*stored["x"][c].after(i - 1))
                            function(act, S, c, i, "xa", ACT.Copy, None, KK[c][0], OX[c], ["inT"], BLK)
                        for c in cs:
                            function(act, S, c, i, "hi", ACT.Identity, "L0_b1", KK[c][2], B1[c], ["proj"], BLK)
                        for c in cs:
                            function(act, S, c, i, "m1", ACT.Relu, "L0_b2", KK[c][0], LV[c], ["mlp1"], BLK)
                        for c in cs:
                            function(act, S, c, i, "m2", ACT.Relu, "L0_b3", KK[c][1], LX[c], ["mlp2"], BLK)
                        for c in cs:
                            act.wait_ge(*stored["r"][c].after(i - 1))
                            function(act, S, c, i, "rows", ACT.Copy, None, KK[c][2], R[c], ["rowsT"], BLK)
                    in_turns(act, body)

                @block.vector
                def _(dve):
                    def body(i, cs):
                        for c in cs:
                            dve.wait_ge(*S.after("inT", c, i))
                            dve.wait_ge(*stored["v"][c].after(i - 1))
                            nc.vector.tensor_copy(OV[c][:], KK[c][1][:]).then_inc(S.did("xb", c), 1)
                        for c in cs:
                            dve.wait_ge(*S.after("hi", c, i))
                            nc.vector.scalar_tensor_tensor(B2[c][:], KK[c][3][:], B["L0_b1"][:, 0:1], B1[c][:], ALU.add, ALU.subtract).then_inc(S.did("d", c), 1)
                        for c in cs:
                            dve.wait_ge(*S.after("m2", c, i))
                            dve.wait_ge(*arr["same"][c].after(i))
                            if c == LB:
                                dve.wait_ge(*S.after("scan", LA, i))
                            else:
                                dve.wait_ge(*S.after("scan", LB, i - 1))
                            dve.wait_ge(*S.after("rowsT", c, i - 1))
                            nc.vector.tensor_tensor_scan(ZM[c][:], LT[c][:], LX[c][:], ZM[1 - c][:, BLK - 1:BLK], ALU.mult, ALU.max).then_inc(S.did("scan", c), 1)
                    start_sums(dve)
                    in_turns(dve, body)
            S.close(TURNS)
            for c in AB:
                for n in ("g1", "g2"):
                    arr[n][c].close(TURNS[c], Q)
                arr["same"][c].close(TURNS[c])
                for n in ("x", "v", "r"):
                    stored[n][c].close(TURNS[c])

        def back_stage(wname, first):
            steps = [("ids", "gather"), ("inT", "pe"), ("in", "act"), ("msg", "pe"), ("scaled", "dve"), ("scan", "dve"), ("rowsT", "pe"), ("rows", "act")]
            S = Steps(lane_sems, lane_base, {LA: steps, LB: steps})
            KK = [[K[2 * c + m] for m in range(2)] for c in range(2)]
            dense = Steps(lane_sems, lane_base, DENSE)

            def beside(eng, body, dense_part):
                with eng.Fori(0, DENSE_BACK) as d:
                    for u in range(TURNS_BACK):
                        body(d * TURNS_BACK + u, (LA, LB), lambda k: dense_part(d, 4 * u + k) if u < 2 else None)
                body(PAIRS, (LA,), lambda k: None)
            with nc.Block() as block:
                @block.gpsimd
                def _(pool):
                    def body(i, cs):
                        for c in cs:
                            gather(pool, S, c, i, i * 2 + c, "inT", [("dst_in_s", tab_u, G1[c], arr["g1"][c].sem)])
                    in_turns(pool, body)

                @block.sync
                def _(sp):
                    def load(i, cs):
                        for c in cs:
                            sp.wait_ge(*S.after("scan", c, i - 1))
                            sp.dma_start(LT[c][:], bcast(C_SAMES, i * 2 + c)).then_inc(arr["same"][c].sem, 16)
                            sp.dma_start(LS[c][:], bcast(C_INVIN, i * 2 + c)).then_inc(arr["s"][c].sem, 16)

                    def store(i, cs):
                        for c in cs:
                            sp.wait_ge(*S.after("rows", c, i))
                            sp.dma_start(rows_of(tab_b)[i * 2 + c], as_rows(R[c])).then_inc(stored["r"][c].sem, 16)

                    def finish():
                        for c in AB:
                            sp.wait_ge(*stored["r"][c].after(TURNS[c] - 1))

                    def turn(d, ints, block_no):
                        last = ints and d == DENSE_BACK - 1
                        for u in range(TURNS_BACK):
                            load(d * TURNS_BACK + (u + 1), (LA,) if last and u == TURNS_BACK - 1 else (LA, LB))
                            if u == 0 and block_no is not None:
                                dense_load(sp, dense, d + 1, block_no)
                            store(d * TURNS_BACK + u, (LA, LB))
                        dense_store(sp, dense, d, d + (first - LAG))

                    load(0, (LA, LB))
                    turn(0, True, min(first + 1, DB - 1))
                    with sp.Fori(1, DENSE_BACK - 1) as d:
                        turn(d, False, d + (first + 1) if first + DENSE_BACK < DB else DB - 1)
                    turn(DENSE_BACK - 1, True, first + DENSE_BACK if first + DENSE_BACK < DB else None)
                    store(PAIRS, (LA,))
                    sp.wait_ge(*stored["r"][D3].after(DENSE_BACK - 1))
                    finish()

                @block.tensor
                def _(pe):
                    def body(i, cs, dense_part):
                        dense_part(0)
                        for c in cs:
                            pe.wait_ge(*arr["g1"][c].after(i, Q))
                            pe.wait_ge(*S.after("rows", c, i - 1))
                            transposes(KK[c][0], G1[c]).then_inc(S.did("inT", c), 1)
                        dense_part(1)
                        for c in cs:
                            pe.wait_ge(*S.after("scaled", c, i - 1))
                            product(pe, S, c, i, "msg", wname, KK[c][1], LV[c], ["in"], BLK)
                        dense_part(2)
                        for c in cs:
                            pe.wait_ge(*S.after("scan", c, i))
                            to_rows(KK[c][0], ZM[c]).then_inc(S.did("rowsT", c), 1)
                        dense_part(3)
                    beside(pe, body, lambda d, part: dense_pe(pe, dense, d, part))

                @block.scalar
                def _(act):
                    def body(i, cs, dense_part):
                        dense_part(0)
                        for c in cs:
                            act.wait_ge(*S.after("msg", c, i - 1))
                            function(act, S, c, i, "in", ACT.Copy, None, KK[c][0], LV[c], ["inT"], BLK)
                        dense_part(1)
                        dense_part(2)
                        for c in cs:
                            act.wait_ge(*stored["r"][c].after(i - 1))
                            function(act, S, c, i, "rows", ACT.Copy, None, KK[c][0], R[c], ["rowsT"], BLK)
                        dense_part(3)
                    beside(act, body, lambda d, part: dense_act(act, dense, d, part))

                @block.vector
                def _(dve):
                    def body(i, cs, dense_part):
                        dense_part(0)
                        dense_part(1)
                        for c in cs:
                            dve.wait_ge(*S.after("msg", c, i))
                            dve.wait_ge(*S.after("scan", c, i - 1))
                            dve.wait_ge(*arr["s"][c].after(i))
                            nc.vector.tensor_tensor(B1[c][:], KK[c][1][:], LS[c][:], ALU.mult).then_inc(S.did("scaled", c), 1)
                            dve.wait_ge(*S.after("scaled", c, i))
                            dve.wait_ge(*arr["same"][c].after(i))
                            if c == LB:
                                dve.wait_ge(*S.after("scan", LA, i))
                            else:
                                dve.wait_ge(*S.after("scan", LB, i - 1))
                            dve.wait_ge(*S.after("rowsT", c, i - 1))
                            nc.vector.tensor_tensor_scan(ZM[c][:], LT[c][:], B1[c][:], ZM[1 - c][:, BLK - 1:BLK], ALU.mult, ALU.add).then_inc(S.did("scan", c), 1)
                        dense_part(2)
                        dense_part(3)
                    start_sums(dve)
                    beside(dve, body, lambda d, part: dense_dve(dve, dense, d, part))
            dense_close(dense, DENSE_BACK)
            S.close(TURNS)
            for c in AB:
                arr["g1"][c].close(TURNS[c], Q)
                arr["same"][c].close(TURNS[c])
                arr["s"][c].close(TURNS[c])
                stored["r"][c].close(TURNS[c])

        def slot_stage(tab, weight=None, bias=None, relu=True, two_way=False, v_from="v", pre=None, post=None,
                       resid=False, lstm=False, rows_to=False, final=False, msg=None, dense=None):
            norm = resid or lstm
            NS_, XS_, TS_ = (NA, NBL), (XA, XB), (TA, TB)
            agg = []
            if weight:
                agg += ([("rowsum", "dve")] if two_way else []) + [("pre", "pe")] + ([("scaled", "dve")] if pre else []) + [("act", "act")]
            else:
                agg += [("pre", "pe")]
            if norm:
                agg += [("z", "dve")]
            elif post:
                agg += [("v", "dve")]
            uT = [("uT", "pe"), ("uR", "act")] if rows_to and not norm else []
            lanes = {LA: [("ids", "gather")] * (two_way) + agg + uT, LB: [("ids", "gather")] * (not final) + agg}
            lag = {LA: 0, LB: 0}
            if norm:
                for c in NS_:
                    lanes[c] = LN + ([("scattered", "pool")] if final else [])
                    lag[c] = 1
                if not final:
                    for c in XS_:
                        lanes[c] = [("lnB", "pe"), ("xf", "act")] + ([("v", "dve")] if post and not lstm else [])
                        lag[c] = 2
                lanes[LNS] = ROOT
                lag[LNS] = 1
            if lstm:
                for c in TS_:
                    lanes[c] = LSTM + [("v", "dve")]
                    lag[c] = 2
            maker = TS_ if lstm else XS_ if norm else AB
            v_step = "v" if post else None if norm else "act"
            out_step = v_step or "xf"
            if msg:
                lanes[LM] = [("msg", "pe")] + ([("scaled", "dve")] if msg[1] is not None else []) + \
                    [("scan", "dve"), ("rowsT", "pe"), ("rows", "act")]
                lag[LM] = lag[maker[0]] + 1
            if dense is not None:
                lanes.update(DENSE)
            S = Steps(lane_sems, lane_base, lanes)
            LAST = max(lag.values())
            out_buf = OV[LB] if v_step else OX[LB]
            KG, KN, KM = K[0], {NA: K[1], NBL: K[2]}, K[3]
            KX = {XA: K[7], XB: K[7] if lstm else K[5]}
            KA = {LA: KG, LB: KG if dense is not None else K[4]}
            KT = {TA: K[5], TB: K[6]}
            fetch = {LA: [("end_ba", tab_b, ROWS2[LA], "g2")] * two_way,
                     LB: [("end_f", tab, ROWS1[LB], "g1")] * (not final) + [("end_bb", tab_b, ROWS2[LB], "g2")] * two_way}
            scale_row = {LA: C_D1A if 1 in (pre, post) else C_D3A, LB: C_D1B if 1 in (pre, post) else C_D3B}
            agg_free = {c: ("uR" if uT and c == LA else "scaled" if pre else "act" if weight else "z") for c in AB}
            scaler = {c: (maker[c] if post else c) for c in AB}
            scale_used = "v" if post else "scaled"

            def rounds(eng, body):
                for i in range(LAST):
                    body(i, i % 2)
                in_pairs(eng, LAST, NB, body)
                for i in range(NB, NB + LAST):
                    body(i, i % 2)

            def place(odd, c):
                return (odd + lag[c]) % 2

            def on(i, c):
                return c in lanes and (not isinstance(i, int) or lag[c] <= i < NB + lag[c])

            def at(i, c):
                return i - lag[c] if lag[c] else i

            def dense_on(i):
                return dense is not None and (not isinstance(i, int) or i < NB)

            with nc.Block() as block:
                @block.gpsimd
                def _(pool):
                    def get(i, odd):
                        for c in AB:
                            if fetch[c]:
                                gather(pool, S, c, i, i, "pre", [(l, t, dst[odd], pairs[s][c].sems[odd]) for l, t, dst, s in fetch[c]], odd, 2)

                    def put(i, odd, first=False):
                        for c in AB:
                            nc.gpsimd.tensor_copy(OI[odd][c][:], IX["out_a" if c == LA else "out_b"][:, bass.ds(i * Q, Q)]).then_inc(out_ids, 1)
                        pool.wait_ge(out_ids, i * 2 + 2)
                        pool.sem_inc(pool_passed, 1)
                        for c, n in zip(AB, NS_):
                            pool.wait_ge(*S.after("norm", n, i))
                            pool.sem_inc(pool_passed, 1)
                            for q in range(Q):
                                nc.gpsimd.indirect_dma_start(
                                    out=out, out_offset=bass.IndirectOffsetOnAxis(ap=OI[odd][c][:, q:q + 1].bitcast(U32), axis=0),
                                    in_=OUT_ROWS[n][odd][:, q * D:(q + 1) * D], in_offset=None, bounds_check=N - 1,
                                    oob_is_err=False).then_inc(out_dma[c].sems[odd], 16)
                        if not first:
                            arrived(i - 1, 1 - odd)

                    def arrived(i, odd):
                        for c, n in zip(AB, NS_):
                            pool.wait_ge(*out_dma[c].after(i, odd, Q))
                            pool.sem_inc(S.did("scattered", n), 1)

                    if final:
                        put(0, 0, first=True)
                        in_pairs(pool, 1, NB, put)
                        arrived(NB - 1, (NB - 1) % 2)
                    else:
                        in_pairs(pool, 0, NB, get)

                @block.sync
                def _(sp):
                    def load_start(i, odd):
                        for c in AB:
                            if weight:
                                sp.wait_ge(*S.after("pre", c, i - 2))
                                sp.dma_start(V_IN[c][odd][:], (st_v if v_from == "v" else st_x)[c, i]).then_inc(pairs["v"][c].sems[odd], 16)
                        sp.wait_ge(*S.after("pre", LA, i - 2))
                        sp.dma_start(as_rows(ROWS1[LA][odd]), rows_of(tab)[i]).then_inc(pairs["rows"][LA].sems[odd], 16)
                        for c in AB:
                            if norm:
                                sp.wait_ge(*S.after("z", c, i - 2))
                                sp.dma_start(X_IN[c][odd][:], st_x[c, i]).then_inc(pairs["x"][c].sems[odd], 16)
                            if pre:
                                sp.wait_ge(*S.after("v" if post else "scaled", c, i - 2))
                                sp.dma_start(S_IN[c][odd][:], bcast(scale_row[c], i)).then_inc(pairs["s"][c].sems[odd], 16)

                    def load_scale(n, b):
                        for c in AB:
                            sp.wait_ge(*S.after("v", maker[c], n - 2))
                            sp.dma_start(S_IN[c][b][:], bcast(scale_row[c], n)).then_inc(pairs["s"][c].sems[b], 16)

                    def load_msg(n, b):
                        sp.wait_ge(*S.after("scan", LM, n - 2))
                        sp.sem_inc(sp_passed, 1)
                        sp.dma_start(SAME[LM][b][:], bcast(C_SAMED, n)).then_inc(pairs["same"][LM].sems[b], 16)
                        if msg[1] is not None:
                            sp.dma_start(S_IN[LM][b][:], bcast(msg[1], n)).then_inc(pairs["s"][LM].sems[b], 16)

                    late_scale = bool(post and not pre)

                    def loads(i, odd):
                        if on(i, LA):
                            load_start(i, odd)
                        if late_scale and on(i, maker[0]):
                            load_scale(at(i, maker[0]), place(odd, maker[0]))
                        if msg and on(i, LM):
                            load_msg(at(i, LM), place(odd, LM))

                    def stores(i):
                        if rows_to and not norm and on(i, LA):
                            sp.wait_ge(*S.after("uR", LA, i))
                            sp.dma_start(rows_of(tab_u)[i], as_rows(R[LA])).then_inc(stored["r"][LA].sem, 16)
                        if norm and rows_to and on(i, NA):
                            n = at(i, NA)
                            sp.wait_ge(*S.after("norm", NA, n))
                            sp.dma_start(rows_of(tab_u)[n], as_rows(R[NA])).then_inc(stored["r"][LA].sem, 16)
                        if norm and not final and on(i, XA):
                            n = at(i, XA)
                            for c in AB:
                                sp.wait_ge(*S.after("xf", XS_[c], n))
                                sp.dma_start(st_x[c, n], OX[c][:]).then_inc(stored["x"][c].sem, 16)
                        if msg and on(i, LM):
                            sp.wait_ge(*S.after("rows", LM, at(i, LM)))
                            sp.dma_start(rows_of(msg[2])[at(i, LM)], as_rows(R[LM])).then_inc(stored["r"][LM].sem, 16)
                        if v_step and on(i, maker[0]):
                            n = at(i, maker[0])
                            for c in AB:
                                sp.wait_ge(*S.after(v_step, maker[c], n))
                                sp.dma_start(st_v[c, n], OV[c][:]).then_inc(stored["v"][c].sem, 16)

                    def round_(i, odd):
                        if not isinstance(i, int) or i + 1 < NB + LAST:
                            loads(i + 1, 1 - odd)
                        if dense_on(i):
                            dense_load(sp, S, i + 1, i + (dense + 1) if not isinstance(i, int) else min(i + dense + 1, DB - 1))
                        stores(i)
                        if dense_on(i):
                            dense_store(sp, S, i, i + (dense - LAG))

                    loads(0, 0)
                    for i in range(LAST):
                        round_(i, i % 2)
                    in_pairs(sp, LAST, NB - 1, round_)
                    for i in range(NB - 1, NB + LAST):
                        round_(i, i % 2)
                    if rows_to:
                        sp.wait_ge(*stored["r"][LA].after(NB - 1))
                    for c in AB:
                        if norm and not final:
                            sp.wait_ge(*stored["x"][c].after(NB - 1))
                        if v_step:
                            sp.wait_ge(*stored["v"][c].after(NB - 1))
                    if msg:
                        sp.wait_ge(*stored["r"][LM].after(NB - 1))
                    if dense is not None:
                        sp.wait_ge(*stored["r"][D3].after(NB - 1))

                @block.tensor
                def _(pe):
                    def aggregate(i, c, odd):
                        if c == LA:
                            pe.wait_ge(*pairs["rows"][c].after(i, odd))
                            pe.wait_ge(*S.after(agg_free[KA[LA] is KA[LB] and LB or LA], KA[LA] is KA[LB] and LB or LA, i - 1))
                        elif KA[LA] is KA[LB]:
                            pe.wait_ge(*S.after("scaled" if pre else "act" if weight else "z", LA, i))
                        else:
                            pe.wait_ge(*S.after(agg_free[c], c, i - 1))
                        for _, _, _, stream in fetch[c]:
                            pe.wait_ge(*pairs[stream][c].after(i, odd, Q))
                        rows = ROWS1[c][odd] if (c == LA or not final) else None
                        if weight:
                            if two_way:
                                pe.wait_ge(*S.after("rowsum", c, i))
                            pe.wait_ge(*pairs["v"][c].after(i, odd))
                            last = nc.tensor.matmul(KA[c][:], W[weight][:], V_IN[c][odd][:], start=True, stop=rows is None)
                            if rows is not None:
                                for q in range(Q):
                                    last = nc.tensor.matmul(tile_cols(KA[c], q), tile_cols(rows, q), ident[:], start=False, stop=(q == Q - 1))
                        else:
                            last = transposes(KA[c], rows)
                        last.then_inc(S.did("pre", c), 1)

                    def body(i, odd):
                        def dense_part(part):
                            if dense_on(i):
                                dense_pe(pe, S, i, part)

                        def rows_to_norm():
                            if norm and on(i, NA):
                                n = at(i, NA)
                                for k, c in enumerate(NS_):
                                    pe.wait_ge(*S.after("z", k, n))
                                    pe.wait_ge(*S.after("norm", c, n - 1))
                                    to_rows(KN[c], Z[k]).then_inc(S.did("lnT", c), 1)

                        def features(k):
                            if norm and not final and on(i, XA):
                                n = at(i, XA)
                                pe.wait_ge(*S.after("norm", NS_[k], n))
                                if KX[XA] is KX[XB]:
                                    pe.wait_ge(*(S.after("xf", XA, n) if k else S.after("xf", XB, n - 1)))
                                else:
                                    pe.wait_ge(*S.after("xf", XS_[k], n - 1))
                                transposes(KX[XS_[k]], R[NS_[k]]).then_inc(S.did("lnB", XS_[k]), 1)
                        def message():
                            if msg and on(i, LM):
                                n = at(i, LM)
                                pe.wait_ge(*S.after(out_step, maker[1], n))
                                pe.wait_ge(*S.after("rows", LM, n - 1))
                                nc.tensor.matmul(KM[:], W[msg[0]][:], out_buf[:], start=True, stop=True).then_inc(S.did("msg", LM), 1)

                        def message_rows():
                            if msg and on(i, LM):
                                pe.wait_ge(*S.after("scan", LM, at(i, LM)))
                                to_rows(KM, ZM[0]).then_inc(S.did("rowsT", LM), 1)

                        def side(c):
                            if on(i, c):
                                aggregate(i, c, odd)

                        def gates(name, weight_, before_):
                            if lstm and on(i, TA):
                                m = at(i, TA)
                                for k, c in enumerate(TS_):
                                    if name == "gate_i":
                                        pe.wait_ge(*S.after("sig_o", c, m - 1))
                                        pe.wait_ge(*S.after("xf", XS_[k], m))
                                    product(pe, S, c, m, name, weight_, KT[c], OX[k], before_, BLK)

                        def values_rows():
                            if uT and on(i, LA):
                                pe.wait_ge(*S.after("act", LA, i))
                                if KA[LA] is KA[LB]:
                                    pe.wait_ge(*S.after("scaled" if pre else "act", LB, i))
                                to_rows(KA[LA], OV[LA]).then_inc(S.did("uT", LA), 1)

                        dense_part(0)
                        if final:
                            side(LA)
                            side(LB)
                        rows_to_norm()
                        features(0)
                        if not norm and dense is None:
                            message()
                        if not final:
                            side(LA)
                        if norm or dense is not None:
                            message()
                        features(1)
                        dense_part(1)
                        dense_part(2)
                        if not final:
                            side(LB)
                        dense_part(3)
                        if not lstm:
                            message_rows()
                        gates("gate_i", "Wi", [])
                        dense_part(4)
                        gates("gate_g", "Wg", ["sig_i"])
                        dense_part(5)
                        gates("gate_o", "Wo", ["tanh_g"])
                        dense_part(6)
                        if lstm:
                            message_rows()
                        values_rows()
                        dense_part(7)
                    rounds(pe, body)

                @block.scalar
                def _(act):
                    def activate(i, c):
                        if v_step == "act":
                            act.wait_ge(*stored["v"][c].after(i - 1))
                            if msg and c == LB:
                                act.wait_ge(*S.after("msg", LM, i - 1))
                        else:
                            act.wait_ge(*S.after("z" if norm else "v", c, i - 1))
                        function(act, S, c, i, "act", ACT.Relu if relu else ACT.Identity, bias, B1[c] if pre else KA[c],
                                 OV[c] if v_step == "act" else B2[c], ["scaled" if pre else "pre"], BLK)

                    def body(i, odd):
                        def dense_part(part):
                            if dense_on(i):
                                dense_act(act, S, i, part)

                        gates = lstm and on(i, TA)
                        m = at(i, TA) if gates else None

                        def gate_acts(k, which):
                            c = TS_[k]
                            if which == 0:
                                function(act, S, c, m, "sig_i", ACT.Sigmoid, "bi", KT[c], BT[c], ["gate_i"], BLK)
                            if which == 1:
                                function(act, S, c, m, "tanh_g", ACT.Tanh, "bg", KT[c], CT[c], ["gate_g"], BLK)
                            if which == 2:
                                function(act, S, c, m, "sig_o", ACT.Sigmoid, "bo", KT[c], SO[c], ["gate_o"], BLK)
                                function(act, S, c, m, "tanh_c", ACT.Tanh, None, BT[c], CT[c], ["cell"], BLK)

                        def features(k):
                            if norm and not final and on(i, XA):
                                n, c = at(i, XA), XS_[k]
                                act.wait_ge(*stored["x"][k].after(n - 1))
                                if lstm:
                                    act.wait_ge(*S.after("gate_o", TS_[k], n - 1))
                                elif post:
                                    act.wait_ge(*S.after("v", c, n - 1))
                                if msg and k == 1 and not v_step:
                                    act.wait_ge(*S.after("msg", LM, n - 1))
                                function(act, S, c, n, "xf", ACT.Copy, None, KX[c], OX[k], ["lnB"], BLK)

                        def norms():
                            if norm and on(i, NA):
                                n = at(i, NA)
                                for k, c in enumerate(NS_):
                                    if rows_to and c == NA:
                                        act.wait_ge(*stored["r"][LA].after(n - 1))
                                    act.wait_ge(*(S.after("scattered", c, n - 2) if final else S.after("lnB", XS_[k], n - 1)))
                                    ln_norm(act, S, c, n, KN[c], OUT_ROWS[c][place(odd, c)] if final else R[c], P)
                        def side(c):
                            if weight and on(i, c):
                                activate(i, c)

                        def message_rows():
                            if msg and on(i, LM):
                                act.wait_ge(*stored["r"][LM].after(at(i, LM) - 1))
                                function(act, S, LM, at(i, LM), "rows", ACT.Copy, None, KM, R[LM], ["rowsT"], BLK)

                        def gate_of_sides(which):
                            if gates:
                                gate_acts(0, which)
                                gate_acts(1, which)

                        def values_rows():
                            if uT and on(i, LA):
                                act.wait_ge(*stored["r"][LA].after(i - 1))
                                function(act, S, LA, i, "uR", ACT.Copy, None, KA[LA], R[LA], ["uT"], BLK)

                        dense_part(0)
                        features(0)
                        side(LA)
                        dense_part(1)
                        features(1)
                        if not lstm and not final:
                            norms()
                        dense_part(2)
                        side(LB)
                        if final:
                            norms()
                        dense_part(3)
                        if not lstm:
                            message_rows()
                        gate_of_sides(0)
                        dense_part(4)
                        gate_of_sides(1)
                        if lstm:
                            norms()
                        dense_part(5)
                        gate_of_sides(2)
                        dense_part(6)
                        if lstm:
                            message_rows()
                        values_rows()
                        dense_part(7)
                    rounds(act, body)

                @block.vector
                def _(dve):
                    def add_ways(i, c, odd):
                        if c == LA:
                            dve.wait_ge(*pairs["rows"][c].after(i, odd))
                        for _, _, _, stream in fetch[c]:
                            dve.wait_ge(*pairs[stream][c].after(i, odd, Q))
                        nc.vector.tensor_tensor(ROWS1[c][odd][:], ROWS1[c][odd][:], ROWS2[c][odd][:], ALU.add).then_inc(S.did("rowsum", c), 1)

                    def scale(i, c, odd):
                        dve.wait_ge(*S.after("pre", c, i))
                        dve.wait_ge(*pairs["s"][c].after(i, odd))
                        dve.wait_ge(*S.after("act", c, i - 1))
                        nc.vector.tensor_tensor(B1[c][:], KA[c][:], S_IN[c][odd][:], ALU.mult).then_inc(S.did("scaled", c), 1)

                    def add_residual(i, c, odd):
                        dve.wait_ge(*S.after("act" if weight else "pre", c, i))
                        dve.wait_ge(*pairs["x"][c].after(i, odd))
                        dve.wait_ge(*S.after("lnT", NS_[c], i - 1))
                        nc.vector.tensor_tensor(Z[c][:], B2[c][:] if weight else KA[c][:], X_IN[c][odd][:], ALU.add).then_inc(S.did("z", c), 1)

                    def keep(i, odd):
                        if post and on(i, maker[0]):
                            n = at(i, maker[0])
                            for k, c in enumerate(maker):
                                dve.wait_ge(*S.after("h" if lstm else "xf" if norm else "act", c, n))
                                dve.wait_ge(*stored["v"][k].after(n - 1))
                                if msg and k == 1:
                                    dve.wait_ge(*S.after("msg", LM, n - 1))
                                dve.wait_ge(*pairs["s"][k].after(n, place(odd, c)))
                                src = BT[c] if lstm else OX[k] if norm else B2[k]
                                nc.vector.tensor_tensor(OV[k][:], src[:], S_IN[k][place(odd, c)][:], ALU.mult).then_inc(S.did("v", c), 1)

                    def body(i, odd):
                        def dense_part(part):
                            if dense_on(i):
                                dense_dve(dve, S, i, part)

                        gates = lstm and on(i, TA)
                        m = at(i, TA) if gates else None
                        def messages():
                            if msg and on(i, LM):
                                n = at(i, LM)
                                dve.wait_ge(*S.after("msg", LM, n))
                                src = KM
                                if msg[1] is not None:
                                    dve.wait_ge(*pairs["s"][LM].after(n, place(odd, LM)))
                                    nc.vector.tensor_tensor(B1[LM][:], KM[:], S_IN[LM][place(odd, LM)][:], ALU.mult).then_inc(S.did("scaled", LM), 1)
                                    dve.wait_ge(*S.after("scaled", LM, n))
                                    src = B1[LM]
                                dve.wait_ge(*pairs["same"][LM].after(n, place(odd, LM)))
                                dve.wait_ge(*S.after("rowsT", LM, n - 1))
                                nc.vector.tensor_tensor_scan(ZM[0][:], SAME[LM][place(odd, LM)][:], src[:], ZM[1][:, BLK - 1:BLK], ALU.mult, ALU.add).then_inc(S.did("scan", LM), 1)
                                dve.wait_ge(*S.after("scan", LM, n))
                                nc.vector.tensor_copy(ZM[1][:, BLK - 1:BLK], ZM[0][:, BLK - 1:BLK]).then_inc(carried, 1)
                                dve.wait_ge(carried, n + (carries[0] + 1))
                        def ways(c):
                            if two_way and on(i, c):
                                add_ways(i, c, odd)

                        def side(c):
                            if on(i, c):
                                if pre and not final:
                                    scale(i, c, odd)
                                if norm:
                                    add_residual(i, c, odd)

                        def scale_first():
                            if final and on(i, LA):
                                for c in AB:
                                    scale(i, c, odd)

                        def roots():
                            if norm and on(i, NA):
                                n = at(i, NA)
                                for c in NS_:
                                    dve.wait_ge(*S.after("norm", c, n - 1))
                                ln_group(dve, S, LNS, [(c, n) for c in NS_], KN, P)

                        if not norm and dense is None:
                            messages()
                        ways(LA)
                        dense_part(0)
                        scale_first()
                        roots()
                        side(LA)
                        ways(LB)
                        if norm or dense is not None:
                            messages()
                        dense_part(1)
                        side(LB)
                        dense_part(2)
                        dense_part(3)
                        dense_part(4)
                        if gates:
                            for k, c in enumerate(TS_):
                                cell(dve, S, c, m, BT[c], CT[c], BLK)
                        dense_part(5)
                        if gates:
                            for k, c in enumerate(TS_):
                                hidden(dve, S, c, m, CT[c], BT[c], BLK)
                        dense_part(6)
                        dense_part(7)
                        keep(i, odd)

                    if msg:
                        start_sums(dve)
                    rounds(dve, body)
            S.close({c: NB for c in lanes})
            for c in AB:
                if weight:
                    pairs["v"][c].close(NB)
                if norm:
                    pairs["x"][c].close(NB)
                if pre or post:
                    pairs["s"][c].close(NB)
                for _, _, _, stream in fetch[c]:
                    pairs[stream][c].close(NB, Q)
                if norm and not final:
                    stored["x"][c].close(NB)
                if v_step:
                    stored["v"][c].close(NB)
            pairs["rows"][LA].close(NB)
            if rows_to:
                stored["r"][LA].close(NB)
            if msg:
                carries[0] += NB
                pairs["same"][LM].close(NB)
                if msg[1] is not None:
                    pairs["s"][LM].close(NB)
                stored["r"][LM].close(NB)
            if dense is not None:
                arr["x"][D0].close(NB)
                stored["r"][D3].close(NB)



        d1 = DENSE_RANK + DENSE_RECORDS
        d2 = d1 + DENSE_BACK + NB
        d3 = d2 + DENSE_BACK + NB
        PLAN = [
            lambda: edge_stage(tab_f0),
            lambda: slot_stage(tab_f0, lstm=True, post=1, msg=("L1_W1", None, tab_f1)),
            lambda: slot_stage(tab_f1, "L1_W1", "L1_b1", pre=1, post=1, msg=("L1_W23", None, tab_f0)),
            lambda: slot_stage(tab_f0, "L1_W23", "L1_b23", pre=1, resid=True, rows_to=True, msg=("W0f", C_INVOUT, tab_f1)),
            lambda: back_stage("W0b", d1),
            lambda: slot_stage(tab_f1, "W0x", "L2_b0", two_way=True, v_from="x", rows_to=True, msg=("W1f", C_INVOUT, tab_f0), dense=d1 + DENSE_BACK),
            lambda: back_stage("W1b", d2),
            lambda: slot_stage(tab_f0, "W1x", "L2_b1", two_way=True, rows_to=True, msg=("W2f", C_INVOUT, tab_f1), dense=d2 + DENSE_BACK),
            lambda: back_stage("W2b", d3),
            lambda: slot_stage(tab_f1, "W2x", "L2_b2", relu=False, two_way=True, resid=True, post=3, msg=("L3_W1", C_W, tab_f0)),
            lambda: slot_stage(tab_f0, "L3_W1", "L3_b1", pre=3, post=3, msg=("L3_W2", C_W, tab_f1)),
            lambda: slot_stage(tab_f1, "L3_W2", "L3_b2", pre=3, resid=True, final=True),
        ]
        for stage in PLAN:
            stage()

def kernel(**inputs):
    import concourse.bacc as bacc
    from concourse.bass_utils import run_bass_kernel_spmd

    nc = bacc.Bacc("TRN2", target_bir_lowering=False, num_devices=1)
    arrays, aps = {}, {}
    for name, x in inputs.items():
        x = np.ascontiguousarray(x)
        arrays["in_" + name] = x
        aps[name] = nc.dram_tensor("in_" + name, x.shape, mybir.dt.from_np(x.dtype), kind="ExternalInput").ap()
    out = nc.dram_tensor("out", (N, D), F32, kind="ExternalOutput").ap()
    build(nc, aps, out)
    r = run_bass_kernel_spmd(nc, [arrays], core_ids=[0])
    return r.results[0]["out"]
```
